# Optimizing a Trainium2 kernel written in Bass

```python
import numpy as np
import jax
import jax.numpy as jnp

def _softmax(x, axis=-1):
    return jax.nn.softmax(x, axis=axis)

def _gelu(x):
    return jax.nn.gelu(x, approximate=True)

def _silu(x):
    return jax.nn.silu(x)

def _sigmoid(x):
    return jax.nn.sigmoid(x)

def _layernorm(x, axis=-1, eps=1e-05):
    m = jnp.mean(x, axis=axis, keepdims=True)
    v = jnp.var(x, axis=axis, keepdims=True)
    return (x - m) / jnp.sqrt(v + eps)

def _scatter_add(tgt, idx, src, axis=0):
    return tgt.at[idx].add(src)

def _segment_sum(src, seg, n):
    return jax.ops.segment_sum(src, seg, n)
kernel_name = 'mk_flamingo_gated_d4_seqx_r4_fbfe89'

def setup_inputs(seed: int=0):
    np.random.seed(seed)
    _w = jnp.asarray

    def _rec_inputs():
        import jax
        import jax.numpy as jnp
        _rk = jax.random.key(seed)
        x = -0.0003929 + 0.9999 * jax.random.normal(jax.random.fold_in(_rk, 1), (8, 256, 256), jnp.float32)
        _lenS = 256 - jax.random.randint(jax.random.fold_in(_rk, 7), (8,), 0, max(1, 256 // 4) + 1, jnp.int32)
        _lenS2 = 256 - jax.random.randint(jax.random.fold_in(_rk, 8), (8,), 0, max(1, 256 // 4) + 1, jnp.int32)
        _ctx_1024P = jax.random.normal(jax.random.fold_in(_rk, 11), (8, 16, 256), jnp.float32)
        _ctx_1024c = jax.random.dirichlet(jax.random.fold_in(_rk, 511), 0.3 * jnp.ones((16,), jnp.float32), (8, 256))
        _ctx_1024t = jnp.einsum('bsk,bkd->bsd', _ctx_1024c, _ctx_1024P)
        _ctx_1024t = _ctx_1024t * jax.lax.rsqrt(jnp.mean(jnp.square(_ctx_1024t)) + 1e-12) * 0.953939
        ctx_1024 = 2.81802e-05 + 1.00001 * (_ctx_1024t + 0.3 * jax.random.normal(jax.random.fold_in(_rk, 611), (8, 256, 256), jnp.float32))
        _validS = jnp.arange(256)[None, :] < _lenS[:, None]
        _validS2 = jnp.arange(256)[None, :] < _lenS2[:, None]
        _causal = jnp.tril(jnp.ones((256, 256), dtype=bool))
        mask_BxS2_if1 = jnp.where(jnp.ones((8, 256), dtype=bool), 1, 0).astype(jnp.int32)
        mask_Bx1xS2_ik0 = jnp.where(jnp.broadcast_to(_validS2[:, None, :], (8, 1, 256)), 0, 1).astype(jnp.int32)
        _g = jax.random.normal(jax.random.fold_in(_rk, 9001), (2, 4), jnp.float32)
        _g = jnp.sign(_g) * jnp.maximum(jnp.abs(_g), 1.0) + (_g == 0) * 1.0
        g_xattn = _g[0]
        g_ffn = _g[1]
        return (x, ctx_1024, mask_BxS2_if1, mask_Bx1xS2_ik0, g_xattn, g_ffn)
    x, ctx_1024, mask_BxS2_if1, mask_Bx1xS2_ik0, g_xattn, g_ffn = _rec_inputs()

    def _L0_xattn_setup():
        import jax, jax.numpy as jnp
        import numpy as np
        B, S, E = (8, 512, 256)
        EPS = 0.001

        def _layer_norm(x, gamma, beta):
            mu = jnp.mean(x, axis=-1, keepdims=True)
            var = jnp.mean(jnp.square(x - mu), axis=-1, keepdims=True)
            return gamma * (x - mu) * jax.lax.rsqrt(var + EPS) + beta

        def _attention(q_in, k_in, v_in, WQ, WK, WV, causal):
            Q = jnp.einsum('bse,ed->bsd', q_in, WQ)
            K = jnp.einsum('bse,ed->bsd', k_in, WK)
            V = jnp.einsum('bse,ed->bsd', v_in, WV)
            d = K.shape[-1]
            scores = jnp.einsum('bqd,bkd->bqk', Q, K) / jnp.sqrt(jnp.float32(d))
            if causal:
                qlen, klen = (scores.shape[-2], scores.shape[-1])
                mask = jnp.triu(jnp.ones((qlen, klen), bool), k=1)
                scores = jnp.where(mask[None], -jnp.inf, scores)
            p = jax.nn.softmax(scores, axis=-1)
            return jnp.einsum('bqk,bkd->bqd', p, V)
        key = jax.random.key(seed)
        ks = jax.random.split(key, 10)
        sc = 1.0 / np.sqrt(E)
        return {'inputs': jax.random.normal(ks[0], (B, S, E), jnp.float32), 'context': jax.random.normal(ks[1], (B, S, E), jnp.float32), 'Wq': jax.random.normal(ks[2], (E, E), jnp.float32) * sc, 'Wk': jax.random.normal(ks[3], (E, E), jnp.float32) * sc, 'Wv': jax.random.normal(ks[4], (E, E), jnp.float32) * sc, 'Wcq': jax.random.normal(ks[5], (E, E), jnp.float32) * sc, 'Wck': jax.random.normal(ks[6], (E, E), jnp.float32) * sc, 'Wcv': jax.random.normal(ks[7], (E, E), jnp.float32) * sc, 'gamma': jnp.ones((E,), jnp.float32), 'beta': jnp.zeros((E,), jnp.float32), 'W1': jax.random.normal(ks[8], (E, E), jnp.float32) * sc, 'b1': jnp.zeros((E,), jnp.float32)}
    _L0_xattn_all = _L0_xattn_setup()
    _L0_xattn_in = {k: v for k, v in _L0_xattn_all.items() if k in ('Wq', 'Wk', 'Wv', 'Wcq', 'Wck', 'Wcv', 'gamma', 'beta', 'W1', 'b1')}
    del _L0_xattn_all

    def _L0_ffn_setup():
        import jax, jax.numpy as jnp
        import numpy as np
        B, L, D = (2, 512, 256)
        E = 15
        H = D * 1
        K = 3
        T = 1.0
        key = jax.random.key(seed)
        ks = jax.random.split(key, 12)
        s = 0.02
        return {'x': jax.random.normal(ks[0], (B, L, D), dtype=jnp.float32), 'router_W': jax.random.normal(ks[1], (D, E), dtype=jnp.float32) * s, 'router_b': jnp.zeros((E,), dtype=jnp.float32), 'sW1': jax.random.normal(ks[2], (D, H), dtype=jnp.float32) * s, 'sb1': jnp.zeros((H,), dtype=jnp.float32), 'sW2': jax.random.normal(ks[3], (H, D), dtype=jnp.float32) * s, 'sb2': jnp.zeros((D,), dtype=jnp.float32), 'eW1': jax.random.normal(ks[4], (E, D, H), dtype=jnp.float32) * s, 'eb1': jnp.zeros((E, H), dtype=jnp.float32), 'eW2': jax.random.normal(ks[5], (E, H, D), dtype=jnp.float32) * s, 'eb2': jnp.zeros((E, D), dtype=jnp.float32)}
    _L0_ffn_all = _L0_ffn_setup()
    _L0_ffn_in = {k: v for k, v in _L0_ffn_all.items() if k in ('router_W', 'router_b', 'sW1', 'sb1', 'sW2', 'sb2', 'eW1', 'eb1', 'eW2', 'eb2')}
    del _L0_ffn_all

    def _L1_xattn_setup():
        import jax, jax.numpy as jnp
        import numpy as np
        import math
        NUM_HEADS = 16
        HIDDEN = 256
        HEAD_DIM = HIDDEN // NUM_HEADS
        ROTARY_BASE = 10000.0
        B, S = (4, 512)

        def _rotary_tables(seq_len):
            inv_freq = 1.0 / ROTARY_BASE ** (jnp.arange(0, HEAD_DIM, 2, dtype=jnp.float32) / HEAD_DIM)
            pos = jnp.arange(seq_len, dtype=jnp.float32)
            freqs = pos[:, None] * inv_freq[None, :]
            return (jnp.cos(freqs), jnp.sin(freqs))

        def _apply_rotary(x, cos, sin):
            even = x[..., 0::2]
            odd = x[..., 1::2]
            c = cos[None, None, :, :]
            s = sin[None, None, :, :]
            return jnp.concatenate([even * c - odd * s, even * s + odd * c], axis=-1)
        key = jax.random.key(seed)
        ks = jax.random.split(key, 12)
        w = 0.02
        return {'query': jax.random.normal(ks[0], (B, S, HIDDEN), jnp.float32), 'key': jax.random.normal(ks[1], (B, S, HIDDEN), jnp.float32), 'value': jax.random.normal(ks[2], (B, S, HIDDEN), jnp.float32), 'padding_mask': jnp.ones((B, S), jnp.int32), 'is_causal': 1, 'Wq': jax.random.normal(ks[3], (HIDDEN, HIDDEN), jnp.float32) * w, 'bq': jnp.zeros((HIDDEN,), jnp.float32), 'Wk': jax.random.normal(ks[4], (HIDDEN, HIDDEN), jnp.float32) * w, 'bk': jnp.zeros((HIDDEN,), jnp.float32), 'Wv': jax.random.normal(ks[5], (HIDDEN, HIDDEN), jnp.float32) * w, 'bv': jnp.zeros((HIDDEN,), jnp.float32), 'Wo': jax.random.normal(ks[6], (HIDDEN, HIDDEN), jnp.float32) * w, 'bo': jnp.zeros((HIDDEN,), jnp.float32)}
    _L1_xattn_all = _L1_xattn_setup()
    _L1_xattn_in = {k: v for k, v in _L1_xattn_all.items() if k in ('Wq', 'bq', 'Wk', 'bk', 'Wv', 'bv', 'Wo', 'bo')}
    del _L1_xattn_all

    def _L1_ffn_setup():
        import jax, jax.numpy as jnp
        import numpy as np
        TOP_K = 2

        def _ffn(x, gw, uw, dw):
            return jax.nn.silu(x @ gw.T) * (x @ uw.T) @ dw.T
        key = jax.random.key(seed)
        ks = jax.random.split(key, 8)
        w = lambda k, shape: jax.random.normal(k, shape, jnp.float32) * 0.02
        return dict(x=jax.random.normal(ks[0], (4, 512, 256), jnp.float32), gate_w=w(ks[1], (8, 256)), expert_gate=w(ks[2], (8, 704, 256)), expert_up=w(ks[3], (8, 704, 256)), expert_down=w(ks[4], (8, 256, 704)), shared_gate=w(ks[5], (704, 256)), shared_up=w(ks[6], (704, 256)), shared_down=w(ks[7], (256, 704)))
    _L1_ffn_all = _L1_ffn_setup()
    _L1_ffn_in = {k: v for k, v in _L1_ffn_all.items() if k in ('gate_w', 'expert_gate', 'expert_up', 'expert_down', 'shared_gate', 'shared_up', 'shared_down')}
    del _L1_ffn_all

    def _L2_xattn_setup():
        import jax, jax.numpy as jnp
        import numpy as np
        B, SQ, SK = (2, 512, 512)
        DQ = DK = DV = DM = DOUT = 256
        H = 16
        DHEAD = DM // H
        key = jax.random.key(seed)
        ks = jax.random.split(key, 12)
        s = 0.02
        return {'Q': jax.random.normal(ks[0], (B, SQ, DQ), jnp.float32), 'K': jax.random.normal(ks[1], (B, SK, DK), jnp.float32), 'V': jax.random.normal(ks[2], (B, SK, DV), jnp.float32), 'mask': jax.random.randint(ks[3], (B, 1, SK), 0, 2, jnp.int32), 'Wq': jax.random.normal(ks[4], (DQ, DM), jnp.float32) * s, 'bq': jnp.zeros((DM,), jnp.float32), 'Wk': jax.random.normal(ks[5], (DK, DM), jnp.float32) * s, 'bk': jnp.zeros((DM,), jnp.float32), 'Wv': jax.random.normal(ks[6], (DV, DM), jnp.float32) * s, 'bv': jnp.zeros((DM,), jnp.float32), 'Wo': jax.random.normal(ks[7], (DM, DOUT), jnp.float32) * s, 'bo': jnp.zeros((DOUT,), jnp.float32)}
    _L2_xattn_all = _L2_xattn_setup()
    _L2_xattn_in = {k: v for k, v in _L2_xattn_all.items() if k in ('Wq', 'bq', 'Wk', 'bk', 'Wv', 'bv', 'Wo', 'bo')}
    del _L2_xattn_all

    def _L2_ffn_setup():
        import math
        import jax, jax.numpy as jnp
        import numpy as np
        D_MODEL = 256
        D_FF = 1024
        E = 8
        K = 2
        CF = 1.25
        CLAMP = 10000.0
        key = jax.random.key(seed)
        k0, k1, k2, k3 = jax.random.split(key, 4)
        B, S = (4, 512)
        x = jax.random.normal(k0, (B, S, D_MODEL), dtype=jnp.float32)
        ln_gamma = jnp.ones((D_MODEL,), jnp.float32)
        ln_beta = jnp.zeros((D_MODEL,), jnp.float32)
        rb = 0.02 * math.sqrt(3.0)
        Wr = jax.random.uniform(k1, (E, D_MODEL), jnp.float32, -rb, rb)
        b12 = math.sqrt(6.0 / (D_MODEL + 2 * D_FF))
        W12 = jax.random.uniform(k2, (E, 2 * D_FF, D_MODEL), jnp.float32, -b12, b12)
        b3 = math.sqrt(6.0 / (D_FF + D_MODEL))
        W3 = jax.random.uniform(k3, (E, D_MODEL, D_FF), jnp.float32, -b3, b3)
        return {'x': x, 'ln_gamma': ln_gamma, 'ln_beta': ln_beta, 'Wr': Wr, 'W12': W12, 'W3': W3}
    _L2_ffn_all = _L2_ffn_setup()
    _L2_ffn_in = {k: v for k, v in _L2_ffn_all.items() if k in ('ln_gamma', 'ln_beta', 'Wr', 'W12', 'W3')}
    del _L2_ffn_all

    def _L3_xattn_setup():
        import jax, jax.numpy as jnp
        import numpy as np
        DIM = 256
        NUM_HEADS = 16
        DIM_HEAD = 64
        INNER = NUM_HEADS * DIM_HEAD
        SCALE = DIM_HEAD ** (-0.5)

        def _layernorm(x, gamma, beta, eps=1e-05):
            mu = jnp.mean(x, axis=-1, keepdims=True)
            var = jnp.mean(jnp.square(x - mu), axis=-1, keepdims=True)
            return (x - mu) * jax.lax.rsqrt(var + eps) * gamma + beta
        key = jax.random.key(seed)
        ks = jax.random.split(key, 8)
        B, SQ, SK = (2, 512, 1024)
        x = jax.random.normal(ks[0], (B, SQ, DIM), dtype=jnp.float32)
        context = jax.random.normal(ks[1], (B, SK, DIM), dtype=jnp.float32)
        ln_gamma = jnp.ones((DIM,), jnp.float32)
        ln_beta = jnp.zeros((DIM,), jnp.float32)
        w_q = jax.random.normal(ks[2], (DIM, INNER), dtype=jnp.float32) / np.sqrt(DIM)
        w_kv = jax.random.normal(ks[3], (DIM, 2 * INNER), dtype=jnp.float32) / np.sqrt(DIM)
        w_out = jax.random.normal(ks[4], (INNER, DIM), dtype=jnp.float32) / np.sqrt(INNER)
        b_out = jnp.zeros((DIM,), jnp.float32)
        gate = jnp.array([0.5], jnp.float32)
        return {'x': x, 'context': context, 'ln_gamma': ln_gamma, 'ln_beta': ln_beta, 'w_q': w_q, 'w_kv': w_kv, 'w_out': w_out, 'b_out': b_out, 'gate': gate}
    _L3_xattn_all = _L3_xattn_setup()
    _L3_xattn_in = {k: v for k, v in _L3_xattn_all.items() if k in ('ln_gamma', 'ln_beta', 'w_q', 'w_kv', 'w_out', 'b_out', 'gate')}
    del _L3_xattn_all

    def _L3_ffn_setup():
        import jax, jax.numpy as jnp
        import numpy as np
        H, F, E_SHARED, E_ROUTED, K = (256, 1024, 1, 8, 2)

        def _expert(x, w_up, w_down):
            h = jax.nn.gelu(jnp.einsum('bsh,hf->bsf', x, w_up), approximate=False)
            return jnp.einsum('bsf,fh->bsh', h, w_down)
        key = jax.random.key(seed)
        ks = jax.random.split(key, 6)
        x = jax.random.normal(ks[0], (4, 512, H), dtype=jnp.float32)
        s = 0.02
        shared_up = jax.random.normal(ks[1], (E_SHARED, H, F), dtype=jnp.float32) * s
        shared_down = jax.random.normal(ks[2], (E_SHARED, F, H), dtype=jnp.float32) * s
        routed_up = jax.random.normal(ks[3], (E_ROUTED, H, F), dtype=jnp.float32) * s
        routed_down = jax.random.normal(ks[4], (E_ROUTED, F, H), dtype=jnp.float32) * s
        router_w = jax.random.normal(ks[5], (H, E_ROUTED), dtype=jnp.float32) * s
        return {'x': x, 'shared_up': shared_up, 'shared_down': shared_down, 'routed_up': routed_up, 'routed_down': routed_down, 'router_w': router_w}
    _L3_ffn_all = _L3_ffn_setup()
    _L3_ffn_in = {k: v for k, v in _L3_ffn_all.items() if k in ('shared_up', 'shared_down', 'routed_up', 'routed_down', 'router_w')}
    del _L3_ffn_all
    return {'x': x, 'ctx_1024': ctx_1024, 'mask_BxS2_if1': mask_BxS2_if1, 'mask_Bx1xS2_ik0': mask_Bx1xS2_ik0, 'g_xattn': g_xattn, 'g_ffn': g_ffn, 'L0_xattn_Wq': _L0_xattn_in['Wq'], 'L0_xattn_Wk': _L0_xattn_in['Wk'], 'L0_xattn_Wv': _L0_xattn_in['Wv'], 'L0_xattn_Wcq': _L0_xattn_in['Wcq'], 'L0_xattn_Wck': _L0_xattn_in['Wck'], 'L0_xattn_Wcv': _L0_xattn_in['Wcv'], 'L0_xattn_gamma': _L0_xattn_in['gamma'], 'L0_xattn_beta': _L0_xattn_in['beta'], 'L0_xattn_W1': _L0_xattn_in['W1'], 'L0_xattn_b1': _L0_xattn_in['b1'], 'L0_ffn_router_W': _L0_ffn_in['router_W'], 'L0_ffn_router_b': _L0_ffn_in['router_b'], 'L0_ffn_sW1': _L0_ffn_in['sW1'], 'L0_ffn_sb1': _L0_ffn_in['sb1'], 'L0_ffn_sW2': _L0_ffn_in['sW2'], 'L0_ffn_sb2': _L0_ffn_in['sb2'], 'L0_ffn_eW1': _L0_ffn_in['eW1'], 'L0_ffn_eb1': _L0_ffn_in['eb1'], 'L0_ffn_eW2': _L0_ffn_in['eW2'], 'L0_ffn_eb2': _L0_ffn_in['eb2'], 'L1_xattn_Wq': _L1_xattn_in['Wq'], 'L1_xattn_bq': _L1_xattn_in['bq'], 'L1_xattn_Wk': _L1_xattn_in['Wk'], 'L1_xattn_bk': _L1_xattn_in['bk'], 'L1_xattn_Wv': _L1_xattn_in['Wv'], 'L1_xattn_bv': _L1_xattn_in['bv'], 'L1_xattn_Wo': _L1_xattn_in['Wo'], 'L1_xattn_bo': _L1_xattn_in['bo'], 'L1_ffn_gate_w': _L1_ffn_in['gate_w'], 'L1_ffn_expert_gate': _L1_ffn_in['expert_gate'], 'L1_ffn_expert_up': _L1_ffn_in['expert_up'], 'L1_ffn_expert_down': _L1_ffn_in['expert_down'], 'L1_ffn_shared_gate': _L1_ffn_in['shared_gate'], 'L1_ffn_shared_up': _L1_ffn_in['shared_up'], 'L1_ffn_shared_down': _L1_ffn_in['shared_down'], 'L2_xattn_Wq': _L2_xattn_in['Wq'], 'L2_xattn_bq': _L2_xattn_in['bq'], 'L2_xattn_Wk': _L2_xattn_in['Wk'], 'L2_xattn_bk': _L2_xattn_in['bk'], 'L2_xattn_Wv': _L2_xattn_in['Wv'], 'L2_xattn_bv': _L2_xattn_in['bv'], 'L2_xattn_Wo': _L2_xattn_in['Wo'], 'L2_xattn_bo': _L2_xattn_in['bo'], 'L2_ffn_ln_gamma': _L2_ffn_in['ln_gamma'], 'L2_ffn_ln_beta': _L2_ffn_in['ln_beta'], 'L2_ffn_Wr': _L2_ffn_in['Wr'], 'L2_ffn_W12': _L2_ffn_in['W12'], 'L2_ffn_W3': _L2_ffn_in['W3'], 'L3_xattn_ln_gamma': _L3_xattn_in['ln_gamma'], 'L3_xattn_ln_beta': _L3_xattn_in['ln_beta'], 'L3_xattn_w_q': _L3_xattn_in['w_q'], 'L3_xattn_w_kv': _L3_xattn_in['w_kv'], 'L3_xattn_w_out': _L3_xattn_in['w_out'], 'L3_xattn_b_out': _L3_xattn_in['b_out'], 'L3_xattn_gate': _L3_xattn_in['gate'], 'L3_ffn_shared_up': _L3_ffn_in['shared_up'], 'L3_ffn_shared_down': _L3_ffn_in['shared_down'], 'L3_ffn_routed_up': _L3_ffn_in['routed_up'], 'L3_ffn_routed_down': _L3_ffn_in['routed_down'], 'L3_ffn_router_w': _L3_ffn_in['router_w']}

def reference(x, ctx_1024, mask_BxS2_if1, mask_Bx1xS2_ik0, g_xattn, g_ffn, L0_xattn_Wq, L0_xattn_Wk, L0_xattn_Wv, L0_xattn_Wcq, L0_xattn_Wck, L0_xattn_Wcv, L0_xattn_gamma, L0_xattn_beta, L0_xattn_W1, L0_xattn_b1, L0_ffn_router_W, L0_ffn_router_b, L0_ffn_sW1, L0_ffn_sb1, L0_ffn_sW2, L0_ffn_sb2, L0_ffn_eW1, L0_ffn_eb1, L0_ffn_eW2, L0_ffn_eb2, L1_xattn_Wq, L1_xattn_bq, L1_xattn_Wk, L1_xattn_bk, L1_xattn_Wv, L1_xattn_bv, L1_xattn_Wo, L1_xattn_bo, L1_ffn_gate_w, L1_ffn_expert_gate, L1_ffn_expert_up, L1_ffn_expert_down, L1_ffn_shared_gate, L1_ffn_shared_up, L1_ffn_shared_down, L2_xattn_Wq, L2_xattn_bq, L2_xattn_Wk, L2_xattn_bk, L2_xattn_Wv, L2_xattn_bv, L2_xattn_Wo, L2_xattn_bo, L2_ffn_ln_gamma, L2_ffn_ln_beta, L2_ffn_Wr, L2_ffn_W12, L2_ffn_W3, L3_xattn_ln_gamma, L3_xattn_ln_beta, L3_xattn_w_q, L3_xattn_w_kv, L3_xattn_w_out, L3_xattn_b_out, L3_xattn_gate, L3_ffn_shared_up, L3_ffn_shared_down, L3_ffn_routed_up, L3_ffn_routed_down, L3_ffn_router_w):
    import jax
    import jax.numpy as jnp

    def _L0_xattn_ref(inputs, context, Wq, Wk, Wv, Wcq, Wck, Wcv, gamma, beta, W1, b1):
        import jax, jax.numpy as jnp
        import numpy as np
        B, S, E = (8, 512, 256)
        EPS = 0.001

        def _layer_norm(x, gamma, beta):
            mu = jnp.mean(x, axis=-1, keepdims=True)
            var = jnp.mean(jnp.square(x - mu), axis=-1, keepdims=True)
            return gamma * (x - mu) * jax.lax.rsqrt(var + EPS) + beta

        def _attention(q_in, k_in, v_in, WQ, WK, WV, causal):
            Q = jnp.einsum('bse,ed->bsd', q_in, WQ)
            K = jnp.einsum('bse,ed->bsd', k_in, WK)
            V = jnp.einsum('bse,ed->bsd', v_in, WV)
            d = K.shape[-1]
            scores = jnp.einsum('bqd,bkd->bqk', Q, K) / jnp.sqrt(jnp.float32(d))
            if causal:
                qlen, klen = (scores.shape[-2], scores.shape[-1])
                mask = jnp.triu(jnp.ones((qlen, klen), bool), k=1)
                scores = jnp.where(mask[None], -jnp.inf, scores)
            p = jax.nn.softmax(scores, axis=-1)
            return jnp.einsum('bqk,bkd->bqd', p, V)
        a = _attention(inputs, inputs, inputs, Wq, Wk, Wv, causal=True) + inputs
        h = _layer_norm(a, gamma, beta)
        c = _attention(h, context, context, Wcq, Wck, Wcv, causal=False) + h
        h = _layer_norm(c, gamma, beta)
        f = jax.nn.relu(jnp.einsum('bse,ed->bsd', h, W1) + b1)
        out = _layer_norm(f + h, gamma, beta)
        return jax.nn.relu(out)

    def _L0_ffn_ref(x, router_W, router_b, sW1, sb1, sW2, sb2, eW1, eb1, eW2, eb2):
        import jax, jax.numpy as jnp
        import numpy as np
        B, L, D = (2, 512, 256)
        E = 15
        H = D * 1
        K = 3
        T = 1.0
        b, l, d = x.shape
        n = b * l
        xt = x.reshape(n, d)
        shared = jax.nn.relu(xt @ sW1 + sb1) @ sW2 + sb2
        logits = xt @ router_W + router_b
        probs = jax.nn.softmax(logits / T, axis=-1)
        top_p, top_i = jax.lax.top_k(probs, K)
        cw = jnp.zeros((n, E), dtype=probs.dtype)
        cw = cw.at[jnp.arange(n)[:, None], top_i].set(top_p)
        h = jax.nn.relu(jnp.einsum('nd,edh->neh', xt, eW1) + eb1)
        ye = jnp.einsum('neh,ehd->ned', h, eW2) + eb2
        routed = jnp.einsum('ned,ne->nd', ye, cw)
        return (shared + routed).reshape(b, l, d)

    def _L1_xattn_ref(query, key, value, padding_mask, is_causal, Wq, bq, Wk, bk, Wv, bv, Wo, bo):
        import jax, jax.numpy as jnp
        import numpy as np
        import math
        NUM_HEADS = 16
        HIDDEN = 256
        HEAD_DIM = HIDDEN // NUM_HEADS
        ROTARY_BASE = 10000.0
        B, S = (4, 512)

        def _rotary_tables(seq_len):
            inv_freq = 1.0 / ROTARY_BASE ** (jnp.arange(0, HEAD_DIM, 2, dtype=jnp.float32) / HEAD_DIM)
            pos = jnp.arange(seq_len, dtype=jnp.float32)
            freqs = pos[:, None] * inv_freq[None, :]
            return (jnp.cos(freqs), jnp.sin(freqs))

        def _apply_rotary(x, cos, sin):
            even = x[..., 0::2]
            odd = x[..., 1::2]
            c = cos[None, None, :, :]
            s = sin[None, None, :, :]
            return jnp.concatenate([even * c - odd * s, even * s + odd * c], axis=-1)
        b, s, _ = query.shape

        def proj(x, W, bias):
            y = x @ W.T + bias
            return y.reshape(b, s, NUM_HEADS, HEAD_DIM).transpose(0, 2, 1, 3)
        q = proj(query, Wq, bq)
        k = proj(key, Wk, bk)
        v = proj(value, Wv, bv)
        cos, sin = _rotary_tables(s)
        q = _apply_rotary(q, cos, sin)
        k = _apply_rotary(k, cos, sin)
        scores = jnp.einsum('bhqd,bhkd->bhqk', q, k) / math.sqrt(HEAD_DIM)
        scores = jnp.where(padding_mask[:, None, None, :] == 0, -1000000000.0, scores)
        if is_causal:
            causal = jnp.triu(jnp.ones((s, s), bool), k=1)
            scores = jnp.where(causal[None, None, :, :], -1000000000.0, scores)
        probs = jax.nn.softmax(scores, axis=-1)
        hidden = jnp.einsum('bhqk,bhkd->bhqd', probs, v)
        hidden = hidden.transpose(0, 2, 1, 3).reshape(b, s, HIDDEN)
        return hidden @ Wo.T + bo

    def _L1_ffn_ref(x, gate_w, expert_gate, expert_up, expert_down, shared_gate, shared_up, shared_down):
        import jax, jax.numpy as jnp
        import numpy as np
        TOP_K = 2

        def _ffn(x, gw, uw, dw):
            return jax.nn.silu(x @ gw.T) * (x @ uw.T) @ dw.T
        B, S, H = x.shape
        xf = x.reshape(-1, H)
        T = xf.shape[0]
        E = expert_gate.shape[0]
        shared = _ffn(xf, shared_gate, shared_up, shared_down)
        logits = xf @ gate_w.T
        probs = jax.nn.softmax(logits, axis=-1)
        topw, topi = jax.lax.top_k(probs, TOP_K)
        topw = topw / (topw.sum(-1, keepdims=True) + 1e-20)
        comb = jnp.zeros((T, E), xf.dtype).at[jnp.arange(T)[:, None], topi].add(topw)

        def body(acc, ws):
            gw, uw, dw, wcol = ws
            return (acc + _ffn(xf, gw, uw, dw) * wcol[:, None], None)
        routed, _ = jax.lax.scan(body, jnp.zeros_like(xf), (expert_gate, expert_up, expert_down, comb.T))
        return (shared + routed).reshape(B, S, H)

    def _L2_xattn_ref(Q, K, V, mask, Wq, bq, Wk, bk, Wv, bv, Wo, bo):
        import jax, jax.numpy as jnp
        import numpy as np
        B, SQ, SK = (2, 512, 512)
        DQ = DK = DV = DM = DOUT = 256
        H = 16
        DHEAD = DM // H
        b, sq, _ = Q.shape
        q = (Q @ Wq + bq).reshape(b, sq, H, DHEAD).transpose(0, 2, 1, 3)
        k = (K @ Wk + bk).reshape(b, -1, H, DHEAD).transpose(0, 2, 1, 3)
        v = (V @ Wv + bv).reshape(b, -1, H, DHEAD).transpose(0, 2, 1, 3)
        scores = jnp.einsum('bhqd,bhkd->bhqk', q, k) / np.sqrt(DHEAD).astype(np.float32)
        m = mask[:, None]
        scores = jnp.where(m == 0, -jnp.inf, scores)
        attn = jax.nn.softmax(scores, axis=-1)
        out = jnp.einsum('bhqk,bhkd->bhqd', attn, v)
        out = out.transpose(0, 2, 1, 3).reshape(b, sq, DM)
        return out @ Wo + bo

    def _L2_ffn_ref(x, ln_gamma, ln_beta, Wr, W12, W3):
        import math
        import jax, jax.numpy as jnp
        import numpy as np
        D_MODEL = 256
        D_FF = 1024
        E = 8
        K = 2
        CF = 1.25
        CLAMP = 10000.0
        B, S, D = x.shape
        T = B * S
        xf = x.reshape(T, D)
        mu = xf.mean(-1, keepdims=True)
        var = ((xf - mu) ** 2).mean(-1, keepdims=True)
        xn = (xf - mu) / jnp.sqrt(var + 1e-05) * ln_gamma + ln_beta
        logits = jnp.clip(xn @ Wr.T, -CLAMP, CLAMP)
        m = logits.max(-1, keepdims=True)
        ex = jnp.exp(logits - m)
        probs = ex / (ex.sum(-1, keepdims=True) + 1e-12)
        top_p, top_i = jax.lax.top_k(probs, K)
        Sslots = T * K
        experts = top_i.reshape(-1)
        weights = top_p.reshape(-1)
        tokens = jnp.repeat(jnp.arange(T, dtype=jnp.int32), K)
        order = jnp.argsort(experts, stable=True)
        e_s = experts[order]
        w_s = weights[order]
        t_s = tokens[order]
        counts = jnp.bincount(e_s, length=E)
        offsets = jnp.concatenate([jnp.zeros((1,), counts.dtype), jnp.cumsum(counts)])
        rank = jnp.arange(Sslots, dtype=counts.dtype) - offsets[e_s]
        cap = max(1, math.ceil(math.ceil(T * K * CF) / E))
        kept = rank < cap
        pos = jnp.where(kept, rank, cap)
        buf = jnp.zeros((E, cap, D), x.dtype).at[e_s, pos].set(xn[t_s], mode='drop')
        gu = jnp.einsum('ecd,efd->ecf', buf, W12)
        g, u = (gu[..., :D_FF], gu[..., D_FF:])
        h = jax.nn.silu(g) * u
        y = jnp.einsum('ecf,edf->ecd', h, W3)
        y_slot = y[e_s, jnp.minimum(pos, cap - 1)] * (w_s * kept.astype(x.dtype))[:, None]
        out = jnp.zeros((T, D), x.dtype).at[t_s].add(y_slot)
        return out.reshape(B, S, D)

    def _L3_xattn_ref(x, context, ln_gamma, ln_beta, w_q, w_kv, w_out, b_out, gate):
        import jax, jax.numpy as jnp
        import numpy as np
        DIM = 256
        NUM_HEADS = 16
        DIM_HEAD = 64
        INNER = NUM_HEADS * DIM_HEAD
        SCALE = DIM_HEAD ** (-0.5)

        def _layernorm(x, gamma, beta, eps=1e-05):
            mu = jnp.mean(x, axis=-1, keepdims=True)
            var = jnp.mean(jnp.square(x - mu), axis=-1, keepdims=True)
            return (x - mu) * jax.lax.rsqrt(var + eps) * gamma + beta
        B, SQ, _ = x.shape
        SK = context.shape[1]
        xn = _layernorm(x, ln_gamma, ln_beta)
        q = (xn @ w_q).reshape(B, SQ, NUM_HEADS, DIM_HEAD)
        kv = context @ w_kv
        k, v = jnp.split(kv, 2, axis=-1)
        k = k.reshape(B, SK, NUM_HEADS, DIM_HEAD)
        v = v.reshape(B, SK, NUM_HEADS, DIM_HEAD)
        scores = jnp.einsum('bqhd,bkhd->bhqk', q * SCALE, k)
        attn = jax.nn.softmax(scores, axis=-1)
        out = jnp.einsum('bhqk,bkhd->bqhd', attn, v).reshape(B, SQ, INNER)
        out = out @ w_out + b_out
        return out * jnp.tanh(gate[0])

    def _L3_ffn_ref(x, shared_up, shared_down, routed_up, routed_down, router_w):
        import jax, jax.numpy as jnp
        import numpy as np
        H, F, E_SHARED, E_ROUTED, K = (256, 1024, 1, 8, 2)

        def _expert(x, w_up, w_down):
            h = jax.nn.gelu(jnp.einsum('bsh,hf->bsf', x, w_up), approximate=False)
            return jnp.einsum('bsf,fh->bsh', h, w_down)
        shared_out = jnp.zeros_like(x)
        for i in range(E_SHARED):
            shared_out = shared_out + _expert(x, shared_up[i], shared_down[i])
        probs = jax.nn.softmax(jnp.einsum('bsh,he->bse', x, router_w), axis=-1)
        top_k_prob, top_k_idx = jax.lax.top_k(probs, K)
        onehot = jax.nn.one_hot(top_k_idx, E_ROUTED, dtype=x.dtype)
        gates = jnp.einsum('bsk,bske->bse', top_k_prob, onehot)
        routed_out = jnp.zeros_like(x)
        for e in range(E_ROUTED):
            y = _expert(x, routed_up[e], routed_down[e])
            routed_out = routed_out + gates[..., e:e + 1] * y
        return shared_out + routed_out + x
    x = x + jnp.tanh(g_xattn[0]) * _L0_xattn_ref(_layernorm(x, axis=-1), ctx_1024, L0_xattn_Wq, L0_xattn_Wk, L0_xattn_Wv, L0_xattn_Wcq, L0_xattn_Wck, L0_xattn_Wcv, L0_xattn_gamma, L0_xattn_beta, L0_xattn_W1, L0_xattn_b1)
    x = x + jnp.tanh(g_ffn[0]) * _L0_ffn_ref(_layernorm(x, axis=-1), L0_ffn_router_W, L0_ffn_router_b, L0_ffn_sW1, L0_ffn_sb1, L0_ffn_sW2, L0_ffn_sb2, L0_ffn_eW1, L0_ffn_eb1, L0_ffn_eW2, L0_ffn_eb2)
    x = x + jnp.tanh(g_xattn[1]) * _L1_xattn_ref(_layernorm(x, axis=-1), ctx_1024, ctx_1024, mask_BxS2_if1, 1, L1_xattn_Wq, L1_xattn_bq, L1_xattn_Wk, L1_xattn_bk, L1_xattn_Wv, L1_xattn_bv, L1_xattn_Wo, L1_xattn_bo)
    x = x + jnp.tanh(g_ffn[1]) * _L1_ffn_ref(_layernorm(x, axis=-1), L1_ffn_gate_w, L1_ffn_expert_gate, L1_ffn_expert_up, L1_ffn_expert_down, L1_ffn_shared_gate, L1_ffn_shared_up, L1_ffn_shared_down)
    x = x + jnp.tanh(g_xattn[2]) * _L2_xattn_ref(_layernorm(x, axis=-1), ctx_1024, ctx_1024, mask_Bx1xS2_ik0, L2_xattn_Wq, L2_xattn_bq, L2_xattn_Wk, L2_xattn_bk, L2_xattn_Wv, L2_xattn_bv, L2_xattn_Wo, L2_xattn_bo)
    x = x + jnp.tanh(g_ffn[2]) * _L2_ffn_ref(_layernorm(x, axis=-1), L2_ffn_ln_gamma, L2_ffn_ln_beta, L2_ffn_Wr, L2_ffn_W12, L2_ffn_W3)
    x = x + jnp.tanh(g_xattn[3]) * _L3_xattn_ref(_layernorm(x, axis=-1), ctx_1024, L3_xattn_ln_gamma, L3_xattn_ln_beta, L3_xattn_w_q, L3_xattn_w_kv, L3_xattn_w_out, L3_xattn_b_out, L3_xattn_gate)
    x = x + jnp.tanh(g_ffn[3]) * _L3_ffn_ref(_layernorm(x, axis=-1), L3_ffn_shared_up, L3_ffn_shared_down, L3_ffn_routed_up, L3_ffn_routed_down, L3_ffn_router_w)
    return x

_drawn_inputs = setup_inputs


def setup_inputs(seed=0):
    import zlib

    import numpy as np

    out = dict(_drawn_inputs(seed))
    spreads = {'L0_xattn_gamma': (1.0, 0.2),
     'L0_xattn_beta': (0.0, 0.1),
     'L0_xattn_b1': (0.0, 0.369),
     'L0_ffn_router_b': (0.0, 0.8),
     'L0_ffn_sb1': (0.0, 0.704),
     'L0_ffn_sb2': (0.0, 0.1),
     'L0_ffn_eb1': (0.0, 0.8),
     'L0_ffn_eb2': (0.0, 0.8),
     'L1_xattn_bq': (0.0, 0.8),
     'L1_xattn_bk': (0.0, 0.8),
     'L1_xattn_bv': (0.0, 0.379),
     'L1_xattn_bo': (0.0, 0.1),
     'L2_xattn_bq': (0.0, 2.0),
     'L2_xattn_bk': (0.0, 2.0),
     'L2_xattn_bv': (0.0, 0.466),
     'L2_xattn_bo': (0.0, 0.1),
     'L2_ffn_ln_gamma': (1.0, 0.6),
     'L2_ffn_ln_beta': (0.0, 0.8),
     'L3_xattn_ln_gamma': (1.0, 0.6),
     'L3_xattn_ln_beta': (0.0, 0.8),
     'L3_xattn_b_out': (0.0, 0.324)}
    factors = {'g_ffn': 28.144,
     'L0_ffn_router_W': 5.251,
     'L0_ffn_eW1': 8.0,
     'L0_ffn_eW2': 7.476,
     'L1_xattn_Wq': 8.0,
     'L1_xattn_Wk': 8.0,
     'L1_ffn_gate_w': 4.829,
     'L1_ffn_expert_gate': 4.307,
     'L1_ffn_expert_up': 4.261,
     'L1_ffn_expert_down': 4.242,
     'L1_ffn_shared_gate': 3.083,
     'L1_ffn_shared_up': 3.062,
     'L1_ffn_shared_down': 3.062,
     'L2_xattn_Wq': 8.0,
     'L2_xattn_Wk': 8.0,
     'L2_ffn_Wr': 2.685,
     'L3_ffn_routed_up': 5.555,
     'L3_ffn_routed_down': 5.428,
     'L3_ffn_router_w': 6.106,
     'L3_ffn_shared_up': 2.814,
     'L3_ffn_shared_down': 2.734}
    for name, (base, spread) in spreads.items():
        noise = np.random.default_rng([zlib.crc32(name.encode()), seed]).standard_normal(out[name].shape)
        drawn = base * np.exp(spread * noise) if base else spread * noise
        out[name] = jnp.asarray(drawn.astype(out[name].dtype))
    for name, factor in factors.items():
        out[name] = (out[name] * factor).astype(out[name].dtype)
    return out
```

```python
from contextlib import ExitStack

import numpy as np

import concourse.bass as bass
from concourse import mybir
from concourse.alu_op_type import AluOpType as ALU

F32 = mybir.dt.float32
F32R = mybir.dt.float32r
BF16 = mybir.dt.bfloat16
I32 = mybir.dt.int32
ACT = mybir.ActivationFunctionType
AX = mybir.AxisListType

P = 128
B = 8
S = 256
D = 256
N = B * S
T = N // P
KC = D // P
TB = S // P
BS = 256
BT = BS // P
XROWS = N + 38 * BS
BIG = 3.0e38


def wait(e, sem, i, lo, a, b):
    if isinstance(i, int):
        if i * a + b > 0:
            e.wait_ge(sem, i * a + b)
    else:
        assert lo * a + b > 0, (lo, a, b)
        e.wait_ge(sem, i * a + b)


def run_loop(e, n, cuts, body, start=0):
    edges = sorted({start, n, *[c for c in cuts if start < c < n]})
    for lo, end in zip(edges, edges[1:]):
        if end - lo == 1:
            body(lo, lo, lo)
        else:
            with e.Fori(lo, end) as i:
                body(i, lo, end - 1)


def rsqrt(v, y, var, tmp, eps):
    v.tensor_scalar(var, var, eps, None, ALU.add)
    v.drain()
    v.tensor_scalar(y.bitcast(I32), var.bitcast(I32), -0.5, float(0x5F3759DF), ALU.mult, ALU.add)
    v.drain()
    for _ in range(3):
        v.scalar_tensor_tensor(tmp, y, -0.5, y, ALU.mult, ALU.mult)
        v.drain()
        v.tensor_tensor(tmp, tmp, var, ALU.mult)
        v.drain()
        v.scalar_tensor_tensor(y, tmp, 1.5, y, ALU.add, ALU.mult)
        v.drain()


def layer_norm(v, dst, src, st, n, eps):
    for t in range(n):
        v.bn_stats(st["bn"][:, t, :], src[:, t, :])
    v.drain()
    for t in range(n):
        v.bn_aggr(st["mv"][:, t, :], st["bn"][:, t, :])
    v.drain()
    rsqrt(v, st["rstd"][:, 0:n], st["mv"][:, 0:n, 1], st["tmp"][:, 0:n], eps)
    for t in range(n):
        v.tensor_scalar(dst[:, t, :], src[:, t, :], st["mv"][:, t, 0:1], st["rstd"][:, t:t + 1],
                        ALU.subtract, ALU.mult)
    v.drain()


def mm3(pe, out, lhs, rhs, first, last, **kw):
    pe.matmul(out, lhs[0], rhs[0], start=first, stop=False, **kw)
    pe.matmul(out, lhs[0], rhs[1], start=False, stop=False, **kw)
    return pe.matmul(out, lhs[1], rhs[0], start=False, stop=last, **kw)


class Alloc:

    def __init__(self, nc, ctx, name):
        self.nc, self.ctx, self.name, self.sems = nc, ctx, name, []
        ctx.callback(self.close)

    def close(self):
        if self.sems:
            self.nc.clear_and_free_semaphores(self.sems)
            self.nc.all_engine_barrier()

    def sb(self, name, shape, dt=F32):
        return self.ctx.enter_context(self.nc.sbuf_tensor(f"{self.name}_{name}", shape, dt))

    def ps(self, name, shape, dt=F32):
        return self.ctx.enter_context(self.nc.psum_tensor(f"{self.name}_{name}", shape, dt))

    def sem(self, name):
        self.sems.append(self.nc.alloc_semaphore(f"{self.name}_{name}"))
        return self.sems[-1]



def moe_phase(nc, G, name, layer, E, K, FC, glu, func, shared, w_dram, rw_dram, rb_dram=None,
              biases=False, renorm=False, eps_sum=0.0, cap=None, clip=None, inner_norm=None, add_input=False):
    NB = (N * K + E * (BS - 1)) // BS
    SJ = N // BS if shared else 0
    NJ = (SJ + NB + 1) // 2 * 2
    NR = NJ - SJ
    NI = NJ // 2
    BASE = N if shared else 0
    ROWS = BASE + NR * BS
    W1 = (2 if glu else 1) * P
    WW = KC * W1 + D
    CW = WW + (1 + P if biases else 0)
    NS = 4
    CI = 2 * FC
    per_slot = CI // NS
    assert CI % NS == 0 and ROWS <= XROWS
    rows_x, rows_y = G["rows_x"], G["rows_y"]
    x, ident = G["x"], G["ident"]
    tg = G["tanh_g"][:, 4 + layer:5 + layer]

    with ExitStack() as ctx:
        A = Alloc(nc, ctx, name)
        sb, ps, sem = A.sb, A.ps, A.sem
        n_all = sb("n_all", [P, T, D])
        st = {"bn": sb("bn", [P, 4, 6]), "mv": sb("mv", [P, 4, 2]), "rstd": sb("rstd", [P, 4]), "tmp": sb("tmp", [P, 4])}
        p_k = [sb(f"p_{k}", [P, T]) for k in range(K)]
        slot_w = sb("slot_w", [P, T, K], I32)
        slot_r = sb("slot_r", [P, T, K], I32)
        blk = sb("blk", [P, NR], I32)

        with ExitStack() as c2:
            R = Alloc(nc, c2, name + "r")
            nT = [R.sb(f"nT_{h}", [P, 2, KC, 512], F32R) for h in ("hi", "lo")]
            rw = R.sb("rw", [P, KC, E])
            rwh, rwl = R.sb("rwh", [P, KC, E], F32R), R.sb("rwl", [P, KC, E], F32R)
            lgT = R.sb("lgT", [P, 2, 512])
            lg, ex = R.sb("lg", [P, T, E]), R.sb("ex", [P, T, E])
            t1, t2 = R.sb("t1", [P, T, E]), R.sb("t2", [P, T, E])
            oh = [R.sb(f"oh{k}", [P, T, E]) for k in range(K)]
            m, r = R.sb("m", [P, T]), R.sb("r", [P, T])
            Mb = R.sb("Mb", [P, T, E], BF16)
            cnt, cnti = R.sb("cnt", [P, E]), R.sb("cnti", [P, E], I32)
            offs, ends = R.sb("offs", [P, E]), R.sb("ends", [P, E])
            tE = R.sb("tE", [P, E, E])
            tB, nblk = R.sb("tB", [P, NR, E]), R.sb("nblk", [P, NR])
            keep = R.sb("keep", [P, T])
            gb = None
            if inner_norm:
                gb = R.sb("gb", [P, 2, D])
            rb = R.sb("rb", [P, E]) if rb_dram is not None else None
            trp = [R.ps(f"trp{q}", [P, 512]) for q in range(2)]
            lgp = R.ps("lgp", [P, 512])
            ltp = R.ps("ltp", [P, T, E])
            rank = R.ps("rank", [P, T, E])
            cntp = R.ps("cntp", [P, 512])
            loaded, n_ready, tr_ready, nT_hi, nT_ready = (R.sem(s) for s in ("loaded", "n_ready", "tr_ready", "nT_hi", "nT_ready"))
            rw_ready, lg_ready, lgT_ready, lt_ready = (R.sem(s) for s in ("rw_ready", "lg_ready", "lgT_ready", "lt_ready"))
            shifted, exped, mask_ready, rank_ready, rows_out = (R.sem(s) for s in ("shifted", "exped", "mask_ready", "rank_ready", "rows_out"))
            n_loads = 1 + 2 * bool(inner_norm) + (rb is not None)
            QT = T // 4

            with nc.Block() as block:
                @block.sync
                def _(sp):
                    sp.dma_start(rw[:, :, :], rw_dram).then_inc(loaded, 16)
                    if inner_norm:
                        for q in range(2):
                            sp.dma_start(gb[:, q, :], inner_norm[q].rearrange("(a d) -> a d", a=1).broadcast_to([P, D])).then_inc(loaded, 16)
                    if rb is not None:
                        sp.dma_start(rb[:, :], rb_dram.rearrange("(a d) -> a d", a=1).broadcast_to([P, E])).then_inc(loaded, 16)
                    for q in range(QT if shared else 0):
                        sp.wait_ge(n_ready, q + 1)
                        sp.dma_start(rows_x[512 * q:512 * (q + 1), :].rearrange("(t p) d -> p t d", p=P),
                                     n_all[:, 4 * q:4 * q + 4, :]).then_inc(rows_out, 16)
                    if shared:
                        sp.wait_ge(rows_out, 16 * QT)

                @block.scalar
                def _(act):
                    act.wait_ge(loaded, 16 * n_loads)
                    act.activation(rwh[:, :, :], rw[:, :, :], ACT.Copy).then_inc(rw_ready, 1)
                    for q in range(QT):
                        for k in range(KC):
                            u = 2 * q + k
                            act.wait_ge(tr_ready, u + 1)
                            if u >= 4:
                                act.wait_ge(lg_ready, q - 1)
                            act.activation(nT[0][:, q % 2, k, :], trp[k][:, :], ACT.Copy).then_inc(nT_hi, 1)
                        act.wait_ge(lg_ready, q + 1)
                        if q >= 2:
                            act.wait_ge(lt_ready, q - 1)
                        act.activation(lgT[0:E, q % 2, :], lgp[0:E, :], ACT.Copy).then_inc(lgT_ready, 1)
                    act.wait_ge(shifted, 1)
                    act.activation(ex[:, :, :], t1[:, :, :], ACT.Exp).then_inc(exped, 1)

                @block.tensor
                def _(pe):
                    for q in range(QT):
                        pe.wait_ge(n_ready, q + 1)
                        for k in range(KC):
                            if q >= 1:
                                pe.wait_ge(nT_ready, 2 * (q - 1) + k + 1)
                            for t in range(4):
                                mm = pe.transpose(trp[k][:, t * P:(t + 1) * P],
                                                  n_all[:, 4 * q + t, k * P:(k + 1) * P], ident[:, :])
                            mm.then_inc(tr_ready, 1)
                        if q == 0:
                            pe.wait_ge(rw_ready, 2)
                        if q >= 1:
                            pe.wait_ge(lgT_ready, q)
                        pe.wait_ge(nT_ready, 2 * (q + 1))
                        for k in range(KC):
                            mm = mm3(pe, lgp[0:E, :], (rwh[:, k, :], rwl[:, k, :]),
                                     (nT[0][:, q % 2, k, :], nT[1][:, q % 2, k, :]), k == 0, k == KC - 1)
                        mm.then_inc(lg_ready, 1)
                        pe.wait_ge(lgT_ready, q + 1)
                        for t in range(4):
                            mm = pe.transpose(ltp[:, 4 * q + t, :], lgT[0:E, q % 2, t * P:(t + 1) * P], ident[0:E, 0:E])
                        mm.then_inc(lt_ready, 1)
                    pe.wait_ge(mask_ready, 1)
                    for s in range(T - 1, 0, -1):
                        pe.matmul(rank[:, s:T, :], G["ones_bf"][:, :], Mb[:, 0:T - s, :], start=(s == T - 1), stop=False,
                                  skip_group_check=True)
                    pe.matmul(rank[:, :, :], G["before_bf"][:, :], Mb[:, :, :], start=False, stop=True, skip_group_check=True)
                    for t in range(T):
                        mm = pe.matmul(cntp[:, 0:E], G["ones_bf"][:, :], Mb[:, t, :], start=(t == 0), stop=(t == T - 1))
                    mm.then_inc(rank_ready, 1)

                @block.vector
                def _(v):
                    def bc_e(a):
                        return a[:, :].rearrange("p (t o) -> p t o", o=1).broadcast_to([P, T, E])

                    v.wait_ge(loaded, 16 * n_loads)
                    v.wait_ge(rw_ready, 1)
                    v.tensor_tensor(rwl[:, :, :], rw[:, :, :], rwh[:, :, :].bitcast(F32), ALU.subtract).then_inc(rw_ready, 1)

                    def lo_parts(q):
                        for k in range(KC):
                            u = 2 * q + k
                            v.wait_ge(nT_hi, u + 1)
                            v.tensor_tensor(nT[1][:, q % 2, k, :], trp[k][:, :], nT[0][:, q % 2, k, :].bitcast(F32),
                                            ALU.subtract).then_inc(nT_ready, 1)

                    for q in range(QT):
                        blk4 = n_all[:, 4 * q:4 * q + 4, :]
                        layer_norm(v, blk4, x[:, 4 * q:4 * q + 4, :], st, 4, 1e-5)
                        if inner_norm:
                            layer_norm(v, blk4, blk4, st, 4, 1e-5)
                            for w, op in ((0, ALU.mult), (1, ALU.add)):
                                for t in range(4):
                                    ins = v.tensor_tensor(n_all[:, 4 * q + t, :], n_all[:, 4 * q + t, :], gb[:, w, :], op)
                                v.drain()
                        v.drain().then_inc(n_ready, 1)
                        if q:
                            lo_parts(q - 1)
                    lo_parts(QT - 1)
                    v.wait_ge(lt_ready, QT)
                    if rb is not None:
                        v.tensor_tensor(lg[:, :, :], ltp[:, :, :], rb[:, :].rearrange("p (o e) -> p o e", o=1).broadcast_to([P, T, E]), ALU.add)
                    elif clip:
                        v.tensor_scalar(lg[:, :, :], ltp[:, :, :], clip, -clip, ALU.min, ALU.max)
                    else:
                        v.tensor_copy(lg[:, :, :], ltp[:, :, :])
                    v.drain()
                    v.tensor_reduce(m[:, :], lg[:, :, :], AX.X, ALU.max)
                    v.drain()
                    v.tensor_tensor(t1[:, :, :], lg[:, :, :], bc_e(m), ALU.subtract).then_inc(shifted, 1)
                    v.wait_ge(exped, 1)
                    v.tensor_reduce(r[:, :], ex[:, :, :], AX.X, ALU.add)
                    v.drain()
                    if eps_sum and not renorm:
                        v.tensor_scalar(r[:, :], r[:, :], eps_sum, None, ALU.add)
                        v.drain()
                    v.reciprocal(r[:, :], r[:, :])
                    v.drain()
                    v.tensor_tensor(ex[:, :, :], ex[:, :, :], bc_e(r), ALU.mult)
                    v.drain()
                    iota = G["iota_e"][:, 0:E].rearrange("p (o e) -> p o e", o=1).broadcast_to([P, T, E])
                    for k in range(K):
                        v.tensor_reduce(p_k[k][:, :], ex[:, :, :], AX.X, ALU.max)
                        v.drain()
                        v.tensor_tensor(t1[:, :, :], ex[:, :, :], bc_e(p_k[k]), ALU.is_lt)
                        v.drain()
                        v.scalar_tensor_tensor(t1[:, :, :], t1[:, :, :], 64.0, iota, ALU.mult, ALU.add)
                        v.drain()
                        v.tensor_reduce(m[:, :], t1[:, :, :], AX.X, ALU.min)
                        v.drain()
                        v.tensor_tensor(oh[k][:, :, :], iota, bc_e(m), ALU.is_equal)
                        v.drain()
                        v.scalar_tensor_tensor(ex[:, :, :], oh[k][:, :, :], -4.0, ex[:, :, :], ALU.mult, ALU.add)
                        v.drain()
                    if renorm:
                        v.tensor_tensor(m[:, :], p_k[0][:, :], p_k[1][:, :], ALU.add)
                        v.drain()
                        v.tensor_scalar(m[:, :], m[:, :], eps_sum, None, ALU.add)
                        v.drain()
                        v.reciprocal(m[:, :], m[:, :])
                        v.drain()
                        for k in range(K):
                            v.tensor_tensor(p_k[k][:, :], p_k[k][:, :], m[:, :], ALU.mult)
                        v.drain()
                    v.tensor_tensor(t1[:, :, :], oh[0][:, :, :], oh[1][:, :, :], ALU.add)
                    v.drain()
                    for k in range(2, K):
                        v.tensor_tensor(t1[:, :, :], t1[:, :, :], oh[k][:, :, :], ALU.add)
                        v.drain()
                    v.tensor_copy(Mb[:, :, :], t1[:, :, :]).then_inc(mask_ready, 1)
                    v.wait_ge(rank_ready, 1)
                    if cap:
                        v.tensor_scalar(cnti[:, :], cntp[:, 0:E], float(cap), float(BS - 1), ALU.min, ALU.add)
                    else:
                        v.tensor_scalar(cnti[:, :], cntp[:, 0:E], float(BS - 1), None, ALU.add)
                    v.drain()
                    sh = BS.bit_length() - 1
                    v.tensor_scalar(cnti[:, :], cnti[:, :], sh, sh, ALU.logical_shift_right, ALU.logical_shift_left)
                    v.drain()
                    v.tensor_copy(cnt[:, :], cnti[:, :])
                    v.drain()
                    v.tensor_tensor(tE[:, :, :], cnt[:, :].rearrange("p (o e) -> p o e", o=1).broadcast_to([P, E, E]),
                                    G["below_e"][:, 0:E, 0:E], ALU.mult)
                    v.drain()
                    v.tensor_reduce(offs[:, :], tE[:, :, :], AX.X, ALU.add)
                    v.drain()
                    v.tensor_tensor(ends[:, :], offs[:, :], cnt[:, :], ALU.add)
                    v.drain()
                    v.tensor_tensor(tB[:, :, :], ends[:, :].rearrange("p (o e) -> p o e", o=1).broadcast_to([P, NR, E]),
                                    G["iota_b"][:, 0:NR].rearrange("p (b o) -> p b o", o=1).broadcast_to([P, NR, E]), ALU.is_le)
                    v.drain()
                    v.tensor_reduce(nblk[:, :], tB[:, :, :], AX.X, ALU.add)
                    v.drain()
                    v.tensor_scalar(blk[:, :], nblk[:, :], float(E - 1), float(shared), ALU.min, ALU.add)
                    if cap:
                        v.tensor_scalar(t2[:, :, :], rank[:, :, :], float(cap), None, ALU.is_lt)
                    v.tensor_tensor(lg[:, :, :], rank[:, :, :], offs[:, :].rearrange("p (o e) -> p o e", o=1).broadcast_to([P, T, E]), ALU.add)
                    v.drain()
                    for k in range(K):
                        v.tensor_tensor(t1[:, :, :], lg[:, :, :], oh[k][:, :, :], ALU.mult)
                        v.drain()
                        v.tensor_reduce(m[:, :], t1[:, :, :], AX.X, ALU.add)
                        v.drain()
                        if cap:
                            v.tensor_tensor(t1[:, :, :], t2[:, :, :], oh[k][:, :, :], ALU.mult)
                            v.drain()
                            v.tensor_reduce(keep[:, :], t1[:, :, :], AX.X, ALU.add)
                            v.drain()
                            v.tensor_tensor(p_k[k][:, :], p_k[k][:, :], keep[:, :], ALU.mult)
                            v.tensor_scalar(r[:, :], keep[:, :], -1.0e6, 1.0e6 + BASE, ALU.mult, ALU.add)
                            v.drain()
                            v.tensor_tensor(m[:, :], m[:, :], r[:, :], ALU.add)
                            v.drain()
                            v.tensor_copy(slot_w[:, :, k], m[:, :])
                            v.tensor_scalar(slot_r[:, :, k], m[:, :], float(ROWS - 1), None, ALU.min)
                        else:
                            v.tensor_scalar(slot_w[:, :, k], m[:, :], float(BASE), None, ALU.add)
                            v.tensor_scalar(slot_r[:, :, k], m[:, :], float(BASE), None, ALU.add)
                        v.tensor_scalar(p_k[k][:, :], p_k[k][:, :], tg, None, ALU.mult)
                        v.drain()

        with ExitStack() as c2:
            M = Alloc(nc, c2, name + "m")
            raw = [M.sb(f"raw{s}", [P, CW]) for s in range(NS)]
            whi = [M.sb(f"whi{s}", [P, WW], F32R) for s in range(NS)]
            wlo = [M.sb(f"wlo{s}", [P, WW], F32R) for s in range(NS)]
            b12 = [M.sb(f"b12_{s}", [P, 1 + P]) for s in range(NS)] if biases else None
            xr = [M.sb(f"xr{q}", [P, BT, D]) for q in range(2)]
            xT = [[M.sb(f"xT{h}{q}", [P, KC, BS], F32R) for q in range(2)] for h in ("hi", "lo")]
            act_sb = [M.sb(f"act{q}", [P, BS]) for q in range(2)]
            h_f = [M.sb(f"h_f{q}", [P, BS]) for q in range(2)] if glu else act_sb
            hh = [[M.sb(f"h{h}{q}", [P, BS], F32R) for q in range(2)] for h in ("hi", "lo")]
            y_sb = [M.sb(f"y{q}", [P, BT, D]) for q in range(2)]
            NG = 4
            gath = [M.sb(f"gath{q}", [P, K + 1, D]) for q in range(NG)]
            gu = [M.ps(f"gu{q}", [P, 512]) for q in range(2)]
            yp = [M.ps(f"yp{q}", [P, 512]) for q in range(2)]
            xtp = [M.ps(f"xtp{q}", [P, 512]) for q in range(2)]
            w_in = [M.sem(f"w_in{s}") for s in range(NS)]
            x_in = [M.sem(f"x_in{q}") for q in range(2)]
            y_out = [M.sem(f"y_out{q}") for q in range(2)]
            w_hi, w_lo_v, w_lo_p, b_ok, scattered, xt_ready, xT_hi, xT_lo, gu_ready, act_done, h_ready, h_used, y_copied = (
                M.sem(s) for s in ("w_hi", "w_lo_v", "w_lo_p", "b_ok", "scattered", "xt_ready", "xT_hi", "xT_lo", "gu_ready",
                                   "act_done", "h_ready", "h_used", "y_copied"))
            all_out = M.sem("all_out")
            g_in = [M.sem(f"g_in{q}") for q in range(NG)]
            s_in = [M.sem(f"s_in{q}") for q in range(NG)]
            g_used = M.sem("g_used")
            SI = SJ // 2
            CUTS = [1, 2, SI - 1, SI, SI + 1, NI - 1] if shared else [1, 2, NI - 1]

            def w_views(s):
                hi, lo = whi[s], wlo[s]
                first = [[(hi[:, k * W1 + g * P:k * W1 + (g + 1) * P], lo[:, k * W1 + g * P:k * W1 + (g + 1) * P])
                          for g in range(W1 // P)] for k in range(KC)]
                return first, (hi[:, KC * W1:WW], lo[:, KC * W1:WW])

            def in_shared(i, lo, hi, job):
                a, b = 2 * lo + job < SJ, 2 * hi + job < SJ
                assert a == b
                return a

            def of_lo(i, lo, hi, c):
                return (w_lo_v, CI, c + 1) if in_shared(i, lo, hi, c // FC) else (w_lo_p, CI, c + 1 - SJ * FC)

            def split_lo(e, i, lo, hi, c):
                s = c % NS
                wait(e, b_ok if biases else w_hi, i, lo, CI, c + 1)
                wait(e, h_used, i, lo, CI, c - NS + 1)
                e.tensor_tensor(wlo[s][:, :], raw[s][:, 0:WW], whi[s][:, :].bitcast(F32), ALU.subtract).then_inc(
                    w_lo_v if in_shared(i, lo, hi, c // FC) else w_lo_p, 1)

            with nc.Block() as block:
                @block.sync
                def _(sp):
                    def load_w(i, lo, hi, c, expert):
                        s = c % NS
                        src = w_dram[expert, c % FC] if isinstance(expert, int) else \
                            w_dram[bass.ds(expert, 1), c % FC].rearrange("o p w -> (o p) w")
                        sem, a, b = of_lo(i, lo, hi, c - NS)
                        wait(sp, sem, i, lo, a, b)
                        sp.dma_start(raw[s][:, :], src).then_inc(w_in[s], 16)

                    def load_x(i, lo, hi, job):
                        q, rows = job % 2, rows_of(rows_x, i, job)
                        wait(sp, xt_ready, i, lo, 2, job - 1)
                        sp.dma_start(xr[q][:, :, :], rows).then_inc(x_in[q], 16)

                    def rows_of(dram, i, job):
                        a = (2 * i + job) * BS
                        if isinstance(i, int):
                            return dram[a:a + BS, :].rearrange("(t p) d -> p t d", p=P)
                        return dram[bass.ds(sp.snap(a), BS), :].rearrange("(t p) d -> p t d", p=P)

                    def expert_of(i, lo, hi, job):
                        if in_shared(i, lo, hi, job):
                            return 0
                        at = 2 * i + (job - SJ)
                        ap = blk[0:1, at:at + 1] if isinstance(i, int) else blk[0:1, bass.ds(at, 1)]
                        return sp.value_load(ap, min_val=0, max_val=E - 1 + shared)

                    first = [expert_of(0, 0, 0, j) for j in range((NS - 1) // FC + 1)]
                    for c in range(NS):
                        load_w(0, 0, 0, c, first[c // FC])
                    if not shared:
                        sp.wait_ge(scattered, 16 * T * K)
                    load_x(0, 0, 0, 0)
                    load_x(0, 0, 0, 1)

                    def body(i, lo, hi):
                        known = {}
                        for c in range(CI):
                            j, cj = divmod(c, FC)
                            if cj == 0:
                                if hi < NI - 1 or j < 0:
                                    if shared and lo == SI - 1 and j == 0:
                                        sp.wait_ge(scattered, 16 * T * K)
                                    load_x(i, lo, hi, j + 2)
                            if hi < NI - 1 or c + NS < CI:
                                tj = (c + NS) // FC
                                if tj not in known:
                                    known[tj] = expert_of(i, lo, hi, tj)
                                load_w(i, lo, hi, c + NS, known[tj])
                            if cj == min(1, FC - 1):
                                if not (lo == 0 and j == 0):
                                    store_y(i, lo, hi, j - 1)

                    def store_y(i, lo, hi, job):
                        q, rows = job % 2, rows_of(rows_y, i, job)
                        wait(sp, y_copied, i, lo, 2, job + 1)
                        sp.dma_start(rows, y_sb[q][:, :, :]).then_inc(y_out[q], 16)

                    run_loop(sp, NI, CUTS, body)
                    store_y(NI - 1, NI - 1, NI - 1, 1)
                    for q in range(2):
                        sp.wait_ge(y_out[q], 16 * NI)
                    sp.nop().then_inc(all_out, 1)
                    if shared:
                        for t in range(T):
                            if t >= NG:
                                sp.wait_ge(g_used, t - NG + 1)
                            sp.dma_start(gath[t % NG][:, K, :], rows_y[t * P:(t + 1) * P, :]).then_inc(s_in[t % NG], 16)

                @block.gpsimd
                def _(pool):
                    def scatter(t, k):
                        pool.indirect_dma_start(out=rows_x[0:ROWS, :],
                                                out_offset=bass.IndirectOffsetOnAxis(ap=slot_w[:, t, k:k + 1], axis=0),
                                                in_=n_all[:, t, :], in_offset=None,
                                                bounds_check=ROWS - 1, oob_is_err=False).then_inc(scattered, 16)

                    for t in range(T):
                        for k in range(K):
                            scatter(t, k)

                    if not shared:
                        for c in range(2):
                            split_lo(pool, 0, 0, 0, c)

                    def body(i, lo, hi):
                        for c in range(2, CI + 2):
                            if hi == NI - 1 and c >= CI:
                                continue
                            if not in_shared(i, lo, hi, c // FC):
                                split_lo(pool, i, lo, hi, c)

                    run_loop(pool, NI, CUTS, body, start=max(SI - 1, 0))
                    pool.wait_ge(all_out, 1)
                    for t in range(T):
                        if t >= NG:
                            pool.wait_ge(g_used, t - NG + 1)
                        for k in range(K):
                            pool.indirect_dma_start(out=gath[t % NG][:, k, :], out_offset=None, in_=rows_y[0:ROWS, :],
                                                    in_offset=bass.IndirectOffsetOnAxis(ap=slot_r[:, t, k:k + 1], axis=0)
                                                    ).then_inc(g_in[t % NG], 16)

                @block.scalar
                def _(act):
                    def split_hi(i, lo, hi, c):
                        s = c % NS
                        wait(act, w_in[s], i, lo, 16 * per_slot, 16 * (c // NS + 1))
                        wait(act, h_used, i, lo, CI, c - NS + 1)
                        act.activation(whi[s][:, :], raw[s][:, 0:WW], ACT.Copy).then_inc(w_hi, 1)

                    def x_hi(i, lo, hi, job):
                        wait(act, xt_ready, i, lo, 2, job + 1)
                        wait(act, gu_ready, i, lo, CI, FC * (job - 1))
                        act.activation(xT[0][job % 2][:, :, :], xtp[job % 2][:, :].rearrange("p (k n) -> p k n", k=KC), ACT.Copy).then_inc(xT_hi, 1)

                    def copy_y(i, lo, hi, job):
                        q = job % 2
                        wait(act, h_used, i, lo, CI, FC * (job + 1))
                        wait(act, y_out[q], i, lo, 16, 16 * ((job - 2 - q) // 2 + 1))
                        act.activation(y_sb[q][:, :, :], yp[q][:, :].rearrange("p (t n) -> p t n", t=BT), ACT.Copy).then_inc(y_copied, 1)

                    split_hi(0, 0, 0, 0)
                    x_hi(0, 0, 0, 0)
                    split_hi(0, 0, 0, 1)

                    def body(i, lo, hi):
                        for c in range(CI):
                            j, cj = divmod(c, FC)
                            last = hi == NI - 1
                            wait(act, gu_ready, i, lo, CI, c + 1)
                            if glu:
                                wait(act, h_ready, i, lo, CI, c - 1)
                                act.activation(act_sb[c % 2][:, :], gu[c % 2][:, 0:BS], func).then_inc(act_done, 1)
                            else:
                                wait(act, h_ready, i, lo, CI, c - 1)
                                if biases:
                                    wait(act, b_ok, i, lo, CI, c + 1)
                                    act.activation(h_f[c % 2][:, :], gu[c % 2][:, 0:BS], func, bias=b12[c % NS][:, 0:1]).then_inc(act_done, 1)
                                else:
                                    act.activation(h_f[c % 2][:, :], gu[c % 2][:, 0:BS], func).then_inc(act_done, 1)
                            if not (last and c + 2 >= CI):
                                split_hi(i, lo, hi, c + 2)
                            if cj == 0 and not (last and j == 1):
                                x_hi(i, lo, hi, j + 1)
                            if not biases and cj == 0 and not (lo == 0 and j == 0):
                                copy_y(i, lo, hi, j - 1)

                    run_loop(act, NI, CUTS, body)
                    if not biases:
                        copy_y(NI - 1, NI - 1, NI - 1, 1)

                @block.vector
                def _(v):
                    def x_lo(i, lo, hi, job):
                        wait(v, xT_hi, i, lo, 2, job + 1)
                        v.tensor_tensor(xT[1][job % 2][:, :, :], xtp[job % 2][:, :].rearrange("p (k n) -> p k n", k=KC),
                                        xT[0][job % 2][:, :, :].bitcast(F32), ALU.subtract).then_inc(xT_lo, 1)

                    def take_b(i, lo, hi, c):
                        s = c % NS
                        wait(v, w_hi, i, lo, CI, c + 1)
                        wait(v, h_used, i, lo, CI, c - NS + 1)
                        v.tensor_copy(b12[s][:, :], raw[s][:, WW:CW]).then_inc(b_ok, 1)

                    def y_bias(i, lo, hi, job):
                        q = job % 2
                        wait(v, h_used, i, lo, CI, FC * (job + 1))
                        wait(v, y_out[q], i, lo, 16, 16 * ((job - 2 - q) // 2 + 1))
                        for cj in range(FC):
                            s = (job * FC + cj) % NS
                            b2 = b12[s][:, 1:1 + P].rearrange("p (o n) -> p o n", o=1).broadcast_to([P, BT, P])
                            ins = v.tensor_tensor(y_sb[q][:, :, cj * P:(cj + 1) * P],
                                                  yp[q][:, :].rearrange("p (t n) -> p t n", t=BT)[:, :, cj * P:(cj + 1) * P], b2, ALU.add)
                        ins.then_inc(y_copied, 1)

                    if biases:
                        take_b(0, 0, 0, 0)
                        take_b(0, 0, 0, 1)
                    if shared:
                        split_lo(v, 0, 0, 0, 0)
                        split_lo(v, 0, 0, 0, 1)
                    x_lo(0, 0, 0, 0)

                    def body(i, lo, hi):
                        for c in range(CI):
                            j, cj = divmod(c, FC)
                            last = hi == NI - 1
                            if biases and cj == 0 and not (lo == 0 and j == 0):
                                y_bias(i, lo, hi, j - 1)
                            wait(v, act_done, i, lo, CI, c + 1)
                            q = c % 2
                            if glu:
                                v.tensor_tensor(h_f[q][:, :], act_sb[q][:, :], gu[q][:, BS:2 * BS], ALU.mult)
                                v.drain()
                            wait(v, h_used, i, lo, CI, c - 1)
                            v.tensor_copy(hh[0][q][:, :], h_f[q][:, :])
                            v.drain()
                            v.tensor_tensor(hh[1][q][:, :], h_f[q][:, :], hh[0][q][:, :].bitcast(F32), ALU.subtract).then_inc(h_ready, 1)
                            if not (last and c + 2 >= CI):
                                if biases:
                                    take_b(i, lo, hi, c + 2)
                                if in_shared(i, lo, hi, (c + 2) // FC):
                                    split_lo(v, i, lo, hi, c + 2)
                            if cj == 0 and not (last and j == 1):
                                x_lo(i, lo, hi, j + 1)

                    run_loop(v, NI, CUTS, body)
                    if biases:
                        y_bias(NI - 1, NI - 1, NI - 1, 1)
                    for t in range(T):
                        q = t % NG
                        v.wait_ge(g_in[q], 16 * K * (t // NG + 1))
                        if shared:
                            v.wait_ge(s_in[q], 16 * (t // NG + 1))
                            v.scalar_tensor_tensor(x[:, t, :], gath[q][:, K, :], tg, x[:, t, :], ALU.mult, ALU.add)
                            v.drain()
                        for k in range(K):
                            ins = v.scalar_tensor_tensor(x[:, t, :], gath[q][:, k, :], p_k[k][:, t:t + 1], x[:, t, :], ALU.mult, ALU.add)
                            v.drain()
                        if add_input:
                            v.scalar_tensor_tensor(x[:, t, :], n_all[:, t, :], tg, x[:, t, :], ALU.mult, ALU.add)
                        v.drain().then_inc(g_used, 1)

                @block.tensor
                def _(pe):
                    def x_turn(i, lo, hi, job):
                        q = job % 2
                        wait(pe, x_in[q], i, lo, 16, 16 * (job // 2 + 1))
                        wait(pe, xT_lo, i, lo, 2, job - 1)
                        for k in range(KC):
                            for t in range(BT):
                                mm = pe.transpose(xtp[q][:, k * BS + t * P:k * BS + (t + 1) * P], xr[q][:, t, k * P:(k + 1) * P], ident[:, :])
                        mm.then_inc(xt_ready, 1)

                    def first_product(i, lo, hi, c):
                        j, cj = divmod(c, FC)
                        q, s = j % 2, c % NS
                        if cj == 0:
                            wait(pe, xT_lo, i, lo, 2, j + 1)
                        wait(pe, w_hi, i, lo, CI, c + 1)
                        sem, a, b = of_lo(i, lo, hi, c)
                        wait(pe, sem, i, lo, a, b)
                        wait(pe, h_ready, i, lo, CI, c - 1)
                        w, _ = w_views(s)
                        for g in range(W1 // P):
                            for k in range(KC):
                                mm = mm3(pe, gu[c % 2][:, g * BS:(g + 1) * BS], w[k][g],
                                         (xT[0][q][:, k, :], xT[1][q][:, k, :]), k == 0, k == KC - 1)
                        mm.then_inc(gu_ready, 1)

                    def second_product(i, lo, hi, c):
                        j, cj = divmod(c, FC)
                        q, s = j % 2, c % NS
                        wait(pe, h_ready, i, lo, CI, c + 1)
                        if cj == 0:
                            wait(pe, y_copied, i, lo, 2, j - 1)
                        _, w = w_views(s)
                        for t in range(BT):
                            h = (hh[0][c % 2][:, t * P:(t + 1) * P], hh[1][c % 2][:, t * P:(t + 1) * P])
                            mm = mm3(pe, yp[q][:, t * D:(t + 1) * D], h, w, cj == 0 and t == 0, cj == FC - 1 and t == BT - 1,
                                     skip_group_check=True)
                        mm.then_inc(h_used, 1)

                    x_turn(0, 0, 0, 0)
                    first_product(0, 0, 0, 0)

                    def body(i, lo, hi):
                        last = hi == NI - 1
                        for c in range(CI):
                            j, cj = divmod(c, FC)
                            if cj == 0 and not (last and j == 1):
                                x_turn(i, lo, hi, j + 1)
                            if not (last and c == CI - 1):
                                first_product(i, lo, hi, c + 1)
                            second_product(i, lo, hi, c)

                    run_loop(pe, NI, CUTS, body)



def constants():
    i = np.arange(P)
    e = np.arange(16)
    f = np.arange(S, dtype=np.float32)[:, None] * (1.0 / 10000.0 ** (np.arange(0, 16, 2, dtype=np.float32) / 16)).astype(np.float32)[None]
    cs = np.stack([np.cos(f), -np.sin(f), np.sin(f)], 1).astype(np.float32).reshape(TB, P, 3, 8).transpose(1, 0, 2, 3)
    later = np.where(np.arange(S)[None, :] > np.arange(S)[:, None], 1e9, 0.0).astype(np.float32).reshape(TB, P, S).transpose(1, 0, 2)
    return {
        "rotary": np.ascontiguousarray(cs),
        "causal": np.ascontiguousarray(later),
        "ident": np.eye(P, dtype=np.float32),
        "before": (i[:, None] < i[None, :]).astype(np.float32),
        "below_e": np.broadcast_to((e[None, :] < e[:, None]).astype(np.float32), (P, 16, 16)).copy(),
        "iota_e": np.broadcast_to(e.astype(np.float32), (P, 16)).copy(),
        "iota_b": np.broadcast_to((BS * np.arange(40)).astype(np.float32), (P, 40)).copy(),
    }


def setup_phase(nc, G, I):
    with ExitStack() as ctx:
        A = Alloc(nc, ctx, "set")
        loaded, cast, zeroed, z_out = A.sem("loaded"), A.sem("cast"), A.sem("zeroed"), A.sem("z_out")
        zeros = A.sb("zeros", [P, 4, D])
        before = A.sb("before", [P, P])
        g8 = A.sb("g8", [P, 8])
        c_raw = [A.sb(f"c_raw{q}", [P, TB, D]) for q in range(2)]
        cT = [[A.sb(f"cT_{h}{q}", [P, KC, S], F32R) for q in range(2)] for h in ("hi", "lo")]
        c_ps = [A.ps(f"c_ps{q}", [P, KC, S]) for q in range(2)]
        c_in = [A.sem(f"c_in{q}") for q in range(2)]
        c_out = [A.sem(f"c_out{q}") for q in range(2)]
        c_turned, c_hi, c_lo = A.sem("c_turned"), A.sem("c_hi"), A.sem("c_lo")
        with nc.Block() as block:
            @block.sync
            def _(sp):
                sp.dma_start(G["x"][:, :, :], I["x"].rearrange("b (t p) d -> p (b t) d", p=P)).then_inc(loaded, 16)
                for q, name in enumerate(("g_xattn", "g_ffn")):
                    sp.dma_start(g8[:, 4 * q:4 * q + 4], I[name].rearrange("(a n) -> a n", a=1).broadcast_to([P, 4])).then_inc(loaded, 16)
                for name in ("ident", "below_e", "iota_e", "iota_b"):
                    sp.dma_start(G[name].ap(), I[name]).then_inc(loaded, 16)
                sp.dma_start(before[:, :], I["before"]).then_inc(loaded, 16)
                def load_c(b):
                    if b >= 2:
                        sp.wait_ge(c_turned, b - 1)
                    sp.dma_start(c_raw[b % 2][:, :, :], I["ctx_1024"][b].rearrange("(t p) d -> p t d", p=P)).then_inc(c_in[b % 2], 16)

                load_c(0)
                load_c(1)
                for b in range(B):
                    sp.wait_ge(c_lo, b + 1)
                    for h in range(2):
                        sp.dma_start(G["ctxT"][h][b], cT[h][b % 2][:, :, :].bitcast(F32)).then_inc(c_out[b % 2], 16)
                    if b + 2 < B:
                        load_c(b + 2)
                for q in range(2):
                    sp.wait_ge(c_out[q], 16 * B)
                sp.wait_ge(zeroed, 1)
                for r in range(0, XROWS, 512):
                    sp.dma_start(G["rows_x"][r:r + 512, :].rearrange("(p t) d -> p t d", p=P), zeros[:, :, :]).then_inc(z_out, 16)
                sp.wait_ge(z_out, 16 * len(range(0, XROWS, 512)))
                sp.wait_ge(loaded, 16 * 8)

            @block.vector
            def _(v):
                v.memset(zeros[:, :, :], 0.0).then_inc(zeroed, 1)
                v.memset(G["ones_bf"][:, :], 1.0)
                v.wait_ge(loaded, 16 * 8)
                v.tensor_copy(G["before_bf"][:, :], before[:, :])
                for b in range(B):
                    v.wait_ge(c_hi, b + 1)
                    v.tensor_tensor(cT[1][b % 2][:, :, :], c_ps[b % 2][:, :, :], cT[0][b % 2][:, :, :].bitcast(F32), ALU.subtract).then_inc(c_lo, 1)

            @block.scalar
            def _(act):
                act.wait_ge(loaded, 16 * 8)
                act.activation(G["tanh_g"][:, :], g8[:, :], ACT.Tanh)
                act.activation(G["identr"][:, :], G["ident"][:, :], ACT.Copy)
                for b in range(B):
                    act.wait_ge(c_turned, b + 1)
                    if b >= 2:
                        act.wait_ge(c_out[b % 2], 32 * (b // 2))
                    act.activation(cT[0][b % 2][:, :, :], c_ps[b % 2][:, :, :], ACT.Copy).then_inc(c_hi, 1)

            @block.tensor
            def _(pe):
                pe.wait_ge(loaded, 16 * 8)
                for b in range(B):
                    pe.wait_ge(c_in[b % 2], 16 * (b // 2 + 1))
                    if b >= 2:
                        pe.wait_ge(c_lo, b - 1)
                    for k in range(KC):
                        for t in range(TB):
                            mm = pe.transpose(c_ps[b % 2][:, k, t * P:(t + 1) * P], c_raw[b % 2][:, t, k * P:(k + 1) * P], G["ident"][:, :])
                    mm.then_inc(c_turned, 1)


def globals_of(nc, A):
    G = {
        "x": A.sb("x", [P, T, D]),
        "ident": A.sb("ident", [P, P]),
        "identr": A.sb("identr", [P, P], F32R),
        "before_bf": A.sb("before_bf", [P, P], BF16),
        "ones_bf": A.sb("ones_bf", [P, P], BF16),
        "below_e": A.sb("below_e", [P, 16, 16]),
        "iota_e": A.sb("iota_e", [P, 16]),
        "iota_b": A.sb("iota_b", [P, 40]),
        "tanh_g": A.sb("tanh_g", [P, 8]),
        "rows_x": nc.dram_tensor("rows_x", [XROWS, D], F32).ap(),
        "ctxT": [nc.dram_tensor(f"ctxT_{h}", [B, P, KC, S], F32).ap() for h in ("hi", "lo")],
        "rows_y": nc.dram_tensor("rows_y", [XROWS, D], F32).ap(),
    }
    return G


def final_phase(nc, G, out):
    with ExitStack() as ctx:
        A = Alloc(nc, ctx, "fin")
        stored = A.sem("stored")
        with nc.Block() as block:
            @block.sync
            def _(sp):
                sp.dma_start(out.rearrange("b (t p) d -> p (b t) d", p=P), G["x"][:, :, :]).then_inc(stored, 16)
                sp.wait_ge(stored, 16)


def moe_layer(nc, G, I, layer):
    if layer == 0:
        moe_phase(nc, G, "moe0", 0, E=15, K=3, FC=2, glu=False, func=ACT.Relu, shared=True, w_dram=I["moe_w0"],
                  rw_dram=I["L0_ffn_router_W"].rearrange("(k p) e -> p k e", p=P), rb_dram=I["L0_ffn_router_b"], biases=True)
    if layer == 1:
        moe_phase(nc, G, "moe1", 1, E=8, K=2, FC=6, glu=True, func=ACT.Silu, shared=True, w_dram=I["moe_w1"],
                  rw_dram=I["rw1"].rearrange("(k p) e -> p k e", p=P), renorm=True, eps_sum=1e-20)
    if layer == 2:
        moe_phase(nc, G, "moe2", 2, E=8, K=2, FC=8, glu=True, func=ACT.Silu, shared=False, w_dram=I["moe_w2"],
                  rw_dram=I["rw2"].rearrange("(k p) e -> p k e", p=P), eps_sum=1e-12, cap=640, clip=10000.0,
                  inner_norm=(I["L2_ffn_ln_gamma"], I["L2_ffn_ln_beta"]))
    if layer == 3:
        moe_phase(nc, G, "moe3", 3, E=8, K=2, FC=8, glu=False, func=ACT.Gelu, shared=True, w_dram=I["moe_w3"],
                  rw_dram=I["L3_ffn_router_w"].rearrange("(k p) e -> p k e", p=P), add_input=True)


def pack_chunks(ups, down, b1=None, b2=None):
    e, _, f = ups[0].shape
    fc = -(-f // P)
    up = np.stack(ups, 2)
    up = np.pad(up, ((0, 0), (0, 0), (0, 0), (0, fc * P - f)))
    up = up.reshape(e, KC, P, len(ups), fc, P).transpose(0, 4, 2, 1, 3, 5)
    dn = np.pad(down, ((0, 0), (0, fc * P - f), (0, 0))).reshape(e, fc, P, D)
    parts = [up.reshape(e, fc, P, -1), dn]
    if b1 is not None:
        parts.append(b1.reshape(e, fc, P, 1))
        parts.append(np.broadcast_to(b2.reshape(e, fc, 1, P), (e, fc, P, P)))
    return np.ascontiguousarray(np.concatenate(parts, 3))


def lay_out(inp):
    a = {k: np.asarray(v) for k, v in inp.items()}
    tr = lambda w: np.swapaxes(w, -1, -2)
    cat = lambda s, e: np.concatenate([s[None], e], 0)
    out = dict(constants())
    for k in ("ctx_1024", "mask_BxS2_if1", "L1_xattn_bo", "L2_xattn_bq", "L2_xattn_bk", "L2_xattn_bv", "L2_xattn_bo", "L2_xattn_Wq",
              "L2_xattn_Wk", "L2_xattn_Wv", "L3_xattn_ln_gamma", "L3_xattn_ln_beta", "L3_xattn_w_q", "L3_xattn_w_out", "L3_xattn_b_out",
              "L3_xattn_gate", "L0_xattn_Wq", "L0_xattn_Wk", "L0_xattn_Wv", "L0_xattn_Wcq", "L0_xattn_Wck", "L0_xattn_Wcv",
              "L0_xattn_gamma", "L0_xattn_beta", "L0_xattn_W1", "L0_xattn_b1"):
        out[k] = a[k]
    turn = lambda w: np.ascontiguousarray(w.reshape(*w.shape[:-1], 16, 8, 2).swapaxes(-1, -2).reshape(w.shape))
    twice = lambda w: np.ascontiguousarray(np.broadcast_to(w.reshape(16, 1, 16, D), (16, 2, 16, D)).reshape(512, D))
    for n in ("q", "k"):
        out[f"L1_W{n}"] = turn(np.ascontiguousarray(tr(a[f"L1_xattn_W{n}"])))
        out[f"L1_b{n}"] = turn(a[f"L1_xattn_b{n}"])
    out["L1_Wv"], out["L1_bv"] = np.ascontiguousarray(tr(a["L1_xattn_Wv"])), a["L1_xattn_bv"]
    out["L1_Wo"], out["L2_Wo"] = twice(tr(a["L1_xattn_Wo"])), twice(a["L2_xattn_Wo"])
    out["mask2"] = a["mask_Bx1xS2_ik0"].reshape(B, S)
    out["L3_w_k"], out["L3_w_v"] = (np.ascontiguousarray(a["L3_xattn_w_kv"][:, 1024 * q:1024 * (q + 1)]) for q in range(2))
    for k in ("x", "g_xattn", "g_ffn", "L0_ffn_router_W", "L0_ffn_router_b", "L2_ffn_ln_gamma", "L2_ffn_ln_beta", "L3_ffn_router_w"):
        out[k] = a[k]
    out["moe_w0"] = pack_chunks([cat(a["L0_ffn_sW1"], a["L0_ffn_eW1"])], cat(a["L0_ffn_sW2"], a["L0_ffn_eW2"]),
                                cat(a["L0_ffn_sb1"], a["L0_ffn_eb1"]), cat(a["L0_ffn_sb2"], a["L0_ffn_eb2"]))
    out["moe_w1"] = pack_chunks([tr(cat(a["L1_ffn_shared_gate"], a["L1_ffn_expert_gate"])), tr(cat(a["L1_ffn_shared_up"], a["L1_ffn_expert_up"]))],
                                tr(cat(a["L1_ffn_shared_down"], a["L1_ffn_expert_down"])))
    out["rw1"] = np.ascontiguousarray(tr(a["L1_ffn_gate_w"]))
    w12 = tr(a["L2_ffn_W12"])
    out["moe_w2"] = pack_chunks([w12[:, :, :1024], w12[:, :, 1024:]], tr(a["L2_ffn_W3"]))
    out["rw2"] = np.ascontiguousarray(tr(a["L2_ffn_Wr"]))
    out["moe_w3"] = pack_chunks([np.concatenate([a["L3_ffn_shared_up"], a["L3_ffn_routed_up"]])], np.concatenate([a["L3_ffn_shared_down"], a["L3_ffn_routed_down"]]))
    return out



def norm_tiles(v, dst, src, st, gb, inner):
    layer_norm(v, dst, src, st, TB, 1e-5)
    if inner:
        layer_norm(v, dst, dst, st, TB, 1e-5)
        scale_shift(v, dst, gb)


def scale_shift(v, a, gb):
    for w, op in ((0, ALU.mult), (1, ALU.add)):
        v.tensor_tensor(a, a, gb[:, w, :].rearrange("p (o d) -> p o d", o=1).broadcast_to([P, TB, D]), op)
        v.drain()


def load_split(nc, name, jobs, st_cols):
    with ExitStack() as ctx:
        A = Alloc(nc, ctx, name)
        raw = [A.sb(f"raw{q}", [P, st_cols]) for q in range(2)]
        came = [A.sem(f"came{q}") for q in range(2)]
        hi_done, lo_done = A.sem("hi_done"), A.sem("lo_done")
        with nc.Block() as block:
            @block.sync
            def _(sp):
                for n, (src, hi, lo) in enumerate(jobs):
                    if n >= 2:
                        sp.wait_ge(lo_done, n - 1)
                    sp.dma_start(raw[n % 2][:, 0:src.shape[1]], src).then_inc(came[n % 2], 16)

            @block.scalar
            def _(act):
                for n, (src, hi, lo) in enumerate(jobs):
                    act.wait_ge(came[n % 2], 16 * (n // 2 + 1))
                    act.activation(hi, raw[n % 2][:, 0:src.shape[1]], ACT.Copy).then_inc(hi_done, 1)

            @block.vector
            def _(v):
                for n, (src, hi, lo) in enumerate(jobs):
                    v.wait_ge(hi_done, n + 1)
                    v.tensor_tensor(lo, raw[n % 2][:, 0:src.shape[1]], hi.bitcast(F32), ALU.subtract).then_inc(lo_done, 1)


def heads_phase(nc, G, I, name, layer, dh, weights, mask=None, rotary=False, inner=None, biases=None, gate=None):
    H = 16
    small = dh == 16
    GH = 4 if small else 2
    NGR = H // GH
    OC = NGR
    LEAD = 3
    scale = 1.0 / float(np.sqrt(dh))
    HD = H * dh
    if small:
        ROUNDS = [(1, "nT", 0), (3, "q", 0), (4, "k", 0), (5, "v", 0), (6, "qT", 0), (7, "kT", 0), (8, "qT", 1), (9, "kT", 1),
                  (10, "qT", 2), (11, "kT", 2), (13, "qT", 3), (14, "kT", 3)]
        OWN = []
    else:
        ROUNDS = [(1, "nT", 0), (2, "nT", 1), (3, "qT", 0), (5, "qT", 1), (6, "kT", 0), (7, "kT", 1), (9, "V0", 0), (9, "qT", 2),
                  (10, "kT", 2), (11, "V0", 1), (13, "qT", 3), (14, "kT", 3)]
        OWN = [(1, "V1", 0), (2, "V1", 1)]
    PRO = len(ROUNDS)
    BODY = sorted(OWN + ROUNDS, key=lambda r: r[0])
    NRD = len(BODY)
    assert PRO % 2 == 0 and NRD % 2 == 0

    with ExitStack() as ctx:
        A = Alloc(nc, ctx, name)
        sb, ps, sem = A.sb, A.ps, A.sem
        hl = lambda n, shape: [sb(f"{n}_{h}", shape, F32R) for h in ("hi", "lo")]
        x, ident, identr = G["x"], G["ident"], G["identr"]
        wq, wk, wv = (hl(n, [P, KC, HD]) for n in ("wq", "wk", "wv"))
        wo = hl("wo", [P, OC, D])
        jobs = []
        for w, src in ((wq, weights["q"]), (wk, weights["k"]), (wv, weights["v"])):
            for k in range(KC):
                jobs.append((src[k * P:(k + 1) * P, :], w[0][:, k, :], w[1][:, k, :]))
        for c in range(OC):
            jobs.append((weights["o"][c * P:(c + 1) * P, :], wo[0][:, c, :], wo[1][:, c, :]))
        load_split(nc, name + "w", jobs, HD)

        n_sb = sb("n", [P, TB, D])
        nT = hl("nT", [P, KC, S])
        cT = hl("cT", [P, KC, S])
        st = {"bn": sb("bn", [P, 4, 6]), "mv": sb("mv", [P, 4, 2]), "rstd": sb("rstd", [P, 4]), "tmp": sb("tmp", [P, 4])}
        tg = sb("tg", [P, 1])
        met = sb("met", [P, 5])
        bo = sb("bo", [P, D])
        gb = sb("gb", [P, 2, D]) if inner else None
        gate_sb = sb("gate", [P, 1]) if gate is not None else None
        if small:
            QT, KT = sb("QT", [P, 8, S], F32R), sb("KT", [P, 8, S], F32R)
            qf, kf, vf = sb("qf", [P, TB, D]), sb("kf", [P, TB, D]), sb("vf", [P, TB, D])
            qs, ks = (sb(n, [P, TB * H, 4, dh], F32R) for n in ("qs", "ks"))
            vp = sb("vp", [P, TB, 4, 640], F32R)
            b3 = sb("b3", [P, 3, D])
            msk = sb("msk", [P, TB, S])
            msk_next = sb("msk_next", [P, TB, S])
            mi = sb("mi", [P, B, S], I32)
            kq = sb("kq", [P, TB])
            s_m = [sb(f"s_m{q}", [P, TB, S]) for q in range(2)]
            if rotary:
                cs = sb("cs", [P, TB, 3, 8])
                r1, r2 = sb("turn1", [P, TB, D]), sb("turn2", [P, TB, D])
                causal = sb("causal", [P, TB, S])
        else:
            QT, KT = hl("QT", [P, H, S]), hl("KT", [P, 8, S])
            V = hl("V", [P, TB, HD])
        p_sb = [sb(f"p{q}", [P, TB, S]) for q in range(4)]
        nm, rs, ri = (sb(n, [P, 4, TB]) for n in ("nm", "rs", "ri"))
        pT = [[sb(f"pT{h}{q}", [P, KC, S], F32R) for q in range(2)] for h in ("hi", "lo")]
        OT = hl("OT", [P, OC, S])
        s_ps = [ps(f"s{q}", [P, TB, S]) for q in range(2)]
        t_ps = [ps(f"t{q}", [P, KC, S]) for q in range(2)]
        o_ps = [ps(f"o{q}", [P, 512]) for q in range(2)]
        r_ps = [ps(f"r{q}", [P, 512]) for q in range(2)]
        loaded, ready, c_in = sem("loaded"), sem("ready"), sem("c_in")
        s_ready, m_ready, e_done, r_done, n_done, t_ready, ph_done, pl_done, pv_done, oh_done, ol_done, out_ready, x_done = (
            sem(n) for n in ("s_ready", "m_ready", "e_done", "r_done", "n_done", "t_ready", "ph_done", "pl_done", "pv_done",
                             "oh_done", "ol_done", "out_ready", "x_done"))
        n_ready, rd_ready, rd_hi, rd_done, f_ready, v_half = (
            sem(n) for n in ("n_ready", "rd_ready", "rd_hi", "rd_done", "f_ready", "v_half"))
        vh_done = sem("vh_done")
        n_small = (3 + 2 + 2 * rotary) if small else 0
        N_LOADS = 1 + (2 if inner else 0) + (gate is not None) + n_small - (1 if small else 0)
        CUTS = [1, B - 1]

        def body_rounds(last):
            return [r for r in BODY if not last or r in OWN]

        def rounds_at(h, last):
            return [(pos, kind, part) for pos, (slot, kind, part) in enumerate(body_rounds(last)) if slot == h]

        def done_by(kind, part=0):
            return [(r[1], r[2]) for r in BODY].index((kind, part)) + 1

        with nc.Block() as block:
            @block.sync
            def _(sp):
                def row(dst, src, n):
                    sp.dma_start(dst, src.rearrange("(a d) -> a d", a=1).broadcast_to([P, n])).then_inc(loaded, 16)
                row(bo[:, :], weights["bo"], D)
                if inner:
                    for q in range(2):
                        row(gb[:, q, :], inner[q], D)
                if gate is not None:
                    row(gate_sb[:, :], gate, 1)
                if small:
                    for q in range(3):
                        row(b3[:, q, :], biases[q], D)
                    sp.dma_start(mi[:, :, :], mask.rearrange("b s -> (b s)").rearrange("(o n) -> o n", o=1).broadcast_to([P, B * S])
                                 .rearrange("p (b s) -> p b s", s=S)).then_inc(loaded, 16)
                    if rotary:
                        sp.dma_start(cs[:, :, :, :], I["rotary"]).then_inc(loaded, 16)
                        sp.dma_start(causal[:, :, :], I["causal"]).then_inc(loaded, 16)
                sp.wait_ge(loaded, 16 * N_LOADS)

            @block.scalar
            def _(act):
                if gate is not None:
                    act.wait_ge(loaded, 16 * N_LOADS)
                    act.activation(st["tmp"][:, 0:1], gate_sb[:, :], ACT.Tanh).then_inc(ready, 1)

            @block.vector
            def _(v):
                v.wait_ge(loaded, 16 * N_LOADS)
                if gate is not None:
                    v.wait_ge(ready, 1)
                    v.tensor_tensor(tg[:, :], st["tmp"][:, 0:1], G["tanh_g"][:, layer:layer + 1], ALU.mult)
                else:
                    v.tensor_copy(tg[:, :], G["tanh_g"][:, layer:layer + 1])
                v.drain()
                v.tensor_scalar(bo[:, :], bo[:, :], tg[:, :], None, ALU.mult)
                if small:
                    v.tensor_scalar(b3[:, 0, :], b3[:, 0, :], -scale, None, ALU.mult)
                    v.memset(vp[:, :, :, :].bitcast(F32), 0.0)
                else:
                    v.memset(QT[0][:, :, :].bitcast(F32), 0.0)
                    v.memset(QT[1][:, :, :].bitcast(F32), 0.0)

        def v_cols(kc, half, e):
            cols = vp[:, kc, 2 * half:2 * half + 2, :].rearrange("p g (j c) -> p g j c", c=P + 32)
            return cols[:, :, :, dh * e:dh * e + dh]

        def vf_cols(kc, half):
            return vf[:, kc, 128 * half:128 * half + 128].rearrange("p (g j d) -> p g j d", g=2, j=4)

        def bc_t(a, n):
            return a.rearrange("p (o n) -> p o n", o=1).broadcast_to([P, TB, n])

        with nc.Block() as block:
            @block.sync
            def _(sp):
                def load_c(i, lo, hi, nxt):
                    b = i + nxt
                    srcs = [G["ctxT"][h][b] if isinstance(b, int) else
                            G["ctxT"][h][bass.ds(sp.snap(b), 1)].rearrange("o p k s -> (o p) k s") for h in range(2)]
                    if small:
                        if not (isinstance(i, int) and i + nxt == 0):
                            wait(sp, rd_ready, i, lo, NRD, PRO + NRD * (nxt - 2) + done_by("v"))
                    elif not (isinstance(i, int) and i + nxt == 0):
                        wait(sp, rd_ready, i, lo, NRD, PRO + NRD * (nxt - 1) + done_by("V1", 1))
                    for h in range(2):
                        sp.dma_start(cT[h][:, :, :].bitcast(F32), srcs[h]).then_inc(c_in, 16)

                load_c(0, 0, 0, 0)

                def body(i, lo, hi):
                    if hi < B - 1:
                        load_c(i, lo, hi, 1)

                run_loop(sp, B, CUTS, body)

            @block.tensor
            def _(pe):
                def scores(i, lo, s):
                    h = s % H
                    q = s % 2
                    part = h // 4
                    if h % 4 == 0:
                        turn = s // H - 1
                        wait(pe, rd_done, i, lo, NRD, PRO + turn * NRD + done_by("kT", part))
                    wait(pe, m_ready if small else e_done, i, lo, H, s - 1)
                    for t in range(TB):
                        if small:
                            r = 64 * (h % 2)
                            mm = pe.matmul(s_ps[q][:, t, :], QT[r:r + 64, h // 2, t * P:(t + 1) * P], KT[r:r + 64, h // 2, :], start=True, stop=True)
                        else:
                            mm = mm3(pe, s_ps[q][:, t, :], [a[:, h, t * P:(t + 1) * P] for a in QT], [a[:, h // 2, :] for a in KT], True, True)
                    mm.then_inc(s_ready, 1)

                def turn_p(i, lo, s):
                    wait(pe, n_done, i, lo, H, s + 1)
                    wait(pe, pl_done, i, lo, H, s - 1)
                    for kc in range(KC):
                        for t in range(TB):
                            mm = pe.transpose(t_ps[s % 2][:, kc, t * P:(t + 1) * P], p_sb[s % 4][:, t, kc * P:(kc + 1) * P], ident[:, :])
                    mm.then_inc(t_ready, 1)

                def values(i, lo, s, last=False):
                    h = s % H
                    g = h // GH
                    if h % GH == 0:
                        wait(pe, ol_done, i, lo, NGR, (s // H) * NGR + g - 1)
                        if g == 1:
                            wait(pe, x_done, i, lo, 1, s // H)
                    wait(pe, pl_done, i, lo, H, s + 1)
                    if small:
                        if h == 0 or h == 8:
                            wait(pe, vh_done, i, lo, 2, 2 * (s // H) + 1 + h // 8)
                        out = o_ps[g % 2][:, 0:S]
                        for kc in range(KC):
                            for e in range(2):
                                mm = pe.matmul(out, vp[:, kc, h // 4, P * (h % 4):P * (h % 4) + P], pT[e][s % 2][:, kc, :], start=(h % GH == 0 and kc == 0 and e == 0),
                                               stop=(h % GH == GH - 1 and kc == KC - 1 and e == 1))
                    else:
                        if h == 0:
                            wait(pe, rd_done, i, lo, NRD, PRO + (s // H - 1) * NRD + done_by("V0", 1))
                        if h == 8:
                            wait(pe, rd_done, i, lo, NRD, PRO + (s // H) * NRD + 1 + [r[1:] for r in body_rounds(last)].index(("V1", 1)))
                        out = o_ps[g % 2][:, (h % 2) * S:(h % 2 + 1) * S]
                        for kc in range(KC):
                            mm = mm3(pe, out, [a[:, kc, (h // 2) * P:(h // 2 + 1) * P] for a in V], [a[s % 2][:, kc, :] for a in pT],
                                     kc == 0, kc == KC - 1)
                    mm.then_inc(pv_done, 1)

                def project(i, lo, nxt):
                    wait(pe, ol_done, i, lo, NGR, (nxt + 1) * NGR)
                    out = o_ps[1][:, :].rearrange("p (t d) -> p t d", t=TB)
                    for t in range(TB):
                        for c in range(OC):
                            mm = mm3(pe, out[:, t, :], [a[:, c, t * P:(t + 1) * P] for a in OT], [a[:, c, :] for a in wo], c == 0, c == OC - 1)
                    mm.then_inc(out_ready, 1)

                def round_(i, lo, a, pos, kind, part):
                    bank = r_ps[pos % 2]
                    wait(pe, rd_done, i, lo, NRD, a + pos - 1)
                    own = kind == "V1"
                    batch = (a - PRO) // NRD + (0 if own else 1)
                    if kind == "nT":
                        wait(pe, n_ready, i, lo, 1, batch + 1)
                        if small:
                            for k in range(KC):
                                for t in range(TB):
                                    mm = pe.transpose(bank[:, k * S + t * P:k * S + (t + 1) * P], n_sb[:, t, k * P:(k + 1) * P], ident[:, :])
                        else:
                            for t in range(TB):
                                mm = pe.transpose(bank[:, t * P:(t + 1) * P], n_sb[:, t, part * P:(part + 1) * P], ident[:, :])
                    elif small and kind in ("q", "k", "v"):
                        src, w = (nT, wq) if kind == "q" else (cT, wk if kind == "k" else wv)
                        if kind == "q":
                            wait(pe, rd_done, i, lo, NRD, a + pos - (done_by("q") - done_by("nT")) + 1)
                        if kind == "k":
                            wait(pe, c_in, i, lo, 32, 32 * (batch + 1))
                        for t in range(TB):
                            for k in range(KC):
                                mm = mm3(pe, bank[:, t * D:(t + 1) * D], [y[:, k, t * P:(t + 1) * P] for y in src], [y[:, k, :] for y in w],
                                         k == 0, k == KC - 1)
                    elif small:
                        src = qs if kind == "qT" else ks
                        if part == 0:
                            back = done_by(kind, 0) - done_by("q" if kind == "qT" else "k")
                            wait(pe, rd_done, i, lo, NRD, a + pos - back + 1)
                        flat = src[:, :, :, :].rearrange("p (t h) g d -> p t (h g d)", t=TB)
                        for c in range(2):
                            for t in range(TB):
                                mm = pe.transpose(bank[:, c * S + t * P:c * S + (t + 1) * P].bitcast(F32R),
                                                  flat[:, t, (2 * part + c) * P:(2 * part + c + 1) * P], identr[:, :])
                    elif kind in ("qT", "kT"):
                        src, w = (nT, wq) if kind == "qT" else (cT, wk)
                        if kind == "qT" and part == 0:
                            wait(pe, rd_done, i, lo, NRD, a + pos - (done_by("qT") - done_by("nT", 1)) + 1)
                        if kind == "kT" and part == 0:
                            wait(pe, c_in, i, lo, 32, 32 * (batch + 1))
                        for c in range(2):
                            for k in range(KC):
                                col = (2 * part + c) * P
                                mm = mm3(pe, bank[:, c * S:(c + 1) * S], [y[:, k, col:col + P] for y in w], [y[:, k, :] for y in src],
                                         k == 0, k == KC - 1)
                    else:
                        half = 512 * (kind == "V1")
                        for k in range(KC):
                            mm = mm3(pe, bank[:, :], [y[:, k, part * P:(part + 1) * P] for y in cT], [y[:, k, half:half + 512] for y in wv],
                                     k == 0, k == KC - 1)
                    mm.then_inc(rd_ready, 1)

                for pos, (_, kind, part) in enumerate(ROUNDS):
                    round_(0, 0, 0, pos, kind, part)
                for s in range(LEAD):
                    scores(0, 0, s)

                def body(i, lo, hi):
                    last = hi == B - 1
                    for h in range(H):
                        if not (last and h + LEAD >= H):
                            scores(i, lo, h + LEAD)
                        for pos, kind, part in rounds_at(h, last):
                            round_(i, lo, PRO, pos, kind, part)
                        turn_p(i, lo, h)
                        if not (lo == 0 and h == 0):
                            values(i, lo, h - 1, last)
                        if h == 2 and lo > 0:
                            project(i, lo, -1)

                run_loop(pe, B, CUTS, body)
                values(B - 1, B - 1, H - 1)
                project(B - 1, B - 1, 0)

            @block.scalar
            def _(act):
                def weights_of(i, lo, s):
                    wait(act, m_ready, i, lo, H, s + 1)
                    wait(act, t_ready, i, lo, H, s - 3)
                    src = s_m[s % 2] if small else s_ps[s % 2]
                    for t in range(TB):
                        ins = act.activation(p_sb[s % 4][:, t, :], src[:, t, :], ACT.Exp, bias=nm[:, s % 4, t:t + 1], scale=-1.0,
                                             accum_out=rs[:, s % 4, t:t + 1])
                    ins.then_inc(e_done, 1)

                def p_hi(i, lo, s):
                    wait(act, t_ready, i, lo, H, s + 1)
                    wait(act, pv_done, i, lo, H, s - 1)
                    act.activation(pT[0][s % 2][:, :, :], t_ps[s % 2][:, :, :], ACT.Copy).then_inc(ph_done, 1)

                def o_hi(i, lo, turn, g):
                    wait(act, pv_done, i, lo, H, turn * H + (g + 1) * GH)
                    if g == 0:
                        wait(act, out_ready, i, lo, 1, turn)
                    if small:
                        ins = act.activation(OT[0][:, g, :], o_ps[g % 2][:, 0:S], ACT.Copy)
                    else:
                        for e in range(2):
                            ins = act.activation(OT[0][64 * e:64 * e + 64, g, :], o_ps[g % 2][64 * e:64 * e + 64, e * S:(e + 1) * S], ACT.Copy)
                    ins.then_inc(oh_done, 1)

                def round_(i, lo, a, pos, kind, part):
                    bank = r_ps[pos % 2]
                    both = lambda y: y[:, :].rearrange("p (c s) -> p c s", c=2)
                    batch = (a - PRO) // NRD + (0 if kind == "V1" else 1)
                    if small and kind in ("q", "k"):
                        wait(act, f_ready, i, lo, 3, 3 * batch + 1 + ("q", "k").index(kind))
                        src, dst = (qf, qs) if kind == "q" else (kf, ks)
                        wait(act, rd_ready, i, lo, NRD, a + pos + 1)
                        src4 = src[:, :, :].rearrange("p t (h o d) -> p (t h) o d", o=1, d=dh).broadcast_to([P, TB * H, 2, dh])
                        out = dst[:, :, 0:2, :] if kind == "q" else dst[:, :, 0:3:2, :]
                        act.activation(out, src4, ACT.Copy).then_inc(rd_hi, 1)
                        return
                    wait(act, rd_ready, i, lo, NRD, a + pos + 1)
                    if small and kind == "v":
                        wait(act, vh_done, i, lo, 2, 2 * batch)
                        act.activation(vf[:, :, :], both(bank), ACT.Copy).then_inc(rd_hi, 1)
                    elif kind == "nT":
                        if small:
                            act.activation(nT[0][:, :, :], both(bank), ACT.Copy).then_inc(rd_hi, 1)
                        else:
                            act.activation(nT[0][:, part, :], bank[:, 0:S], ACT.Copy).then_inc(rd_hi, 1)
                    elif small:
                        wait(act, s_ready, i, lo, H, H * batch - H + 4 * part + 4)
                        dst = QT if kind == "qT" else KT
                        act.activation(dst[:, 2 * part, :], bank[:, 0:S], ACT.Copy).then_inc(rd_hi, 1)
                    elif kind == "qT":
                        wait(act, s_ready, i, lo, H, H * batch - H + 4 * part + 4)
                        for e in range(2):
                            ins = act.activation(QT[0][64 * e:64 * e + 64, 4 * part + e:4 * part + 4:2, :], both(bank)[64 * e:64 * e + 64], ACT.Copy,
                                                 scale=-scale)
                        ins.then_inc(rd_hi, 1)
                    elif kind == "kT":
                        wait(act, s_ready, i, lo, H, H * batch - H + 4 * part + 4)
                        act.activation(KT[0][:, 2 * part:2 * part + 2, :], both(bank), ACT.Copy).then_inc(rd_hi, 1)
                    else:
                        half = 512 * (kind == "V1")
                        wait(act, pv_done, i, lo, H, H * batch - H + (16 if half else 8))
                        act.activation(V[0][:, part, half:half + 512], bank[:, :], ACT.Copy).then_inc(rd_hi, 1)

                def v_hi(i, lo, turn, half):
                    wait(act, f_ready, i, lo, 3, 3 * (turn + 1))
                    wait(act, pv_done, i, lo, H, H * turn - H + 8 * half + 8)
                    for kc in range(KC):
                        ins = act.activation(v_cols(kc, half, 0), vf_cols(kc, half), ACT.Copy)
                    ins.then_inc(v_half, 1)

                for pos, (_, kind, part) in enumerate(ROUNDS):
                    round_(0, 0, 0, pos, kind, part)
                if small:
                    v_hi(0, 0, 0, 0)
                for s in range(LEAD - 1):
                    weights_of(0, 0, s)

                def body(i, lo, hi):
                    last = hi == B - 1
                    for h in range(H):
                        if not (last and h + 2 >= H):
                            weights_of(i, lo, h + 2)
                        p_hi(i, lo, h)
                        if h == 0 and lo > 0:
                            o_hi(i, lo, -1, NGR - 1)
                        if h > 0 and h % GH == 0:
                            o_hi(i, lo, 0, h // GH - 1)
                        for pos, kind, part in rounds_at(h, last):
                            round_(i, lo, PRO, pos, kind, part)
                        if small and h == 1:
                            v_hi(i, lo, 0, 1)
                        if small and h == 9 and not last:
                            v_hi(i, lo, 1, 0)

                run_loop(act, B, CUTS, body)
                o_hi(B - 1, B - 1, 0, NGR - 1)

            @block.vector
            def _(v):
                def max_of(i, lo, s):
                    wait(v, e_done, i, lo, H, s - 1)
                    wait(v, s_ready, i, lo, H, s + 1)
                    if small:
                        v.tensor_copy(met[:, s % 4:s % 4 + 1], tg[:, 0:1])
                        for t in range(TB):
                            ins = v.tensor_tensor_reduce(out=s_m[s % 2][:, t, :], in0=s_ps[s % 2][:, t, :], in1=msk[:, t, :], scale=1.0,
                                                         scalar=BIG, op0=ALU.add, op1=ALU.min, accum_out=nm[:, s % 4, t:t + 1])
                    else:
                        ins = v.tensor_reduce(nm[:, s % 4, :], s_ps[s % 2][:, :, :], AX.X, ALU.min)
                    ins.then_inc(m_ready, 1)

                def inverse(i, lo, s):
                    wait(v, e_done, i, lo, H, s + 1)
                    v.reciprocal(ri[:, s % 4, :], rs[:, s % 4, :]).then_inc(r_done, 1)

                def p_lo(i, lo, s):
                    wait(v, ph_done, i, lo, H, s + 1)
                    v.tensor_tensor(pT[1][s % 2][:, :, :], t_ps[s % 2][:, :, :], pT[0][s % 2][:, :, :].bitcast(F32), ALU.subtract).then_inc(pl_done, 1)

                def o_lo(i, lo, turn, g):
                    wait(v, oh_done, i, lo, NGR, turn * NGR + g + 1)
                    if small:
                        ins = v.tensor_tensor(OT[1][:, g, :], o_ps[g % 2][:, 0:S], OT[0][:, g, :].bitcast(F32), ALU.subtract)
                    else:
                        for e in range(2):
                            r = slice(64 * e, 64 * e + 64)
                            ins = v.tensor_tensor(OT[1][r, g, :], o_ps[g % 2][r, e * S:(e + 1) * S], OT[0][r, g, :].bitcast(F32), ALU.subtract)
                    ins.then_inc(ol_done, 1)

                def x_of(i, b):
                    at = TB * (i + b)
                    return x[:, at:at + TB, :] if isinstance(i, int) else x[:, bass.ds(at, TB), :]

                def residual(i, lo, turn):
                    wait(v, out_ready, i, lo, 1, turn + 1)
                    out = o_ps[1][:, :].rearrange("p (t d) -> p t d", t=TB)
                    v.scalar_tensor_tensor(x_of(i, turn), out, tg[:, 0:1], x_of(i, turn), ALU.mult, ALU.add)
                    v.drain()
                    v.tensor_tensor(x_of(i, turn), x_of(i, turn), bc_t(bo[:, :], D), ALU.add).then_inc(x_done, 1)

                def norm(i, lo, turn):
                    if not (isinstance(i, int) and i + turn == 0):
                        wait(v, rd_ready, i, lo, NRD, PRO + (turn - 2) * NRD + done_by("nT", 0 if small else 1))
                    v.tensor_copy(met[:, 4:5], tg[:, 0:1])
                    norm_tiles(v, n_sb[:, :, :], x_of(i, turn), st, gb, inner)
                    if small:
                        b = i + turn
                        mrow = mi[:, b, :] if isinstance(b, int) else mi[:, bass.ds(b, 1), :].rearrange("p o s -> p (o s)")
                        fill = 1.0e9 if rotary else BIG
                        v.tensor_scalar(msk_next[:, 0, :], mrow, 0.0, fill, ALU.is_equal, ALU.mult)
                        v.drain()
                        v.tensor_copy(msk_next[:, 1, :], msk_next[:, 0, :])
                        v.drain()
                        if rotary:
                            v.tensor_tensor(msk_next[:, :, :], msk_next[:, :, :], causal[:, :, :], ALU.max)
                            v.drain()
                            v.tensor_reduce(kq[:, :], msk_next[:, :, :], AX.X, ALU.min)
                            v.drain()
                            v.tensor_scalar(kq[:, :], kq[:, :], 0.0, None, ALU.is_equal)
                            v.drain()
                    v.drain().then_inc(n_ready, 1)

                def rotate(f):
                    half = lambda y, e: y[:, :, :].rearrange("p t (h e d) -> p t h e d", e=2, d=8)[:, :, :, e, :]
                    tab = lambda j, n: cs[:, :, j, :].rearrange("p t (o d) -> p t o d", o=1).broadcast_to([P, TB, n, 8])
                    v.tensor_tensor(r1[:, :, :].rearrange("p t (h d) -> p t h d", d=8), f[:, :, :].rearrange("p t (h d) -> p t h d", d=8), tab(0, 32), ALU.mult)
                    v.tensor_tensor(half(r2, 0), half(f, 1), tab(1, 16), ALU.mult)
                    v.tensor_tensor(half(r2, 1), half(f, 0), tab(2, 16), ALU.mult)
                    v.drain()
                    v.tensor_tensor(f[:, :, :], r1[:, :, :], r2[:, :, :], ALU.add)

                def round_(i, lo, a, pos, kind, part):
                    bank = r_ps[pos % 2]
                    both = bank[:, :].rearrange("p (c s) -> p c s", c=2)
                    if small and kind == "v":
                        wait(v, rd_hi, i, lo, NRD, a + pos + 1)
                        v.tensor_tensor(vf[:, :, :], vf[:, :, :], bc_t(b3[:, 2, :], D), ALU.add)
                        v.drain().then_inc(f_ready, 1)
                        v.drain().then_inc(rd_done, 1)
                        return
                    if small and kind in ("q", "k"):
                        wait(v, rd_ready, i, lo, NRD, a + pos + 1)
                        f = {"q": qf, "k": kf}[kind]
                        j = ("q", "k").index(kind)
                        v.scalar_tensor_tensor(f[:, :, :], both, -scale if kind == "q" else 1.0, bc_t(b3[:, j, :], D), ALU.mult, ALU.add)
                        v.drain()
                        if rotary:
                            rotate(f)
                            v.drain()
                            if kind == "q":
                                for t in range(TB):
                                    v.tensor_scalar(f[:, t, :], f[:, t, :], kq[:, t:t + 1], None, ALU.mult)
                                v.drain()
                        v.drain().then_inc(f_ready, 1)
                        wait(v, rd_hi, i, lo, NRD, a + pos + 1)
                        dst = qs if kind == "q" else ks
                        src4 = f[:, :, :].rearrange("p t (h o d) -> p (t h) o d", o=1, d=dh).broadcast_to([P, TB * H, 2, dh])
                        hi_, lo_ = (dst[:, :, 0:2, :], dst[:, :, 2:4, :]) if kind == "q" else (dst[:, :, 0:3:2, :], dst[:, :, 1:4:2, :])
                        v.tensor_tensor(lo_, src4, hi_.bitcast(F32), ALU.subtract).then_inc(rd_done, 1)
                        return
                    wait(v, rd_hi, i, lo, NRD, a + pos + 1)
                    if kind == "nT":
                        if small:
                            v.tensor_tensor(nT[1][:, :, :], both, nT[0][:, :, :].bitcast(F32), ALU.subtract).then_inc(rd_done, 1)
                        else:
                            v.tensor_tensor(nT[1][:, part, :], bank[:, 0:S], nT[0][:, part, :].bitcast(F32), ALU.subtract).then_inc(rd_done, 1)
                    elif small:
                        dst = QT if kind == "qT" else KT
                        v.tensor_copy(dst[:, 2 * part + 1, :], bank[:, S:2 * S]).then_inc(rd_done, 1)
                    elif kind == "qT":
                        for e in range(2):
                            r = slice(64 * e, 64 * e + 64)
                            heads = slice(4 * part + e, 4 * part + 4, 2)
                            ins = v.scalar_tensor_tensor(QT[1][r, heads, :], both[r], -scale, QT[0][r, heads, :].bitcast(F32), ALU.mult, ALU.subtract)
                        ins.then_inc(rd_done, 1)
                    elif kind == "kT":
                        v.tensor_tensor(KT[1][:, 2 * part:2 * part + 2, :], both, KT[0][:, 2 * part:2 * part + 2, :].bitcast(F32), ALU.subtract).then_inc(rd_done, 1)
                    else:
                        half = 512 * (kind == "V1")
                        v.tensor_tensor(V[1][:, part, half:half + 512], bank[:, :], V[0][:, part, half:half + 512].bitcast(F32), ALU.subtract).then_inc(rd_done, 1)

                def v_lo(i, lo, turn, half):
                    wait(v, v_half, i, lo, 2, 2 * turn + half + 1)
                    for kc in range(KC):
                        ins = v.tensor_tensor(v_cols(kc, half, 1), vf_cols(kc, half), v_cols(kc, half, 0).bitcast(F32), ALU.subtract)
                    ins.then_inc(vh_done, 1)

                def take_mask():
                    v.drain()
                    v.tensor_copy(msk[:, :, :], msk_next[:, :, :])
                    v.drain()

                norm(0, 0, 0)
                if small:
                    take_mask()
                for pos, (_, kind, part) in enumerate(ROUNDS):
                    round_(0, 0, 0, pos, kind, part)
                if small:
                    v_lo(0, 0, 0, 0)
                for s in range(LEAD):
                    max_of(0, 0, s)
                for s in range(LEAD - 1):
                    inverse(0, 0, s)

                def body(i, lo, hi):
                    last = hi == B - 1
                    for h in range(H):
                        if small and h + LEAD == H and not last:
                            take_mask()
                        if not (last and h + LEAD >= H):
                            max_of(i, lo, h + LEAD)
                        p_lo(i, lo, h)
                        if h == 0 and lo > 0:
                            o_lo(i, lo, -1, NGR - 1)
                        if h > 0 and h % GH == 0:
                            o_lo(i, lo, 0, h // GH - 1)
                        if not (last and h + 2 >= H):
                            inverse(i, lo, h + 2)
                        if h == 0 and not last:
                            norm(i, lo, 1)
                        for pos, kind, part in rounds_at(h, last):
                            round_(i, lo, PRO, pos, kind, part)
                        if small and h == 1:
                            v_lo(i, lo, 0, 1)
                        if small and h == 9 and not last:
                            v_lo(i, lo, 1, 0)
                        if h == 3 and lo > 0:
                            residual(i, lo, -1)

                run_loop(v, B, CUTS, body)
                o_lo(B - 1, B - 1, 0, NGR - 1)
                residual(B - 1, B - 1, 0)

            @block.gpsimd
            def _(pool):
                def normalize(i, lo, s):
                    wait(pool, r_done, i, lo, H, s + 1)
                    pool.tensor_tensor(p_sb[s % 4][:, :, :], p_sb[s % 4][:, :, :],
                                       ri[:, s % 4, :].rearrange("p (t o) -> p t o", o=1).broadcast_to([P, TB, S]), ALU.mult).then_inc(n_done, 1)

                for s in range(LEAD - 1):
                    normalize(0, 0, s)

                def body(i, lo, hi):
                    for h in range(H):
                        if not (hi == B - 1 and h + 2 >= H):
                            normalize(i, lo, h + 2)

                run_loop(pool, B, CUTS, body)


def attention_layer(nc, G, I, layer):
    if layer == 0:
        single_phase(nc, G, I, "att0", {n: I["L0_xattn_" + n] for n in ("Wq", "Wk", "Wv", "Wcq", "Wck", "Wcv", "W1")},
                     (I["L0_xattn_gamma"], I["L0_xattn_beta"], I["L0_xattn_b1"]))
    if layer == 1:
        heads_phase(nc, G, I, "att1", 1, 16, {"q": I["L1_Wq"], "k": I["L1_Wk"], "v": I["L1_Wv"], "o": I["L1_Wo"], "bo": I["L1_xattn_bo"]},
                    mask=I["mask_BxS2_if1"], rotary=True, biases=(I["L1_bq"], I["L1_bk"], I["L1_bv"]))
    if layer == 2:
        heads_phase(nc, G, I, "att2", 2, 16, {"q": I["L2_xattn_Wq"], "k": I["L2_xattn_Wk"], "v": I["L2_xattn_Wv"], "o": I["L2_Wo"],
                                              "bo": I["L2_xattn_bo"]},
                    mask=I["mask2"], biases=(I["L2_xattn_bq"], I["L2_xattn_bk"], I["L2_xattn_bv"]))
    if layer == 3:
        heads_phase(nc, G, I, "att3", 3, 64, {"q": I["L3_xattn_w_q"], "k": I["L3_w_k"], "v": I["L3_w_v"], "o": I["L3_xattn_w_out"],
                                              "bo": I["L3_xattn_b_out"]},
                    inner=(I["L3_xattn_ln_gamma"], I["L3_xattn_ln_beta"]), gate=I["L3_xattn_gate"])


def single_phase(nc, G, I, name, weights, rows):
    NU, NT = 2, 4
    NI = T // (NU * NT)
    C = NT * P
    scale = -1.0 / 16.0
    W = {"Wq": 0, "Wk": 1, "Wv": 2, "Wcq": 3, "Wck": 4, "Wcv": 5, "W1": 6}
    PRODUCTS = ["nT", "QT", "KT", "V", "S", "cKT", "pT", "A", "cV", "hT", "cQT", "cS", "cpT", "cA", "h2T", "F"]
    NP = len(PRODUCTS)
    at = PRODUCTS.index
    SPLIT = [p for p in PRODUCTS if p not in ("S", "A", "cS", "cA", "F")]
    ROWS = {"nT": 1, "hT": 2, "h2T": 3}

    with ExitStack() as ctx:
        A = Alloc(nc, ctx, name)
        sb, sem = A.sb, A.sem
        hl = lambda n, shape: [sb(f"{n}_{h}", shape, F32R) for h in ("hi", "lo")]
        x, ident, tg = G["x"], G["ident"], G["tanh_g"][:, 0:1]
        w_all = hl("w", [P, len(W), KC, D])
        jobs = []
        for wn, q in W.items():
            for k in range(KC):
                jobs.append((weights[wn][k * P:(k + 1) * P, :], w_all[0][:, q, k, :], w_all[1][:, q, k, :]))
        load_split(nc, name + "w", jobs, D)

        U = range(NU)
        per = lambda n, shape: [sb(f"{n}{u}", shape) for u in U]
        hl_u = lambda n: [hl(f"{n}{u}", [P, 2, 512]) for u in U]
        n_sb, p_sb, a_sb, h_sb, s_m = (per(n, [P, NT, D]) for n in ("n", "p", "a", "h", "s_m"))
        xT, QT, KT, V, pT, cT = (hl_u(n) for n in ("xT", "QT", "KT", "V", "pT", "cT"))
        nm, rs, ri = (per(n, [P, NT]) for n in ("nm", "rs", "ri"))
        st = [{"bn": sb(f"bn{u}", [P, 4, 6]), "mv": sb(f"mv{u}", [P, 4, 2]), "rstd": sb(f"rstd{u}", [P, 4]), "tmp": sb(f"tmp{u}", [P, 4])} for u in U]
        gamma, beta, b1 = (sb(n, [P, D]) for n in ("gamma", "beta", "b1"))
        causal = sb("causal", [P, TB, S])
        met = sb("met", [P, NU])
        ps = [[A.ps(f"ps{u}{q}", [P, 2, 512]) for q in range(2)] for u in U]
        per_sem = lambda n: [sem(f"{n}{u}") for u in U]
        product, hi_done, used, rows_ready, m_ready, e_ready, c_in, gated, unit_free = (
            per_sem(n) for n in ("product", "hi_done", "used", "rows_ready", "m_ready", "e_ready", "c_in", "gated", "unit_free"))
        loaded = sem("loaded")

        rows4 = lambda y: y.rearrange("p a (b n) -> p (a b) n", n=D)
        dest = {"nT": xT, "hT": xT, "h2T": xT, "QT": QT, "cQT": QT, "KT": KT, "cKT": KT, "V": V, "cV": V, "pT": pT, "cpT": pT}

        def bank(u, name):
            return ps[u][at(name) % 2]

        def x_of(i, u):
            return x[:, bass.ds(i * (NU * NT) + u * NT, NT), :]

        with nc.Block() as block:
            @block.sync
            def _(sp):
                for dst, src in zip((gamma, beta, b1), rows):
                    sp.dma_start(dst[:, :], src.rearrange("(a d) -> a d", a=1).broadcast_to([P, D])).then_inc(loaded, 16)
                sp.dma_start(causal[:, :, :], I["causal"]).then_inc(loaded, 16)
                sp.wait_ge(loaded, 64)

            @block.gpsimd
            def _(pool):
                for u in U:
                    pool.nop().then_inc(unit_free[u], 1)

        with nc.Block() as block:
            @block.sync
            def _(sp):
                with sp.Fori(0, NI) as i:
                    for u in U:
                        srcs = [[G["ctxT"][h][bass.ds(sp.snap(i * (2 * NU) + 2 * u + b), 1)].rearrange("o p k s -> (o p) k s") for b in range(2)]
                                for h in range(2)]
                        sp.wait_ge(unit_free[u], i + 1)
                        for b in range(2):
                            for h in range(2):
                                sp.dma_start(cT[u][h][:, :, b * S:(b + 1) * S].bitcast(F32), srcs[h][b]).then_inc(c_in[u], 16)

            @block.tensor
            def _(pe):
                def turn_rows(i, u, name, rows):
                    for k in range(2):
                        for t in range(NT):
                            mm = pe.transpose(bank(u, name)[:, k, t * P:(t + 1) * P], rows[u][:, t, k * P:(k + 1) * P], ident[:, :])
                    return mm

                def features(i, u, name, src, w):
                    for c in range(2):
                        for k in range(KC):
                            mm = mm3(pe, bank(u, name)[:, c, :], [y[:, W[w], k, c * P:(c + 1) * P] for y in w_all],
                                     [y[:, k, :] for y in src[u]], k == 0, k == KC - 1)
                    return mm

                def tokens(i, u, name, src, moving):
                    out = rows4(bank(u, name)[:, :, :])
                    for t in range(NT):
                        for k in range(KC):
                            mm = mm3(pe, out[:, t, :], [y[:, k, t * P:(t + 1) * P] for y in src[u]], moving(u, t, k), k == 0, k == KC - 1)
                    return mm

                weight = lambda w: (lambda u, t, k: [y[:, W[w], k, :] for y in w_all])
                keys = lambda u, t, k: [y[:, k, (t // TB) * S:(t // TB + 1) * S] for y in KT[u]]
                vals = lambda u, t, k: [rows4(y[:, :, :])[:, (t // TB) * TB + k, :] for y in V[u]]

                with pe.Fori(0, NI) as i:
                    def before(u, name, operand):
                        need = max(at(operand) + 1 if operand else 0, at(name) - 1)
                        if need > 0:
                            pe.wait_ge(used[u], i * NP + need)

                    for name in PRODUCTS:
                        for u in U:
                            if name == "nT":
                                before(u, name, None)
                                pe.wait_ge(rows_ready[u], i * 3 + 1)
                                mm = turn_rows(i, u, name, n_sb)
                            elif name in ("hT", "h2T"):
                                before(u, name, None)
                                pe.wait_ge(rows_ready[u], i * 3 + ROWS[name])
                                mm = turn_rows(i, u, name, h_sb if name == "hT" else n_sb)
                            elif name in ("pT", "cpT"):
                                before(u, name, None)
                                pe.wait_ge(e_ready[u], i * 2 + (1 if name == "pT" else 2))
                                mm = turn_rows(i, u, name, p_sb)
                            elif name in ("QT", "KT"):
                                before(u, name, "nT")
                                mm = features(i, u, name, xT, {"QT": "Wq", "KT": "Wk"}[name])
                            elif name == "V":
                                before(u, name, "nT")
                                mm = tokens(i, u, name, xT, weight("Wv"))
                            elif name in ("S", "cS"):
                                before(u, name, "KT" if name == "S" else "cQT")
                                mm = tokens(i, u, name, QT, keys)
                            elif name == "cKT":
                                before(u, name, None)
                                pe.wait_ge(c_in[u], i * 64 + 64)
                                mm = features(i, u, name, cT, "Wck")
                            elif name in ("A", "cA"):
                                before(u, name, "pT" if name == "A" else "cpT")
                                mm = tokens(i, u, name, pT, vals)
                            elif name == "cV":
                                before(u, name, None)
                                mm = tokens(i, u, name, cT, weight("Wcv"))
                            elif name == "cQT":
                                before(u, name, "hT")
                                mm = features(i, u, name, xT, "Wcq")
                            else:
                                before(u, name, "h2T")
                                mm = tokens(i, u, name, xT, weight("W1"))
                            mm.then_inc(product[u], 1)

            @block.scalar
            def _(act):
                with act.Fori(0, NI) as i:
                    for name in PRODUCTS:
                        for u in U:
                            if name in SPLIT:
                                act.wait_ge(product[u], i * NP + at(name) + 1)
                                act.activation(dest[name][u][0][:, :, :], bank(u, name)[:, :, :], ACT.Copy,
                                               scale=scale if name in ("QT", "cQT") else 1.0).then_inc(hi_done[u], 1)
                            elif name in ("S", "cS"):
                                act.wait_ge(m_ready[u], i * 2 + (1 if name == "S" else 2))
                                src = s_m[u] if name == "S" else rows4(bank(u, name)[:, :, :])
                                for t in range(NT):
                                    ins = act.activation(p_sb[u][:, t, :], src[:, t, :], ACT.Exp, bias=nm[u][:, t:t + 1], scale=-1.0,
                                                         accum_out=rs[u][:, t:t + 1])
                                ins.then_inc(e_ready[u], 1)

            @block.vector
            def _(v):
                def norm(u, dst, src):
                    s = st[u]
                    for t in range(NT):
                        v.bn_stats(s["bn"][:, t, :], src[:, t, :])
                    v.drain()
                    for t in range(NT):
                        v.bn_aggr(s["mv"][:, t, :], s["bn"][:, t, :])
                    v.drain()
                    rsqrt(v, s["rstd"][:, :], s["mv"][:, :, 1], s["tmp"][:, :], 1e-3)
                    for t in range(NT):
                        v.scalar_tensor_tensor(src[:, t, :], src[:, t, :], s["mv"][:, t, 0:1], gamma[:, :], ALU.subtract, ALU.mult)
                    v.drain()
                    for t in range(NT):
                        ins = v.scalar_tensor_tensor(dst[:, t, :], src[:, t, :], s["rstd"][:, t:t + 1], beta[:, :], ALU.mult, ALU.add)
                    return ins

                with v.Fori(0, NI) as i:
                    split = [p for p in SPLIT]
                    for u in U:
                        v.wait_ge(unit_free[u], i + 1)
                        v.tensor_copy(met[:, u:u + 1], tg)
                        layer_norm(v, n_sb[u][:, :, :], x_of(i, u), st[u], NT, 1e-5)
                        v.drain().then_inc(rows_ready[u], 1)
                    for name in PRODUCTS:
                        for u in U:
                            src = bank(u, name)
                            tiles = rows4(src[:, :, :])
                            if name in SPLIT:
                                v.wait_ge(hi_done[u], i * len(SPLIT) + split.index(name) + 1)
                                hi_, lo_ = (y[:, :, :] for y in dest[name][u])
                                if name in ("QT", "cQT"):
                                    ins = v.scalar_tensor_tensor(lo_, src[:, :, :], scale, hi_.bitcast(F32), ALU.mult, ALU.subtract)
                                else:
                                    ins = v.tensor_tensor(lo_, src[:, :, :], hi_.bitcast(F32), ALU.subtract)
                                ins.then_inc(used[u], 1)
                                continue
                            v.wait_ge(product[u], i * NP + at(name) + 1)
                            if name == "S":
                                v.tensor_copy(met[:, u:u + 1], tg)
                                for t in range(NT):
                                    ins = v.tensor_tensor_reduce(out=s_m[u][:, t, :], in0=tiles[:, t, :], in1=causal[:, t % TB, :], scale=1.0,
                                                                 scalar=BIG, op0=ALU.add, op1=ALU.min, accum_out=nm[u][:, t:t + 1])
                                ins.then_inc(m_ready[u], 1)
                                v.wait_ge(e_ready[u], i * 2 + 1)
                                v.reciprocal(ri[u][:, :], rs[u][:, :]).then_inc(used[u], 1)
                            elif name == "cS":
                                v.tensor_reduce(nm[u][:, :], tiles, AX.X, ALU.min).then_inc(m_ready[u], 1)
                                v.wait_ge(e_ready[u], i * 2 + 2)
                                v.reciprocal(ri[u][:, :], rs[u][:, :]).then_inc(used[u], 1)
                            elif name in ("A", "cA"):
                                base, out = (n_sb, h_sb) if name == "A" else (h_sb, n_sb)
                                for t in range(NT):
                                    ins = v.scalar_tensor_tensor(a_sb[u][:, t, :], tiles[:, t, :], ri[u][:, t:t + 1], base[u][:, t, :], ALU.mult, ALU.add)
                                ins.then_inc(used[u], 1)
                                v.drain()
                                norm(u, out[u], a_sb[u]).then_inc(rows_ready[u], 1)
                            else:
                                v.tensor_tensor(a_sb[u][:, :, :], tiles, b1[:, :].rearrange("p (o d) -> p o d", o=1).broadcast_to([P, NT, D]),
                                                ALU.add).then_inc(used[u], 1)
                                v.drain()
                                v.scalar_tensor_tensor(a_sb[u][:, :, :], a_sb[u][:, :, :], 0.0, n_sb[u][:, :, :], ALU.max, ALU.add)
                                v.drain()
                                norm(u, a_sb[u], a_sb[u])
                                v.drain()
                                v.tensor_scalar(a_sb[u][:, :, :], a_sb[u][:, :, :], 0.0, tg, ALU.max, ALU.mult).then_inc(gated[u], 1)

            @block.gpsimd
            def _(pool):
                with pool.Fori(0, NI) as i:
                    for u in U:
                        pool.wait_ge(gated[u], i + 1)
                        pool.tensor_tensor(x_of(i, u), x_of(i, u), a_sb[u][:, :, :], ALU.add).then_inc(unit_free[u], 1)



def build_program(nc, I, out):
    with ExitStack() as ctx:
        G = globals_of(nc, Alloc(nc, ctx, "g"))
        setup_phase(nc, G, I)
        for layer in range(4):
            attention_layer(nc, G, I, layer)
            moe_layer(nc, G, I, layer)
        final_phase(nc, G, out)


def kernel(**inputs):
    import concourse.bacc as bacc
    from concourse.bass_utils import run_bass_kernel_spmd

    nc = bacc.Bacc("TRN2", target_bir_lowering=False, num_devices=1)
    arrays = {f"in_{name}": np.ascontiguousarray(a) for name, a in lay_out(inputs).items()}
    I = {name[3:]: nc.dram_tensor(name, a.shape, mybir.dt.from_np(a.dtype), kind="ExternalInput").ap()
         for name, a in arrays.items()}
    out = nc.dram_tensor("out", (B, S, D), F32, kind="ExternalOutput").ap()
    build_program(nc, I, out)
    r = run_bass_kernel_spmd(nc, [arrays], core_ids=[0])
    return r.results[0]["out"]
```

```python
from contextlib import ExitStack

import numpy as np

import concourse.bass as bass
from concourse import mybir
from concourse.alu_op_type import AluOpType as ALU

F32 = mybir.dt.float32
F32R = mybir.dt.float32r
BF16 = mybir.dt.bfloat16
I32 = mybir.dt.int32
ACT = mybir.ActivationFunctionType
AX = mybir.AxisListType

P = 128
B = 8
S = 256
D = 256
N = B * S
T = N // P
KC = D // P
TB = S // P
BS = 256
BT = BS // P
XROWS = N + 38 * BS
BIG = 3.0e38


def wait(e, sem, i, lo, a, b):
    if isinstance(i, int):
        if i * a + b > 0:
            e.wait_ge(sem, i * a + b)
    else:
        assert lo * a + b > 0, (lo, a, b)
        e.wait_ge(sem, i * a + b)


def run_loop(e, n, cuts, body, start=0):
    edges = sorted({start, n, *[c for c in cuts if start < c < n]})
    for lo, end in zip(edges, edges[1:]):
        if end - lo == 1:
            body(lo, lo, lo)
        else:
            with e.Fori(lo, end) as i:
                body(i, lo, end - 1)


def rsqrt(v, y, var, tmp, eps):
    v.tensor_scalar(var, var, eps, None, ALU.add)
    v.drain()
    v.tensor_scalar(y.bitcast(I32), var.bitcast(I32), -0.5, float(0x5F3759DF), ALU.mult, ALU.add)
    v.drain()
    for _ in range(3):
        v.scalar_tensor_tensor(tmp, y, -0.5, y, ALU.mult, ALU.mult)
        v.drain()
        v.tensor_tensor(tmp, tmp, var, ALU.mult)
        v.drain()
        v.scalar_tensor_tensor(y, tmp, 1.5, y, ALU.add, ALU.mult)
        v.drain()


def layer_norm(v, dst, src, st, n, eps):
    for t in range(n):
        v.bn_stats(st["bn"][:, t, :], src[:, t, :])
    v.drain()
    for t in range(n):
        v.bn_aggr(st["mv"][:, t, :], st["bn"][:, t, :])
    v.drain()
    rsqrt(v, st["rstd"][:, 0:n], st["mv"][:, 0:n, 1], st["tmp"][:, 0:n], eps)
    for t in range(n):
        v.tensor_scalar(dst[:, t, :], src[:, t, :], st["mv"][:, t, 0:1], st["rstd"][:, t:t + 1],
                        ALU.subtract, ALU.mult)
    v.drain()


def mm3(pe, out, lhs, rhs, first, last, **kw):
    pe.matmul(out, lhs[0], rhs[0], start=first, stop=False, **kw)
    pe.matmul(out, lhs[0], rhs[1], start=False, stop=False, **kw)
    return pe.matmul(out, lhs[1], rhs[0], start=False, stop=last, **kw)


class Alloc:

    def __init__(self, nc, ctx, name):
        self.nc, self.ctx, self.name, self.sems = nc, ctx, name, []
        ctx.callback(self.close)

    def close(self):
        if self.sems:
            self.nc.clear_and_free_semaphores(self.sems)
            self.nc.all_engine_barrier()

    def sb(self, name, shape, dt=F32):
        return self.ctx.enter_context(self.nc.sbuf_tensor(f"{self.name}_{name}", shape, dt))

    def ps(self, name, shape, dt=F32):
        return self.ctx.enter_context(self.nc.psum_tensor(f"{self.name}_{name}", shape, dt))

    def sem(self, name):
        self.sems.append(self.nc.alloc_semaphore(f"{self.name}_{name}"))
        return self.sems[-1]



def moe_phase(nc, G, name, layer, E, K, FC, glu, func, shared, w_dram, rw_dram, rb_dram=None,
              biases=False, renorm=False, eps_sum=0.0, cap=None, clip=None, inner_norm=None, add_input=False):
    NB = (N * K + E * (BS - 1)) // BS
    SJ = N // BS if shared else 0
    NJ = (SJ + NB + 1) // 2 * 2
    NR = NJ - SJ
    NI = NJ // 2
    BASE = N if shared else 0
    ROWS = BASE + NR * BS
    W1 = (2 if glu else 1) * P
    WW = KC * W1 + D
    CW = WW + (1 + P if biases else 0)
    CI = 2 * FC
    NS = max(FC, 4)
    LA = 2 if biases else 3
    per_slot = CI // NS
    assert CI % NS == 0 and ROWS <= XROWS
    rows_x, rows_y = G["rows_x"], G["rows_y"]
    x, ident = G["x"], G["ident"]
    tg = G["tanh_g"][:, 4 + layer:5 + layer]

    with ExitStack() as ctx:
        A = Alloc(nc, ctx, name)
        sb, ps, sem = A.sb, A.ps, A.sem
        n_all = sb("n_all", [P, T, D])
        p_k = [sb(f"p_{k}", [P, T]) for k in range(K)]
        slot_w = sb("slot_w", [P, T, K], I32)
        slot_r = sb("slot_r", [P, T, K], I32)
        blk = sb("blk", [P, NR], I32)

        with ExitStack() as c2:
            R = Alloc(nc, c2, name + "r")
            nT = R.sb("nT", [P, 2, KC, 512])
            bn, mv = R.sb("bn", [P, T, 6]), R.sb("mv", [P, T, 2])
            rstd, nb, tmp = (R.sb(n, [P, T]) for n in ("rstd", "nb", "tmp"))
            rw = R.sb("rw", [P, KC, E])
            lgT = R.sb("lgT", [P, 2, 512])
            lg, ex = R.sb("lg", [P, T, E]), R.sb("ex", [P, T, E])
            t1, t2 = R.sb("t1", [P, T, E]), R.sb("t2", [P, T, E])
            oh = [R.sb(f"oh{k}", [P, T, E]) for k in range(K)]
            m, r = R.sb("m", [P, T]), R.sb("r", [P, T])
            Mb = R.sb("Mb", [P, T, E], BF16)
            cnt, cnti = R.sb("cnt", [P, E]), R.sb("cnti", [P, E], I32)
            offs, ends = R.sb("offs", [P, E]), R.sb("ends", [P, E])
            tE = R.sb("tE", [P, E, E])
            tB, nblk = R.sb("tB", [P, NR, E]), R.sb("nblk", [P, NR])
            keep = R.sb("keep", [P, T])
            gb = None
            if inner_norm:
                gb = R.sb("gb", [P, 2, D])
            rb = R.sb("rb", [P, E]) if rb_dram is not None else None
            trp = [[R.ps(f"trp{q}{k}", [P, 512]) for k in range(KC)] for q in range(2)]
            lgp = [R.ps(f"lgp{q}", [P, 512]) for q in range(2)]
            small = R.ps("small", [P, 512])
            ltp, rank = (small[:, a:a + T * E].rearrange("p (t e) -> p t e", e=E) for a in (0, T * E))
            cntp = small[:, 2 * T * E:2 * T * E + E]
            loaded, stats, stats2, normed, scaled, n_ready, tr_ready, nT_ready = (R.sem(s) for s in (
                "loaded", "stats", "stats2", "normed", "scaled", "n_ready", "tr_ready", "nT_ready"))
            lg_ready, lgT_ready, lt_ready = (R.sem(s) for s in ("lg_ready", "lgT_ready", "lt_ready"))
            shifted, exped, mask_ready, rank_ready, rows_out = (R.sem(s) for s in ("shifted", "exped", "mask_ready", "rank_ready", "rows_out"))
            n_loads = 1 + 2 * bool(inner_norm) + (rb is not None)
            QT = T // 4

            with nc.Block() as block:
                @block.sync
                def _(sp):
                    sp.dma_start(rw[:, :, :], rw_dram).then_inc(loaded, 16)
                    if inner_norm:
                        for q in range(2):
                            sp.dma_start(gb[:, q, :], inner_norm[q].rearrange("(a d) -> a d", a=1).broadcast_to([P, D])).then_inc(loaded, 16)
                    if rb is not None:
                        sp.dma_start(rb[:, :], rb_dram.rearrange("(a d) -> a d", a=1).broadcast_to([P, E])).then_inc(loaded, 16)
                    for q in range(QT if shared else 0):
                        sp.wait_ge(n_ready, q + 1)
                        sp.dma_start(rows_x[512 * q:512 * (q + 1), :].rearrange("(t p) d -> p t d", p=P),
                                     n_all[:, 4 * q:4 * q + 4, :]).then_inc(rows_out, 16)
                    if shared:
                        sp.wait_ge(rows_out, 16 * QT)

                @block.scalar
                def _(act):
                    def apply(g, src, sem, done):
                        act.wait_ge(sem, g + 1)
                        for t in range(8 * g, 8 * g + 8):
                            ins = act.activation(n_all[:, t, :], src[:, t, :], ACT.Identity, scale=rstd[:, t:t + 1], bias=nb[:, t:t + 1])
                            if t % 4 == 3:
                                ins.then_inc(done, 1)

                    for g in range(2):
                        if inner_norm:
                            if g == 0:
                                apply(0, x, stats, normed)
                                apply(1, x, stats, normed)
                            apply(g, n_all, stats2, normed)
                        else:
                            apply(g, x, stats, n_ready)
                        for q in (2 * g, 2 * g + 1):
                            act.wait_ge(tr_ready, q + 1)
                            if q >= 2:
                                act.wait_ge(lg_ready, q - 1)
                            for k in range(KC):
                                ins = act.activation(nT[:, q % 2, k, :], trp[q % 2][k][:, :], ACT.Copy)
                            ins.then_inc(nT_ready, 1)
                        for q in (2 * g, 2 * g + 1):
                            act.wait_ge(lg_ready, q + 1)
                            if q >= 2:
                                act.wait_ge(lt_ready, q - 1)
                            act.activation(lgT[0:E, q % 2, :], lgp[q % 2][0:E, :], ACT.Copy).then_inc(lgT_ready, 1)
                    act.wait_ge(shifted, 1)
                    act.activation(ex[:, :, :], t1[:, :, :], ACT.Exp).then_inc(exped, 1)

                if inner_norm:
                    @block.gpsimd
                    def _(pool):
                        pool.wait_ge(loaded, 16 * n_loads)
                        for q in range(QT):
                            pool.wait_ge(scaled, q + 1)
                            blk4 = n_all[:, 4 * q:4 * q + 4, :]
                            pool.tensor_tensor(blk4, blk4, gb[:, 1, :].rearrange("p (o d) -> p o d", o=1).broadcast_to([P, 4, D]),
                                               ALU.add).then_inc(n_ready, 1)

                @block.tensor
                def _(pe):
                    def turn_rows(q):
                        pe.wait_ge(n_ready, q + 1)
                        if q >= 2:
                            pe.wait_ge(nT_ready, q - 1)
                        for k in range(KC):
                            for t in range(4):
                                mm = pe.transpose(trp[q % 2][k][:, t * P:(t + 1) * P],
                                                  n_all[:, 4 * q + t, k * P:(k + 1) * P], ident[:, :])
                        mm.then_inc(tr_ready, 1)

                    def logits(q):
                        if q == 0:
                            pe.wait_ge(loaded, 16 * n_loads)
                        if q >= 2:
                            pe.wait_ge(lgT_ready, q - 1)
                        pe.wait_ge(nT_ready, q + 1)
                        for k in range(KC):
                            mm = pe.matmul(lgp[q % 2][0:E, :], rw[:, k, :], nT[:, q % 2, k, :], start=(k == 0), stop=(k == KC - 1))
                        mm.then_inc(lg_ready, 1)

                    def turn_logits(q):
                        pe.wait_ge(lgT_ready, q + 1)
                        for t in range(4):
                            mm = pe.transpose(ltp[:, 4 * q + t, :], lgT[0:E, q % 2, t * P:(t + 1) * P], ident[0:E, 0:E])
                        mm.then_inc(lt_ready, 1)

                    for g in range(2):
                        turn_rows(2 * g)
                        turn_rows(2 * g + 1)
                        logits(2 * g)
                        logits(2 * g + 1)
                        turn_logits(2 * g)
                        turn_logits(2 * g + 1)
                    pe.wait_ge(mask_ready, 1)
                    for s in range(T - 1, 0, -1):
                        pe.matmul(rank[:, s:T, :], G["ones_bf"][:, :], Mb[:, 0:T - s, :], start=(s == T - 1), stop=False,
                                  skip_group_check=True)
                    pe.matmul(rank[:, :, :], G["before_bf"][:, :], Mb[:, :, :], start=False, stop=True, skip_group_check=True)
                    for t in range(T):
                        mm = pe.matmul(cntp, G["ones_bf"][:, :], Mb[:, t, :], start=(t == 0), stop=(t == T - 1), skip_group_check=True)
                    mm.then_inc(rank_ready, 1)

                @block.vector
                def _(v):
                    def bc_e(a):
                        return a[:, :].rearrange("p (t o) -> p t o", o=1).broadcast_to([P, T, E])

                    def stats_of(g, src, done):
                        r8 = slice(8 * g, 8 * g + 8)
                        for t in range(8 * g, 8 * g + 8):
                            v.bn_stats(bn[:, t, :], src[:, t, :])
                        v.drain()
                        for t in range(8 * g, 8 * g + 8):
                            v.bn_aggr(mv[:, t, :], bn[:, t, :])
                        v.drain()
                        rsqrt(v, rstd[:, r8], mv[:, r8, 1], tmp[:, r8], 1e-5)
                        v.scalar_tensor_tensor(nb[:, r8], mv[:, r8, 0], -1.0, rstd[:, r8], ALU.mult, ALU.mult).then_inc(done, 1)

                    stats_of(0, x, stats)
                    stats_of(1, x, stats)
                    if inner_norm:
                        v.wait_ge(loaded, 16 * n_loads)
                        for g in range(2):
                            v.wait_ge(normed, 2 * g + 2)
                            stats_of(g, n_all, stats2)
                        for q in range(QT):
                            v.wait_ge(normed, 4 + q + 1)
                            blk4 = n_all[:, 4 * q:4 * q + 4, :]
                            v.tensor_tensor(blk4, blk4, gb[:, 0, :].rearrange("p (o d) -> p o d", o=1).broadcast_to([P, 4, D]),
                                            ALU.mult).then_inc(scaled, 1)
                    v.wait_ge(loaded, 16 * n_loads)
                    v.wait_ge(lt_ready, QT)
                    if rb is not None:
                        v.tensor_tensor(lg[:, :, :], ltp[:, :, :], rb[:, :].rearrange("p (o e) -> p o e", o=1).broadcast_to([P, T, E]), ALU.add)
                    elif clip:
                        v.tensor_scalar(lg[:, :, :], ltp[:, :, :], clip, -clip, ALU.min, ALU.max)
                    else:
                        v.tensor_copy(lg[:, :, :], ltp[:, :, :])
                    v.drain()
                    v.tensor_reduce(m[:, :], lg[:, :, :], AX.X, ALU.max)
                    v.drain()
                    v.tensor_tensor(t1[:, :, :], lg[:, :, :], bc_e(m), ALU.subtract).then_inc(shifted, 1)
                    v.wait_ge(exped, 1)
                    v.tensor_reduce(r[:, :], ex[:, :, :], AX.X, ALU.add)
                    v.drain()
                    if eps_sum and not renorm:
                        v.tensor_scalar(r[:, :], r[:, :], eps_sum, None, ALU.add)
                        v.drain()
                    v.reciprocal(r[:, :], r[:, :])
                    v.drain()
                    v.tensor_tensor(ex[:, :, :], ex[:, :, :], bc_e(r), ALU.mult)
                    v.drain()
                    iota = G["iota_e"][:, 0:E].rearrange("p (o e) -> p o e", o=1).broadcast_to([P, T, E])
                    for k in range(K):
                        v.tensor_reduce(p_k[k][:, :], ex[:, :, :], AX.X, ALU.max)
                        v.drain()
                        v.tensor_tensor(t1[:, :, :], ex[:, :, :], bc_e(p_k[k]), ALU.is_lt)
                        v.drain()
                        v.scalar_tensor_tensor(t1[:, :, :], t1[:, :, :], 64.0, iota, ALU.mult, ALU.add)
                        v.drain()
                        v.tensor_reduce(m[:, :], t1[:, :, :], AX.X, ALU.min)
                        v.drain()
                        v.tensor_tensor(oh[k][:, :, :], iota, bc_e(m), ALU.is_equal)
                        v.drain()
                        v.scalar_tensor_tensor(ex[:, :, :], oh[k][:, :, :], -4.0, ex[:, :, :], ALU.mult, ALU.add)
                        v.drain()
                    if renorm:
                        v.tensor_tensor(m[:, :], p_k[0][:, :], p_k[1][:, :], ALU.add)
                        v.drain()
                        v.tensor_scalar(m[:, :], m[:, :], eps_sum, None, ALU.add)
                        v.drain()
                        v.reciprocal(m[:, :], m[:, :])
                        v.drain()
                        for k in range(K):
                            v.tensor_tensor(p_k[k][:, :], p_k[k][:, :], m[:, :], ALU.mult)
                        v.drain()
                    v.tensor_tensor(t1[:, :, :], oh[0][:, :, :], oh[1][:, :, :], ALU.add)
                    v.drain()
                    for k in range(2, K):
                        v.tensor_tensor(t1[:, :, :], t1[:, :, :], oh[k][:, :, :], ALU.add)
                        v.drain()
                    v.tensor_copy(Mb[:, :, :], t1[:, :, :]).then_inc(mask_ready, 1)
                    v.wait_ge(rank_ready, 1)
                    if cap:
                        v.tensor_scalar(cnti[:, :], cntp, float(cap), float(BS - 1), ALU.min, ALU.add)
                    else:
                        v.tensor_scalar(cnti[:, :], cntp, float(BS - 1), None, ALU.add)
                    v.drain()
                    sh = BS.bit_length() - 1
                    v.tensor_scalar(cnti[:, :], cnti[:, :], sh, sh, ALU.logical_shift_right, ALU.logical_shift_left)
                    v.drain()
                    v.tensor_copy(cnt[:, :], cnti[:, :])
                    v.drain()
                    v.tensor_tensor(tE[:, :, :], cnt[:, :].rearrange("p (o e) -> p o e", o=1).broadcast_to([P, E, E]),
                                    G["below_e"][:, 0:E, 0:E], ALU.mult)
                    v.drain()
                    v.tensor_reduce(offs[:, :], tE[:, :, :], AX.X, ALU.add)
                    v.drain()
                    v.tensor_tensor(ends[:, :], offs[:, :], cnt[:, :], ALU.add)
                    v.drain()
                    v.tensor_tensor(tB[:, :, :], ends[:, :].rearrange("p (o e) -> p o e", o=1).broadcast_to([P, NR, E]),
                                    G["iota_b"][:, 0:NR].rearrange("p (b o) -> p b o", o=1).broadcast_to([P, NR, E]), ALU.is_le)
                    v.drain()
                    v.tensor_reduce(nblk[:, :], tB[:, :, :], AX.X, ALU.add)
                    v.drain()
                    v.tensor_scalar(blk[:, :], nblk[:, :], float(E - 1), float(shared), ALU.min, ALU.add)
                    if cap:
                        v.tensor_scalar(t2[:, :, :], rank[:, :, :], float(cap), None, ALU.is_lt)
                    v.tensor_tensor(lg[:, :, :], rank[:, :, :], offs[:, :].rearrange("p (o e) -> p o e", o=1).broadcast_to([P, T, E]), ALU.add)
                    v.drain()
                    for k in range(K):
                        v.tensor_tensor(t1[:, :, :], lg[:, :, :], oh[k][:, :, :], ALU.mult)
                        v.drain()
                        v.tensor_reduce(m[:, :], t1[:, :, :], AX.X, ALU.add)
                        v.drain()
                        if cap:
                            v.tensor_tensor(t1[:, :, :], t2[:, :, :], oh[k][:, :, :], ALU.mult)
                            v.drain()
                            v.tensor_reduce(keep[:, :], t1[:, :, :], AX.X, ALU.add)
                            v.drain()
                            v.tensor_tensor(p_k[k][:, :], p_k[k][:, :], keep[:, :], ALU.mult)
                            v.tensor_scalar(r[:, :], keep[:, :], -1.0e6, 1.0e6 + BASE, ALU.mult, ALU.add)
                            v.drain()
                            v.tensor_tensor(m[:, :], m[:, :], r[:, :], ALU.add)
                            v.drain()
                            v.tensor_copy(slot_w[:, :, k], m[:, :])
                            v.tensor_scalar(slot_r[:, :, k], m[:, :], float(ROWS - 1), None, ALU.min)
                        else:
                            v.tensor_scalar(slot_w[:, :, k], m[:, :], float(BASE), None, ALU.add)
                            v.tensor_scalar(slot_r[:, :, k], m[:, :], float(BASE), None, ALU.add)
                        v.tensor_scalar(p_k[k][:, :], p_k[k][:, :], tg, None, ALU.mult)
                        v.drain()

        with ExitStack() as c2:
            M = Alloc(nc, c2, name + "m")
            raw = [M.sb(f"raw{s}", [P, CW]) for s in range(NS)]
            whi = [M.sb(f"whi{s}", [P, WW], F32R) for s in range(NS)]
            wlo = [M.sb(f"wlo{s}", [P, WW], F32R) for s in range(NS)]
            b12 = [M.sb(f"b12_{s}", [P, 1 + P]) for s in range(NS)] if biases else None
            xr = [M.sb(f"xr{q}", [P, BT, D]) for q in range(2)]
            xT = [[M.sb(f"xT{h}{q}", [P, KC, BS], F32R) for q in range(2)] for h in ("hi", "lo")]
            act_sb = [M.sb(f"act{q}", [P, BS]) for q in range(2)]
            h_f = [M.sb(f"h_f{q}", [P, BS]) for q in range(2)] if glu else act_sb
            hh = [[M.sb(f"h{h}{q}", [P, BS], F32R) for q in range(2)] for h in ("hi", "lo")]
            y_sb = [M.sb(f"y{q}", [P, BT, D]) for q in range(2)]
            NG = 4
            gath = [M.sb(f"gath{q}", [P, K + 1, D]) for q in range(NG)]
            gu = [M.ps(f"gu{q}", [P, 512]) for q in range(2)]
            yp = [M.ps(f"yp{q}", [P, 512]) for q in range(2)]
            xtp = [M.ps(f"xtp{q}", [P, 512]) for q in range(2)]
            w_in = [M.sem(f"w_in{s}") for s in range(NS)]
            x_in = [M.sem(f"x_in{q}") for q in range(2)]
            y_out = [M.sem(f"y_out{q}") for q in range(2)]
            w_hi, w_lo_v, w_lo_p, b_ok, scattered, xt_ready, xT_hi, xT_lo, gu_ready, act_done, h_ready, h_used, y_copied = (
                M.sem(s) for s in ("w_hi", "w_lo_v", "w_lo_p", "b_ok", "scattered", "xt_ready", "xT_hi", "xT_lo", "gu_ready",
                                   "act_done", "h_ready", "h_used", "y_copied"))
            all_out = M.sem("all_out")
            g_in = [M.sem(f"g_in{q}") for q in range(NG)]
            s_in = [M.sem(f"s_in{q}") for q in range(NG)]
            g_used = M.sem("g_used")
            SI = SJ // 2
            CUTS = [1, 2, SI - 1, SI, SI + 1, NI - 1] if shared else [1, 2, NI - 1]

            def w_views(s):
                hi, lo = whi[s], wlo[s]
                first = [[(hi[:, k * W1 + g * P:k * W1 + (g + 1) * P], lo[:, k * W1 + g * P:k * W1 + (g + 1) * P])
                          for g in range(W1 // P)] for k in range(KC)]
                return first, (hi[:, KC * W1:WW], lo[:, KC * W1:WW])

            def in_shared(i, lo, hi, job):
                a, b = 2 * lo + job < SJ, 2 * hi + job < SJ
                assert a == b
                return a

            def of_lo(i, lo, hi, c):
                return (w_lo_v, CI, c + 1) if in_shared(i, lo, hi, c // FC) else (w_lo_p, CI, c + 1 - SJ * FC)

            def split_lo(e, i, lo, hi, c):
                s = c % NS
                wait(e, b_ok if biases else w_hi, i, lo, CI, c + 1)
                wait(e, h_used, i, lo, CI, c - NS + 1)
                e.tensor_tensor(wlo[s][:, :], raw[s][:, 0:WW], whi[s][:, :].bitcast(F32), ALU.subtract).then_inc(
                    w_lo_v if in_shared(i, lo, hi, c // FC) else w_lo_p, 1)

            with nc.Block() as block:
                @block.sync
                def _(sp):
                    def load_w(i, lo, hi, c, expert):
                        s = c % NS
                        src = w_dram[expert, c % FC] if isinstance(expert, int) else \
                            w_dram[bass.ds(expert, 1), c % FC].rearrange("o p w -> (o p) w")
                        sem, a, b = of_lo(i, lo, hi, c - NS)
                        wait(sp, sem, i, lo, a, b)
                        sp.dma_start(raw[s][:, :], src).then_inc(w_in[s], 16)

                    def load_x(i, lo, hi, job):
                        q, rows = job % 2, rows_of(rows_x, i, job)
                        wait(sp, xt_ready, i, lo, 2, job - 1)
                        sp.dma_start(xr[q][:, :, :], rows).then_inc(x_in[q], 16)

                    def rows_of(dram, i, job):
                        a = (2 * i + job) * BS
                        if isinstance(i, int):
                            return dram[a:a + BS, :].rearrange("(t p) d -> p t d", p=P)
                        return dram[bass.ds(sp.snap(a), BS), :].rearrange("(t p) d -> p t d", p=P)

                    def expert_of(i, lo, hi, job):
                        if in_shared(i, lo, hi, job):
                            return 0
                        at = 2 * i + (job - SJ)
                        ap = blk[0:1, at:at + 1] if isinstance(i, int) else blk[0:1, bass.ds(at, 1)]
                        return sp.value_load(ap, min_val=0, max_val=E - 1 + shared)

                    first = [expert_of(0, 0, 0, j) for j in range((NS - 1) // FC + 1)]
                    for c in range(NS):
                        load_w(0, 0, 0, c, first[c // FC])
                    if not shared:
                        sp.wait_ge(scattered, 16 * T * K)
                    load_x(0, 0, 0, 0)
                    load_x(0, 0, 0, 1)

                    def body(i, lo, hi):
                        known = {}
                        for c in range(CI):
                            j, cj = divmod(c, FC)
                            if cj == 0:
                                if hi < NI - 1 or j < 0:
                                    if shared and lo == SI - 1 and j == 0:
                                        sp.wait_ge(scattered, 16 * T * K)
                                    load_x(i, lo, hi, j + 2)
                            if hi < NI - 1 or c + NS < CI:
                                tj = (c + NS) // FC
                                if tj not in known:
                                    known[tj] = expert_of(i, lo, hi, tj)
                                load_w(i, lo, hi, c + NS, known[tj])
                            if cj == min(1, FC - 1):
                                if not (lo == 0 and j == 0):
                                    store_y(i, lo, hi, j - 1)

                    def store_y(i, lo, hi, job):
                        q, rows = job % 2, rows_of(rows_y, i, job)
                        wait(sp, y_copied, i, lo, 2, job + 1)
                        sp.dma_start(rows, y_sb[q][:, :, :]).then_inc(y_out[q], 16)

                    run_loop(sp, NI, CUTS, body)
                    store_y(NI - 1, NI - 1, NI - 1, 1)
                    for q in range(2):
                        sp.wait_ge(y_out[q], 16 * NI)
                    sp.nop().then_inc(all_out, 1)
                    if shared:
                        for t in range(T):
                            if t >= NG:
                                sp.wait_ge(g_used, t - NG + 1)
                            sp.dma_start(gath[t % NG][:, K, :], rows_y[t * P:(t + 1) * P, :]).then_inc(s_in[t % NG], 16)

                @block.gpsimd
                def _(pool):
                    def scatter(t, k):
                        pool.indirect_dma_start(out=rows_x[0:ROWS, :],
                                                out_offset=bass.IndirectOffsetOnAxis(ap=slot_w[:, t, k:k + 1], axis=0),
                                                in_=n_all[:, t, :], in_offset=None,
                                                bounds_check=ROWS - 1, oob_is_err=False).then_inc(scattered, 16)

                    for t in range(T):
                        for k in range(K):
                            scatter(t, k)

                    if not shared:
                        for c in range(LA):
                            split_lo(pool, 0, 0, 0, c)

                    def body(i, lo, hi):
                        for c in range(LA, CI + LA):
                            if hi == NI - 1 and c >= CI:
                                continue
                            if not in_shared(i, lo, hi, c // FC):
                                split_lo(pool, i, lo, hi, c)

                    run_loop(pool, NI, CUTS, body, start=max(SI - 1, 0))
                    pool.wait_ge(all_out, 1)
                    for t in range(T):
                        if t >= NG:
                            pool.wait_ge(g_used, t - NG + 1)
                        for k in range(K):
                            pool.indirect_dma_start(out=gath[t % NG][:, k, :], out_offset=None, in_=rows_y[0:ROWS, :],
                                                    in_offset=bass.IndirectOffsetOnAxis(ap=slot_r[:, t, k:k + 1], axis=0)
                                                    ).then_inc(g_in[t % NG], 16)

                @block.scalar
                def _(act):
                    def split_hi(i, lo, hi, c):
                        s = c % NS
                        wait(act, w_in[s], i, lo, 16 * per_slot, 16 * (c // NS + 1))
                        wait(act, h_used, i, lo, CI, c - NS + 1)
                        act.activation(whi[s][:, :], raw[s][:, 0:WW], ACT.Copy).then_inc(w_hi, 1)

                    def x_hi(i, lo, hi, job):
                        wait(act, xt_ready, i, lo, 2, job + 1)
                        wait(act, gu_ready, i, lo, CI, FC * (job - 1))
                        act.activation(xT[0][job % 2][:, :, :], xtp[job % 2][:, :].rearrange("p (k n) -> p k n", k=KC), ACT.Copy).then_inc(xT_hi, 1)

                    def copy_y(i, lo, hi, job):
                        q = job % 2
                        wait(act, h_used, i, lo, CI, FC * (job + 1))
                        wait(act, y_out[q], i, lo, 16, 16 * ((job - 2 - q) // 2 + 1))
                        act.activation(y_sb[q][:, :, :], yp[q][:, :].rearrange("p (t n) -> p t n", t=BT), ACT.Copy).then_inc(y_copied, 1)

                    split_hi(0, 0, 0, 0)
                    x_hi(0, 0, 0, 0)
                    for c in range(1, LA):
                        split_hi(0, 0, 0, c)

                    def body(i, lo, hi):
                        for c in range(CI):
                            j, cj = divmod(c, FC)
                            last = hi == NI - 1
                            wait(act, gu_ready, i, lo, CI, c + 1)
                            if glu:
                                wait(act, h_ready, i, lo, CI, c - 1)
                                act.activation(act_sb[c % 2][:, :], gu[c % 2][:, 0:BS], func).then_inc(act_done, 1)
                            else:
                                wait(act, h_ready, i, lo, CI, c - 1)
                                if biases:
                                    wait(act, b_ok, i, lo, CI, c + 1)
                                    act.activation(h_f[c % 2][:, :], gu[c % 2][:, 0:BS], func, bias=b12[c % NS][:, 0:1]).then_inc(act_done, 1)
                                else:
                                    act.activation(h_f[c % 2][:, :], gu[c % 2][:, 0:BS], func).then_inc(act_done, 1)
                            if not (last and c + LA >= CI):
                                split_hi(i, lo, hi, c + LA)
                            if cj == 0 and not (last and j == 1):
                                x_hi(i, lo, hi, j + 1)
                            if not biases and cj == 0 and not (lo == 0 and j == 0):
                                copy_y(i, lo, hi, j - 1)

                    run_loop(act, NI, CUTS, body)
                    if not biases:
                        copy_y(NI - 1, NI - 1, NI - 1, 1)

                @block.vector
                def _(v):
                    def x_lo(i, lo, hi, job):
                        wait(v, xT_hi, i, lo, 2, job + 1)
                        v.tensor_tensor(xT[1][job % 2][:, :, :], xtp[job % 2][:, :].rearrange("p (k n) -> p k n", k=KC),
                                        xT[0][job % 2][:, :, :].bitcast(F32), ALU.subtract).then_inc(xT_lo, 1)

                    def take_b(i, lo, hi, c):
                        s = c % NS
                        wait(v, w_hi, i, lo, CI, c + 1)
                        wait(v, h_used, i, lo, CI, c - NS + 1)
                        v.tensor_copy(b12[s][:, :], raw[s][:, WW:CW]).then_inc(b_ok, 1)

                    def y_bias(i, lo, hi, job):
                        q = job % 2
                        wait(v, h_used, i, lo, CI, FC * (job + 1))
                        wait(v, y_out[q], i, lo, 16, 16 * ((job - 2 - q) // 2 + 1))
                        for cj in range(FC):
                            s = (job * FC + cj) % NS
                            b2 = b12[s][:, 1:1 + P].rearrange("p (o n) -> p o n", o=1).broadcast_to([P, BT, P])
                            ins = v.tensor_tensor(y_sb[q][:, :, cj * P:(cj + 1) * P],
                                                  yp[q][:, :].rearrange("p (t n) -> p t n", t=BT)[:, :, cj * P:(cj + 1) * P], b2, ALU.add)
                        ins.then_inc(y_copied, 1)

                    for c in range(LA if biases else 0):
                        take_b(0, 0, 0, c)
                    for c in range(LA if shared else 0):
                        split_lo(v, 0, 0, 0, c)
                    x_lo(0, 0, 0, 0)

                    def body(i, lo, hi):
                        for c in range(CI):
                            j, cj = divmod(c, FC)
                            last = hi == NI - 1
                            if biases and cj == 0 and not (lo == 0 and j == 0):
                                y_bias(i, lo, hi, j - 1)
                            wait(v, act_done, i, lo, CI, c + 1)
                            q = c % 2
                            if glu:
                                v.tensor_tensor(h_f[q][:, :], act_sb[q][:, :], gu[q][:, BS:2 * BS], ALU.mult)
                                v.drain()
                            wait(v, h_used, i, lo, CI, c - 1)
                            v.tensor_copy(hh[0][q][:, :], h_f[q][:, :])
                            v.drain()
                            v.tensor_tensor(hh[1][q][:, :], h_f[q][:, :], hh[0][q][:, :].bitcast(F32), ALU.subtract).then_inc(h_ready, 1)
                            if not (last and c + LA >= CI):
                                if biases:
                                    take_b(i, lo, hi, c + LA)
                                if in_shared(i, lo, hi, (c + LA) // FC):
                                    split_lo(v, i, lo, hi, c + LA)
                            if cj == 0 and not (last and j == 1):
                                x_lo(i, lo, hi, j + 1)

                    run_loop(v, NI, CUTS, body)
                    if biases:
                        y_bias(NI - 1, NI - 1, NI - 1, 1)
                    for t in range(T):
                        q = t % NG
                        v.wait_ge(g_in[q], 16 * K * (t // NG + 1))
                        if shared:
                            v.wait_ge(s_in[q], 16 * (t // NG + 1))
                            v.scalar_tensor_tensor(x[:, t, :], gath[q][:, K, :], tg, x[:, t, :], ALU.mult, ALU.add)
                            v.drain()
                        for k in range(K):
                            ins = v.scalar_tensor_tensor(x[:, t, :], gath[q][:, k, :], p_k[k][:, t:t + 1], x[:, t, :], ALU.mult, ALU.add)
                            v.drain()
                        if add_input:
                            v.scalar_tensor_tensor(x[:, t, :], n_all[:, t, :], tg, x[:, t, :], ALU.mult, ALU.add)
                        v.drain().then_inc(g_used, 1)

                @block.tensor
                def _(pe):
                    def x_turn(i, lo, hi, job):
                        q = job % 2
                        wait(pe, x_in[q], i, lo, 16, 16 * (job // 2 + 1))
                        wait(pe, xT_lo, i, lo, 2, job - 1)
                        for k in range(KC):
                            for t in range(BT):
                                mm = pe.transpose(xtp[q][:, k * BS + t * P:k * BS + (t + 1) * P], xr[q][:, t, k * P:(k + 1) * P], ident[:, :])
                        mm.then_inc(xt_ready, 1)

                    def first_product(i, lo, hi, c):
                        j, cj = divmod(c, FC)
                        q, s = j % 2, c % NS
                        if cj == 0:
                            wait(pe, xT_lo, i, lo, 2, j + 1)
                        wait(pe, w_hi, i, lo, CI, c + 1)
                        sem, a, b = of_lo(i, lo, hi, c)
                        wait(pe, sem, i, lo, a, b)
                        wait(pe, h_ready, i, lo, CI, c - 1)
                        w, _ = w_views(s)
                        for g in range(W1 // P):
                            for k in range(KC):
                                mm = mm3(pe, gu[c % 2][:, g * BS:(g + 1) * BS], w[k][g],
                                         (xT[0][q][:, k, :], xT[1][q][:, k, :]), k == 0, k == KC - 1)
                        mm.then_inc(gu_ready, 1)

                    def second_product(i, lo, hi, c):
                        j, cj = divmod(c, FC)
                        q, s = j % 2, c % NS
                        wait(pe, h_ready, i, lo, CI, c + 1)
                        if cj == 0:
                            wait(pe, y_copied, i, lo, 2, j - 1)
                        _, w = w_views(s)
                        for t in range(BT):
                            h = (hh[0][c % 2][:, t * P:(t + 1) * P], hh[1][c % 2][:, t * P:(t + 1) * P])
                            mm = mm3(pe, yp[q][:, t * D:(t + 1) * D], h, w, cj == 0 and t == 0, cj == FC - 1 and t == BT - 1,
                                     skip_group_check=True)
                        mm.then_inc(h_used, 1)

                    x_turn(0, 0, 0, 0)
                    first_product(0, 0, 0, 0)

                    def body(i, lo, hi):
                        last = hi == NI - 1
                        for c in range(CI):
                            j, cj = divmod(c, FC)
                            if cj == 0 and not (last and j == 1):
                                x_turn(i, lo, hi, j + 1)
                            if not (last and c == CI - 1):
                                first_product(i, lo, hi, c + 1)
                            second_product(i, lo, hi, c)

                    run_loop(pe, NI, CUTS, body)



def constants():
    i = np.arange(P)
    e = np.arange(16)
    f = np.arange(S, dtype=np.float32)[:, None] * (1.0 / 10000.0 ** (np.arange(0, 16, 2, dtype=np.float32) / 16)).astype(np.float32)[None]
    cs = np.stack([np.cos(f), -np.sin(f), np.sin(f)], 1).astype(np.float32).reshape(TB, P, 3, 8).transpose(1, 0, 2, 3)
    later = np.where(np.arange(S)[None, :] > np.arange(S)[:, None], 1e9, 0.0).astype(np.float32).reshape(TB, P, S).transpose(1, 0, 2)
    return {
        "rotary": np.ascontiguousarray(cs),
        "causal": np.ascontiguousarray(later),
        "ident": np.eye(P, dtype=np.float32),
        "before": (i[:, None] < i[None, :]).astype(np.float32),
        "below_e": np.broadcast_to((e[None, :] < e[:, None]).astype(np.float32), (P, 16, 16)).copy(),
        "iota_e": np.broadcast_to(e.astype(np.float32), (P, 16)).copy(),
        "iota_b": np.broadcast_to((BS * np.arange(40)).astype(np.float32), (P, 40)).copy(),
    }


def setup_phase(nc, G, I):
    with ExitStack() as ctx:
        A = Alloc(nc, ctx, "set")
        loaded = A.sem("loaded")
        before = A.sb("before", [P, P])
        g8 = A.sb("g8", [P, 8])
        c_raw = [A.sb(f"c_raw{q}", [P, TB, D]) for q in range(2)]
        cT = [[A.sb(f"cT_{h}{q}", [P, KC, S], F32R) for q in range(2)] for h in ("hi", "lo")]
        c_ps = [A.ps(f"c_ps{q}", [P, KC, S]) for q in range(2)]
        c_in = [A.sem(f"c_in{q}") for q in range(2)]
        c_out = [A.sem(f"c_out{q}") for q in range(2)]
        c_turned, c_hi, c_lo = A.sem("c_turned"), A.sem("c_hi"), A.sem("c_lo")
        with nc.Block() as block:
            @block.sync
            def _(sp):
                sp.dma_start(G["x"][:, :, :], I["x"].rearrange("b (t p) d -> p (b t) d", p=P)).then_inc(loaded, 16)
                for q, name in enumerate(("g_xattn", "g_ffn")):
                    sp.dma_start(g8[:, 4 * q:4 * q + 4], I[name].rearrange("(a n) -> a n", a=1).broadcast_to([P, 4])).then_inc(loaded, 16)
                for name in ("ident", "below_e", "iota_e", "iota_b"):
                    sp.dma_start(G[name].ap(), I[name]).then_inc(loaded, 16)
                sp.dma_start(before[:, :], I["before"]).then_inc(loaded, 16)
                def load_c(b):
                    if b >= 2:
                        sp.wait_ge(c_turned, b - 1)
                    sp.dma_start(c_raw[b % 2][:, :, :], I["ctx_1024"][b].rearrange("(t p) d -> p t d", p=P)).then_inc(c_in[b % 2], 16)

                load_c(0)
                load_c(1)
                for b in range(B):
                    sp.wait_ge(c_lo, b + 1)
                    for h in range(2):
                        sp.dma_start(G["ctxT"][h][b], cT[h][b % 2][:, :, :].bitcast(F32)).then_inc(c_out[b % 2], 16)
                    if b + 2 < B:
                        load_c(b + 2)
                for q in range(2):
                    sp.wait_ge(c_out[q], 16 * B)
                sp.wait_ge(loaded, 16 * 8)

            @block.vector
            def _(v):
                v.memset(G["ones_bf"][:, :], 1.0)
                v.wait_ge(loaded, 16 * 8)
                v.tensor_copy(G["before_bf"][:, :], before[:, :])
                for b in range(B):
                    v.wait_ge(c_hi, b + 1)
                    v.tensor_tensor(cT[1][b % 2][:, :, :], c_ps[b % 2][:, :, :], cT[0][b % 2][:, :, :].bitcast(F32), ALU.subtract).then_inc(c_lo, 1)

            @block.scalar
            def _(act):
                act.wait_ge(loaded, 16 * 8)
                act.activation(G["tanh_g"][:, :], g8[:, :], ACT.Tanh)
                act.activation(G["identr"][:, :], G["ident"][:, :], ACT.Copy)
                for b in range(B):
                    act.wait_ge(c_turned, b + 1)
                    if b >= 2:
                        act.wait_ge(c_out[b % 2], 32 * (b // 2))
                    act.activation(cT[0][b % 2][:, :, :], c_ps[b % 2][:, :, :], ACT.Copy).then_inc(c_hi, 1)

            @block.tensor
            def _(pe):
                pe.wait_ge(loaded, 16 * 8)
                for b in range(B):
                    pe.wait_ge(c_in[b % 2], 16 * (b // 2 + 1))
                    if b >= 2:
                        pe.wait_ge(c_lo, b - 1)
                    for k in range(KC):
                        for t in range(TB):
                            mm = pe.transpose(c_ps[b % 2][:, k, t * P:(t + 1) * P], c_raw[b % 2][:, t, k * P:(k + 1) * P], G["ident"][:, :])
                    mm.then_inc(c_turned, 1)


def globals_of(nc, A):
    G = {
        "x": A.sb("x", [P, T, D]),
        "ident": A.sb("ident", [P, P]),
        "identr": A.sb("identr", [P, P], F32R),
        "before_bf": A.sb("before_bf", [P, P], BF16),
        "ones_bf": A.sb("ones_bf", [P, P], BF16),
        "below_e": A.sb("below_e", [P, 16, 16]),
        "iota_e": A.sb("iota_e", [P, 16]),
        "iota_b": A.sb("iota_b", [P, 40]),
        "tanh_g": A.sb("tanh_g", [P, 8]),
        "rows_x": nc.dram_tensor("rows_x", [XROWS, D], F32).ap(),
        "ctxT": [nc.dram_tensor(f"ctxT_{h}", [B, P, KC, S], F32).ap() for h in ("hi", "lo")],
        "rows_y": nc.dram_tensor("rows_y", [XROWS, D], F32).ap(),
    }
    return G


def final_phase(nc, G, out):
    with ExitStack() as ctx:
        A = Alloc(nc, ctx, "fin")
        stored = A.sem("stored")
        with nc.Block() as block:
            @block.sync
            def _(sp):
                sp.dma_start(out.rearrange("b (t p) d -> p (b t) d", p=P), G["x"][:, :, :]).then_inc(stored, 16)
                sp.wait_ge(stored, 16)


def moe_layer(nc, G, I, layer):
    if layer == 0:
        moe_phase(nc, G, "moe0", 0, E=15, K=3, FC=2, glu=False, func=ACT.Relu, shared=True, w_dram=I["moe_w0"],
                  rw_dram=I["L0_ffn_router_W"].rearrange("(k p) e -> p k e", p=P), rb_dram=I["L0_ffn_router_b"], biases=True)
    if layer == 1:
        moe_phase(nc, G, "moe1", 1, E=8, K=2, FC=6, glu=True, func=ACT.Silu, shared=True, w_dram=I["moe_w1"],
                  rw_dram=I["rw1"].rearrange("(k p) e -> p k e", p=P), renorm=True, eps_sum=1e-20)
    if layer == 2:
        moe_phase(nc, G, "moe2", 2, E=8, K=2, FC=8, glu=True, func=ACT.Silu, shared=False, w_dram=I["moe_w2"],
                  rw_dram=I["rw2"].rearrange("(k p) e -> p k e", p=P), eps_sum=1e-12, cap=640, clip=10000.0,
                  inner_norm=(I["L2_ffn_ln_gamma"], I["L2_ffn_ln_beta"]))
    if layer == 3:
        moe_phase(nc, G, "moe3", 3, E=8, K=2, FC=8, glu=False, func=ACT.Gelu, shared=True, w_dram=I["moe_w3"],
                  rw_dram=I["L3_ffn_router_w"].rearrange("(k p) e -> p k e", p=P), add_input=True)


def pack_chunks(ups, down, b1=None, b2=None):
    e, _, f = ups[0].shape
    fc = -(-f // P)
    up = np.stack(ups, 2)
    up = np.pad(up, ((0, 0), (0, 0), (0, 0), (0, fc * P - f)))
    up = up.reshape(e, KC, P, len(ups), fc, P).transpose(0, 4, 2, 1, 3, 5)
    dn = np.pad(down, ((0, 0), (0, fc * P - f), (0, 0))).reshape(e, fc, P, D)
    parts = [up.reshape(e, fc, P, -1), dn]
    if b1 is not None:
        parts.append(b1.reshape(e, fc, P, 1))
        parts.append(np.broadcast_to(b2.reshape(e, fc, 1, P), (e, fc, P, P)))
    return np.ascontiguousarray(np.concatenate(parts, 3))


def lay_out(inp):
    a = {k: np.asarray(v) for k, v in inp.items()}
    tr = lambda w: np.swapaxes(w, -1, -2)
    cat = lambda s, e: np.concatenate([s[None], e], 0)
    out = dict(constants())
    for k in ("ctx_1024", "mask_BxS2_if1", "L1_xattn_bo", "L2_xattn_bq", "L2_xattn_bk", "L2_xattn_bv", "L2_xattn_bo", "L2_xattn_Wq",
              "L2_xattn_Wk", "L2_xattn_Wv", "L3_xattn_ln_gamma", "L3_xattn_ln_beta", "L3_xattn_w_q", "L3_xattn_w_out", "L3_xattn_b_out",
              "L3_xattn_gate", "L0_xattn_Wq", "L0_xattn_Wk", "L0_xattn_Wv", "L0_xattn_Wcq", "L0_xattn_Wck", "L0_xattn_Wcv",
              "L0_xattn_gamma", "L0_xattn_beta", "L0_xattn_W1", "L0_xattn_b1"):
        out[k] = a[k]
    turn = lambda w: np.ascontiguousarray(w.reshape(*w.shape[:-1], 16, 8, 2).swapaxes(-1, -2).reshape(w.shape))
    twice = lambda w: np.ascontiguousarray(np.broadcast_to(w.reshape(16, 1, 16, D), (16, 2, 16, D)).reshape(512, D))
    for n in ("q", "k"):
        out[f"L1_W{n}"] = turn(np.ascontiguousarray(tr(a[f"L1_xattn_W{n}"])))
        out[f"L1_b{n}"] = turn(a[f"L1_xattn_b{n}"])
    out["L1_Wv"], out["L1_bv"] = np.ascontiguousarray(tr(a["L1_xattn_Wv"])), a["L1_xattn_bv"]
    out["L1_Wo"], out["L2_Wo"] = twice(tr(a["L1_xattn_Wo"])), twice(a["L2_xattn_Wo"])
    out["mask2"] = a["mask_Bx1xS2_ik0"].reshape(B, S)
    out["L3_w_k"], out["L3_w_v"] = (np.ascontiguousarray(a["L3_xattn_w_kv"][:, 1024 * q:1024 * (q + 1)]) for q in range(2))
    for k in ("x", "g_xattn", "g_ffn", "L0_ffn_router_W", "L0_ffn_router_b", "L2_ffn_ln_gamma", "L2_ffn_ln_beta", "L3_ffn_router_w"):
        out[k] = a[k]
    out["moe_w0"] = pack_chunks([cat(a["L0_ffn_sW1"], a["L0_ffn_eW1"])], cat(a["L0_ffn_sW2"], a["L0_ffn_eW2"]),
                                cat(a["L0_ffn_sb1"], a["L0_ffn_eb1"]), cat(a["L0_ffn_sb2"], a["L0_ffn_eb2"]))
    out["moe_w1"] = pack_chunks([tr(cat(a["L1_ffn_shared_gate"], a["L1_ffn_expert_gate"])), tr(cat(a["L1_ffn_shared_up"], a["L1_ffn_expert_up"]))],
                                tr(cat(a["L1_ffn_shared_down"], a["L1_ffn_expert_down"])))
    out["rw1"] = np.ascontiguousarray(tr(a["L1_ffn_gate_w"]))
    w12 = tr(a["L2_ffn_W12"])
    out["moe_w2"] = pack_chunks([w12[:, :, :1024], w12[:, :, 1024:]], tr(a["L2_ffn_W3"]))
    out["rw2"] = np.ascontiguousarray(tr(a["L2_ffn_Wr"]))
    out["moe_w3"] = pack_chunks([np.concatenate([a["L3_ffn_shared_up"], a["L3_ffn_routed_up"]])], np.concatenate([a["L3_ffn_shared_down"], a["L3_ffn_routed_down"]]))
    return out



def stats_all(v, src, st, nmean, rstd):
    for t in range(T):
        v.bn_stats(st["bn"][:, t, :], src[:, t, :])
    v.drain()
    for t in range(T):
        v.bn_aggr(st["mv"][:, t, :], st["bn"][:, t, :])
    v.drain()
    v.tensor_scalar(nmean, st["mv"][:, :, 0], -1.0, None, ALU.mult)
    rsqrt(v, rstd, st["mv"][:, :, 1], st["tmp"][:, :], 1e-5)


def load_split(nc, name, jobs, st_cols, loads=None, vector_first=None, scalar_first=None, pool_work=None):
    with ExitStack() as ctx:
        A = Alloc(nc, ctx, name)
        NR = 4
        raw = [A.sb(f"raw{q}", [P, st_cols]) for q in range(NR)]
        came = [A.sem(f"came{q}") for q in range(NR)]
        hi_done, lo_done = A.sem("hi_done"), A.sem("lo_done")
        with nc.Block() as block:
            @block.sync
            def _(sp):
                if loads:
                    loads(sp)
                for n, (src, hi, lo) in enumerate(jobs):
                    if n >= NR:
                        sp.wait_ge(lo_done, n - NR + 1)
                    sp.dma_start(raw[n % NR][:, 0:src.shape[1]], src).then_inc(came[n % NR], 16)

            @block.scalar
            def _(act):
                if scalar_first:
                    scalar_first(act)
                for n, (src, hi, lo) in enumerate(jobs):
                    act.wait_ge(came[n % NR], 16 * (n // NR + 1))
                    act.activation(hi, raw[n % NR][:, 0:src.shape[1]], ACT.Copy).then_inc(hi_done, 1)

            @block.vector
            def _(v):
                if vector_first:
                    vector_first(v)
                for n, (src, hi, lo) in enumerate(jobs):
                    v.wait_ge(hi_done, n + 1)
                    v.tensor_tensor(lo, raw[n % NR][:, 0:src.shape[1]], hi.bitcast(F32), ALU.subtract).then_inc(lo_done, 1)

            if pool_work:
                @block.gpsimd
                def _(pool):
                    pool_work(pool)


def heads_phase(nc, G, I, name, layer, dh, weights, mask=None, rotary=False, inner=None, biases=None, gate=None):
    H = 16
    small = dh == 16
    GH = 4 if small else 2
    NGR = H // GH
    OC = NGR
    LEAD = 3
    scale = 1.0 / float(np.sqrt(dh))
    HD = H * dh
    if small:
        ROUNDS = [(3, "nT", 0), (4, "q", 0), (5, "v", 0), (6, "k", 0), (7, "qT", 0), (8, "kT", 0), (9, "qT", 1), (10, "kT", 1),
                  (11, "qT", 2), (12, "kT", 2), (13, "qT", 3), (14, "kT", 3)]
        OWN = []
    else:
        ROUNDS = [(4, "nT", 0), (5, "nT", 1), (6, "qT", 0), (7, "kT", 0), (8, "qT", 1), (9, "kT", 1), (10, "V0", 0), (10, "qT", 2),
                  (11, "kT", 2), (12, "V0", 1), (13, "qT", 3), (14, "kT", 3)]
        OWN = [(2, "V1", 0), (3, "V1", 1)]
    PRO = len(ROUNDS)
    BODY = sorted(OWN + ROUNDS, key=lambda r: r[0])
    NRD = len(BODY)
    assert PRO % 2 == 0 and NRD % 2 == 0

    with ExitStack() as ctx:
        A = Alloc(nc, ctx, name)
        sb, ps, sem = A.sb, A.ps, A.sem
        hl = lambda n, shape: [sb(f"{n}_{h}", shape, F32R) for h in ("hi", "lo")]
        x, ident, identr = G["x"], G["ident"], G["identr"]
        wq, wk, wv = (hl(n, [P, KC, HD]) for n in ("wq", "wk", "wv"))
        wo = hl("wo", [P, OC, D])
        jobs = []
        for w, src in ((wq, weights["q"]), (wk, weights["k"]), (wv, weights["v"])):
            for k in range(KC):
                jobs.append((src[k * P:(k + 1) * P, :], w[0][:, k, :], w[1][:, k, :]))
        for c in range(OC):
            jobs.append((weights["o"][c * P:(c + 1) * P, :], wo[0][:, c, :], wo[1][:, c, :]))
        nmean, rstd = ([sb(f"{n}{q}", [P, T]) for q in range(2 if inner else 1)] for n in ("nmean", "rstd"))
        tg = sb("tg", [P, 1])
        bo = sb("bo", [P, D])
        gb = sb("gb", [P, 2, D]) if inner else None
        gate_sb = sb("gate", [P, 1]) if gate is not None else None
        if small:
            b3 = sb("b3", [P, 3, D])
            MT = TB if rotary else 1
            mask16 = sb("mask16", [P, B, MT, S], BF16)
            ident16 = sb("ident16", [P, P], BF16)
            kq = sb("kq", [P, B * TB])
            cs = sb("cs", [P, TB, 3, 8]) if rotary else None

            vp = sb("vp", [P, TB, 4, 640], F32R)
        else:
            QT = hl("QT", [P, H, S])

        with ExitStack() as c2:
            R = Alloc(nc, c2, name + "p")
            st = {"bn": R.sb("bn", [P, T, 6]), "mv": R.sb("mv", [P, T, 2]), "tmp": R.sb("tmp", [P, T])}
            loaded, tg_ready, once, normed = (R.sem(n) for n in ("loaded", "tg_ready", "once", "normed"))
            n1 = R.sb("n1", [P, T, D]) if inner else None
            nb = R.sb("nb", [P, T]) if inner else None
            if small:
                mi = R.sb("mi", [P, B, S], I32)
                row0 = R.sb("row0", [P, B, S], BF16)
                causal, causal16 = (R.sb("causal", [P, TB, S]), R.sb("causal16", [P, TB, S], BF16)) if rotary else (None, None)
            n_loads = 1 + (2 if inner else 0) + (gate is not None) + ((4 + 2 * rotary) if small else 0)

            def loads(sp):
                def row(dst, src, n):
                    sp.dma_start(dst, src.rearrange("(a d) -> a d", a=1).broadcast_to([P, n])).then_inc(loaded, 16)
                if small:
                    sp.dma_start(mi[:, :, :], mask.rearrange("b s -> (b s)").rearrange("(o n) -> o n", o=1).broadcast_to([P, B * S])
                                 .rearrange("p (b s) -> p b s", s=S)).then_inc(loaded, 16)
                    if rotary:
                        sp.dma_start(cs[:, :, :, :], I["rotary"]).then_inc(loaded, 16)
                        sp.dma_start(causal[:, :, :], I["causal"]).then_inc(loaded, 16)
                    for q in range(3):
                        row(b3[:, q, :], biases[q], D)
                row(bo[:, :], weights["bo"], D)
                if inner:
                    for q in range(2):
                        row(gb[:, q, :], inner[q], D)
                if gate is not None:
                    row(gate_sb[:, :], gate, 1)

            def vector_first(v):
                stats_all(v, x, st, nmean[0][:, :], rstd[0][:, :])
                if inner:
                    v.tensor_tensor(nb[:, :], nmean[0][:, :], rstd[0][:, :], ALU.mult).then_inc(once, 1)
                    v.wait_ge(normed, 1)
                    stats_all(v, n1, st, nmean[1][:, :], rstd[1][:, :])
                v.wait_ge(loaded, 16 * n_loads)
                if gate is not None:
                    v.wait_ge(tg_ready, 1)
                    v.tensor_tensor(tg[:, :], gate_sb[:, :], G["tanh_g"][:, layer:layer + 1], ALU.mult)
                else:
                    v.tensor_copy(tg[:, :], G["tanh_g"][:, layer:layer + 1])
                v.drain()
                v.tensor_scalar(bo[:, :], bo[:, :], tg[:, :], None, ALU.mult)
                if small:
                    v.tensor_scalar(b3[:, 0, :], b3[:, 0, :], -scale, None, ALU.mult)
                    v.tensor_copy(ident16[:, :], ident[:, :])
                    v.tensor_scalar(row0[:, :, :] if rotary else mask16[:, :, 0, :], mi[:, :, :], 0.0, 1.0e9 if rotary else BIG,
                                    ALU.is_equal, ALU.mult)
                if rotary:
                    v.tensor_copy(causal16[:, :, :], causal[:, :, :])
                    v.drain()
                    for b in range(B):
                        v.tensor_tensor(mask16[:, b, :, :], causal16[:, :, :],
                                        row0[:, b, :].rearrange("p (o s) -> p o s", o=1).broadcast_to([P, TB, S]), ALU.max)
                    v.drain()
                    v.tensor_reduce(kq[:, :], mask16[:, :, :, :].rearrange("p b t s -> p (b t) s"), AX.X, ALU.min)
                    v.drain()
                    v.tensor_scalar(kq[:, :], kq[:, :], 0.0, None, ALU.is_equal)

            def scalar_first(act):
                if inner:
                    act.wait_ge(once, 1)
                    for t in range(T):
                        ins = act.activation(n1[:, t, :], x[:, t, :], ACT.Identity, scale=rstd[0][:, t:t + 1], bias=nb[:, t:t + 1])
                    ins.then_inc(normed, 1)
                if gate is not None:
                    act.wait_ge(loaded, 16 * n_loads)
                    act.activation(gate_sb[:, :], gate_sb[:, :], ACT.Tanh).then_inc(tg_ready, 1)

            def pool_work(pool):
                if small:
                    pool.memset(vp[:, :, :, :].bitcast(F32), 0.0)
                else:
                    for y in QT:
                        pool.memset(y[:, :, :].bitcast(F32), 0.0)

            load_split(nc, name + "w", jobs, HD, loads, vector_first, scalar_first, pool_work)

        n_sb = sb("n", [P, TB, D])
        nT = hl("nT", [P, KC, S])
        cT = hl("cT", [P, KC, S])
        if small:
            QT, KT = sb("QT", [P, 8, S], F32R), sb("KT", [P, 8, S], F32R)
            qf, kf, vf = sb("qf", [P, TB, D]), sb("kf", [P, TB, D]), sb("vf", [P, TB, D])
            qs, ks = (sb(n, [P, TB * H, 4, dh], F32R) for n in ("qs", "ks"))
            if rotary:
                r1, r2 = sb("turn1", [P, TB, D]), sb("turn2", [P, TB, D])
        else:
            KT = hl("KT", [P, 8, S])
            V = hl("V", [P, TB, HD])
        p_sb = [sb(f"p{q}", [P, TB, S]) for q in range(4)]
        nm, rs, ri = (sb(n, [P, 4, TB]) for n in ("nm", "rs", "ri"))
        pT = [[sb(f"pT{h}{q}", [P, KC, S], F32R) for q in range(4)] for h in ("hi", "lo")]
        OT = hl("OT", [P, OC, S])
        s_ps = [ps(f"s{q}", [P, TB, S]) for q in range(2)]
        t_ps = [ps(f"t{q}", [P, KC, S]) for q in range(2)]
        o_ps = [ps(f"o{q}", [P, 512]) for q in range(2)]
        r_ps = [ps(f"r{q}", [P, 512]) for q in range(2)]
        c_in, normed = sem("c_in"), sem("normed")
        s_ready, m_ready, e_done, r_done, n_done, t_ready, ph_done, pl_done, pv_done, oh_done, ol_done, out_ready, x_done = (
            sem(n) for n in ("s_ready", "m_ready", "e_done", "r_done", "n_done", "t_ready", "ph_done", "pl_done", "pv_done",
                             "oh_done", "ol_done", "out_ready", "x_done"))
        n_ready, rd_ready, rd_hi, rd_done, f_ready, v_half = (
            sem(n) for n in ("n_ready", "rd_ready", "rd_hi", "rd_done", "f_ready", "v_half"))
        vh_done = sem("vh_done")
        CUTS = [1, B - 1]

        def body_rounds(last):
            return [r for r in BODY if not last or r in OWN]

        def rounds_at(h, last):
            return [(pos, kind, part) for pos, (slot, kind, part) in enumerate(body_rounds(last)) if slot == h]

        def done_by(kind, part=0):
            return [(r[1], r[2]) for r in BODY].index((kind, part)) + 1

        def _(v):
                if small:
                    v.memset(vp[:, :, :, :].bitcast(F32), 0.0)
                else:
                    v.memset(QT[0][:, :, :].bitcast(F32), 0.0)
                    v.memset(QT[1][:, :, :].bitcast(F32), 0.0)

        def x_of(i, b):
            at = TB * (i + b)
            return x[:, at:at + TB, :] if isinstance(i, int) else x[:, bass.ds(at, TB), :]

        def v_cols(kc, half, e):
            cols = vp[:, kc, 2 * half:2 * half + 2, :].rearrange("p g (j c) -> p g j c", c=P + 32)
            return cols[:, :, :, dh * e:dh * e + dh]

        def vf_cols(kc, half):
            return vf[:, kc, 128 * half:128 * half + 128].rearrange("p (g j d) -> p g j d", g=2, j=4)

        def bc_t(a, n):
            return a.rearrange("p (o n) -> p o n", o=1).broadcast_to([P, TB, n])

        with nc.Block() as block:
            @block.sync
            def _(sp):
                def load_c(i, lo, hi, nxt):
                    b = i + nxt
                    srcs = [G["ctxT"][h][b] if isinstance(b, int) else
                            G["ctxT"][h][bass.ds(sp.snap(b), 1)].rearrange("o p k s -> (o p) k s") for h in range(2)]
                    if small:
                        if not (isinstance(i, int) and i + nxt == 0):
                            wait(sp, rd_ready, i, lo, NRD, PRO + NRD * (nxt - 2) + done_by("k"))
                    elif not (isinstance(i, int) and i + nxt == 0):
                        wait(sp, rd_ready, i, lo, NRD, PRO + NRD * (nxt - 1) + done_by("V1", 1))
                    for h in range(2):
                        sp.dma_start(cT[h][:, :, :].bitcast(F32), srcs[h]).then_inc(c_in, 16)

                load_c(0, 0, 0, 0)

                def body(i, lo, hi):
                    if hi < B - 1:
                        load_c(i, lo, hi, 1)

                run_loop(sp, B, CUTS, body)

            @block.tensor
            def _(pe):
                def scores(i, lo, s):
                    h = s % H
                    q = s % 2
                    part = h // 4
                    if h % 4 == 0:
                        turn = s // H - 1
                        wait(pe, rd_done, i, lo, NRD, PRO + turn * NRD + done_by("kT", part))
                    wait(pe, e_done, i, lo, H, s - 1)
                    if small:
                        b = i + s // H
                        row = mask16[:, b, :, :] if isinstance(b, int) else mask16[:, bass.ds(b, 1), :, :].rearrange("p o t s -> p (o t) s")
                        pe.matmul(s_ps[q][:, :, :], ident16[:, :], row if rotary else row.broadcast_to([P, TB, S]), start=True, stop=False,
                                  skip_group_check=True)
                    for t in range(TB):
                        if small:
                            r = 64 * (h % 2)
                            mm = pe.matmul(s_ps[q][:, t, :], QT[r:r + 64, h // 2, t * P:(t + 1) * P], KT[r:r + 64, h // 2, :], start=False, stop=True,
                                           skip_group_check=True)
                        else:
                            mm = mm3(pe, s_ps[q][:, t, :], [a[:, h, t * P:(t + 1) * P] for a in QT], [a[:, h // 2, :] for a in KT], True, True)
                    mm.then_inc(s_ready, 1)

                def turn_p(i, lo, s):
                    wait(pe, n_done, i, lo, H, s + 1)
                    wait(pe, pl_done, i, lo, H, s - 1)
                    for kc in range(KC):
                        for t in range(TB):
                            mm = pe.transpose(t_ps[s % 2][:, kc, t * P:(t + 1) * P], p_sb[s % 4][:, t, kc * P:(kc + 1) * P], ident[:, :])
                    mm.then_inc(t_ready, 1)

                def values(i, lo, s, last=False):
                    h = s % H
                    g = h // GH
                    if h % GH == 0:
                        wait(pe, ol_done, i, lo, NGR, (s // H) * NGR + g - 1)
                        if g == 1:
                            wait(pe, x_done, i, lo, 1, s // H)
                    wait(pe, pl_done, i, lo, H, s + 1)
                    if small:
                        if h == 0 or h == 8:
                            wait(pe, vh_done, i, lo, 2, 2 * (s // H) + 1 + h // 8)
                        out = o_ps[g % 2][:, 0:S]
                        for kc in range(KC):
                            for e in range(2):
                                mm = pe.matmul(out, vp[:, kc, h // 4, P * (h % 4):P * (h % 4) + P], pT[e][s % 4][:, kc, :], start=(h % GH == 0 and kc == 0 and e == 0),
                                               stop=(h % GH == GH - 1 and kc == KC - 1 and e == 1))
                    else:
                        if h == 0:
                            wait(pe, rd_done, i, lo, NRD, PRO + (s // H - 1) * NRD + done_by("V0", 1))
                        if h == 8:
                            wait(pe, rd_done, i, lo, NRD, PRO + (s // H) * NRD + 1 + [r[1:] for r in body_rounds(last)].index(("V1", 1)))
                        out = o_ps[g % 2][:, (h % 2) * S:(h % 2 + 1) * S]
                        for kc in range(KC):
                            mm = mm3(pe, out, [a[:, kc, (h // 2) * P:(h // 2 + 1) * P] for a in V], [a[s % 4][:, kc, :] for a in pT],
                                     kc == 0, kc == KC - 1)
                    mm.then_inc(pv_done, 1)

                def project(i, lo, nxt):
                    wait(pe, ol_done, i, lo, NGR, (nxt + 1) * NGR)
                    out = o_ps[1][:, :].rearrange("p (t d) -> p t d", t=TB)
                    for t in range(TB):
                        for c in range(OC):
                            mm = mm3(pe, out[:, t, :], [a[:, c, t * P:(t + 1) * P] for a in OT], [a[:, c, :] for a in wo], c == 0, c == OC - 1)
                    mm.then_inc(out_ready, 1)

                def round_(i, lo, a, pos, kind, part):
                    bank = r_ps[pos % 2]
                    wait(pe, rd_done, i, lo, NRD, a + pos - 1)
                    own = kind == "V1"
                    batch = (a - PRO) // NRD + (0 if own else 1)
                    if kind == "nT":
                        wait(pe, n_ready, i, lo, 1, batch + 1)
                        if small:
                            for k in range(KC):
                                for t in range(TB):
                                    mm = pe.transpose(bank[:, k * S + t * P:k * S + (t + 1) * P], n_sb[:, t, k * P:(k + 1) * P], ident[:, :])
                        else:
                            for t in range(TB):
                                mm = pe.transpose(bank[:, t * P:(t + 1) * P], n_sb[:, t, part * P:(part + 1) * P], ident[:, :])
                    elif small and kind in ("q", "k", "v"):
                        src, w = (nT, wq) if kind == "q" else (cT, wk if kind == "k" else wv)
                        if kind == "q":
                            wait(pe, rd_done, i, lo, NRD, a + pos - (done_by("q") - done_by("nT")) + 1)
                        if kind == "v":
                            wait(pe, c_in, i, lo, 32, 32 * (batch + 1))
                        for t in range(TB):
                            for k in range(KC):
                                mm = mm3(pe, bank[:, t * D:(t + 1) * D], [y[:, k, t * P:(t + 1) * P] for y in src], [y[:, k, :] for y in w],
                                         k == 0, k == KC - 1)
                    elif small:
                        src = qs if kind == "qT" else ks
                        if part == 0:
                            back = done_by(kind, 0) - done_by("q" if kind == "qT" else "k")
                            wait(pe, rd_done, i, lo, NRD, a + pos - back + 1)
                        flat = src[:, :, :, :].rearrange("p (t h) g d -> p t (h g d)", t=TB)
                        for c in range(2):
                            for t in range(TB):
                                mm = pe.transpose(bank[:, c * S + t * P:c * S + (t + 1) * P].bitcast(F32R),
                                                  flat[:, t, (2 * part + c) * P:(2 * part + c + 1) * P], identr[:, :])
                    elif kind in ("qT", "kT"):
                        src, w = (nT, wq) if kind == "qT" else (cT, wk)
                        if kind == "qT" and part == 0:
                            wait(pe, rd_done, i, lo, NRD, a + pos - (done_by("qT") - done_by("nT", 1)) + 1)
                        if kind == "kT" and part == 0:
                            wait(pe, c_in, i, lo, 32, 32 * (batch + 1))
                        for c in range(2):
                            for k in range(KC):
                                col = (2 * part + c) * P
                                mm = mm3(pe, bank[:, c * S:(c + 1) * S], [y[:, k, col:col + P] for y in w], [y[:, k, :] for y in src],
                                         k == 0, k == KC - 1)
                    else:
                        half = 512 * (kind == "V1")
                        for k in range(KC):
                            mm = mm3(pe, bank[:, :], [y[:, k, part * P:(part + 1) * P] for y in cT], [y[:, k, half:half + 512] for y in wv],
                                     k == 0, k == KC - 1)
                    mm.then_inc(rd_ready, 1)

                for pos, (_, kind, part) in enumerate(ROUNDS):
                    round_(0, 0, 0, pos, kind, part)
                for s in range(LEAD):
                    scores(0, 0, s)

                def body(i, lo, hi):
                    last = hi == B - 1
                    for h in range(H):
                        if not (last and h + LEAD >= H):
                            scores(i, lo, h + LEAD)
                        turn_p(i, lo, h)
                        for pos, kind, part in rounds_at(h, last):
                            round_(i, lo, PRO, pos, kind, part)
                        if not (lo == 0 and h < 2):
                            values(i, lo, h - 2, last)
                        if h == 2 and lo > 0:
                            project(i, lo, -1)

                run_loop(pe, B, CUTS, body)
                values(B - 1, B - 1, H - 2, True)
                values(B - 1, B - 1, H - 1, True)
                project(B - 1, B - 1, 0)

            @block.scalar
            def _(act):
                def weights_of(i, lo, s):
                    wait(act, m_ready, i, lo, H, s + 1)
                    wait(act, t_ready, i, lo, H, s - 3)
                    src = s_ps[s % 2]
                    for t in range(TB):
                        ins = act.activation(p_sb[s % 4][:, t, :], src[:, t, :], ACT.Exp, bias=nm[:, s % 4, t:t + 1], scale=-1.0,
                                             accum_out=rs[:, s % 4, t:t + 1])
                    ins.then_inc(e_done, 1)

                def p_hi(i, lo, s):
                    wait(act, t_ready, i, lo, H, s + 1)
                    wait(act, pv_done, i, lo, H, s - 3)
                    act.activation(pT[0][s % 4][:, :, :], t_ps[s % 2][:, :, :], ACT.Copy).then_inc(ph_done, 1)

                def o_hi(i, lo, turn, g):
                    wait(act, pv_done, i, lo, H, turn * H + (g + 1) * GH)
                    if g == 0:
                        wait(act, out_ready, i, lo, 1, turn)
                    if small:
                        ins = act.activation(OT[0][:, g, :], o_ps[g % 2][:, 0:S], ACT.Copy)
                    else:
                        for e in range(2):
                            ins = act.activation(OT[0][64 * e:64 * e + 64, g, :], o_ps[g % 2][64 * e:64 * e + 64, e * S:(e + 1) * S], ACT.Copy)
                    ins.then_inc(oh_done, 1)

                def round_(i, lo, a, pos, kind, part):
                    bank = r_ps[pos % 2]
                    both = lambda y: y[:, :].rearrange("p (c s) -> p c s", c=2)
                    batch = (a - PRO) // NRD + (0 if kind == "V1" else 1)
                    if small and kind in ("q", "k"):
                        wait(act, f_ready, i, lo, 3, 3 * batch + 1 + ("q", "v", "k").index(kind))
                        src, dst = (qf, qs) if kind == "q" else (kf, ks)
                        wait(act, rd_ready, i, lo, NRD, a + pos + 1)
                        src4 = src[:, :, :].rearrange("p t (h o d) -> p (t h) o d", o=1, d=dh).broadcast_to([P, TB * H, 2, dh])
                        out = dst[:, :, 0:2, :] if kind == "q" else dst[:, :, 0:3:2, :]
                        act.activation(out, src4, ACT.Copy).then_inc(rd_hi, 1)
                        return
                    wait(act, rd_ready, i, lo, NRD, a + pos + 1)
                    if small and kind == "v":
                        wait(act, vh_done, i, lo, 2, 2 * batch)
                        act.activation(vf[:, :, :], both(bank), ACT.Copy).then_inc(rd_hi, 1)
                    elif kind == "nT":
                        if small:
                            act.activation(nT[0][:, :, :], both(bank), ACT.Copy).then_inc(rd_hi, 1)
                        else:
                            act.activation(nT[0][:, part, :], bank[:, 0:S], ACT.Copy).then_inc(rd_hi, 1)
                    elif small:
                        wait(act, s_ready, i, lo, H, H * batch - H + 4 * part + 4)
                        dst = QT if kind == "qT" else KT
                        act.activation(dst[:, 2 * part, :], bank[:, 0:S], ACT.Copy).then_inc(rd_hi, 1)
                    elif kind == "qT":
                        wait(act, s_ready, i, lo, H, H * batch - H + 4 * part + 4)
                        for e in range(2):
                            ins = act.activation(QT[0][64 * e:64 * e + 64, 4 * part + e:4 * part + 4:2, :], both(bank)[64 * e:64 * e + 64], ACT.Copy,
                                                 scale=-scale)
                        ins.then_inc(rd_hi, 1)
                    elif kind == "kT":
                        wait(act, s_ready, i, lo, H, H * batch - H + 4 * part + 4)
                        act.activation(KT[0][:, 2 * part:2 * part + 2, :], both(bank), ACT.Copy).then_inc(rd_hi, 1)
                    else:
                        half = 512 * (kind == "V1")
                        wait(act, pv_done, i, lo, H, H * batch - H + (16 if half else 8))
                        act.activation(V[0][:, part, half:half + 512], bank[:, :], ACT.Copy).then_inc(rd_hi, 1)

                def v_hi(i, lo, turn, half):
                    wait(act, f_ready, i, lo, 3, 3 * turn + 2)
                    wait(act, pv_done, i, lo, H, H * turn - H + 8 * half + 8)
                    for kc in range(KC):
                        ins = act.activation(v_cols(kc, half, 0), vf_cols(kc, half), ACT.Copy)
                    ins.then_inc(v_half, 1)

                for pos, (_, kind, part) in enumerate(ROUNDS):
                    round_(0, 0, 0, pos, kind, part)
                if small:
                    v_hi(0, 0, 0, 0)
                for s in range(LEAD - 1):
                    weights_of(0, 0, s)

                def body(i, lo, hi):
                    last = hi == B - 1
                    for h in range(H):
                        if not (last and h + 2 >= H):
                            weights_of(i, lo, h + 2)
                        p_hi(i, lo, h)
                        if h == 1 and lo > 0:
                            o_hi(i, lo, -1, NGR - 1)
                        if h > 1 and h % GH == 1:
                            o_hi(i, lo, 0, h // GH - 1)
                        for pos, kind, part in rounds_at(h, last):
                            round_(i, lo, PRO, pos, kind, part)
                        if small and h == 2:
                            v_hi(i, lo, 0, 1)
                        if small and h == 10 and not last:
                            v_hi(i, lo, 1, 0)

                run_loop(act, B, CUTS, body)
                o_hi(B - 1, B - 1, 0, NGR - 1)

            @block.vector
            def _(v):
                def max_of(i, lo, s):
                    wait(v, e_done, i, lo, H, s - 1)
                    wait(v, s_ready, i, lo, H, s + 1)
                    v.tensor_reduce(nm[:, s % 4, :], s_ps[s % 2][:, :, :], AX.X, ALU.min).then_inc(m_ready, 1)

                def inverse(i, lo, s):
                    wait(v, e_done, i, lo, H, s + 1)
                    v.reciprocal(ri[:, s % 4, :], rs[:, s % 4, :]).then_inc(r_done, 1)

                def p_lo(i, lo, s):
                    wait(v, ph_done, i, lo, H, s + 1)
                    v.tensor_tensor(pT[1][s % 4][:, :, :], t_ps[s % 2][:, :, :], pT[0][s % 4][:, :, :].bitcast(F32), ALU.subtract).then_inc(pl_done, 1)

                def o_lo(i, lo, turn, g):
                    wait(v, oh_done, i, lo, NGR, turn * NGR + g + 1)
                    if small:
                        ins = v.tensor_tensor(OT[1][:, g, :], o_ps[g % 2][:, 0:S], OT[0][:, g, :].bitcast(F32), ALU.subtract)
                    else:
                        for e in range(2):
                            r = slice(64 * e, 64 * e + 64)
                            ins = v.tensor_tensor(OT[1][r, g, :], o_ps[g % 2][r, e * S:(e + 1) * S], OT[0][r, g, :].bitcast(F32), ALU.subtract)
                    ins.then_inc(ol_done, 1)

                def residual(i, lo, turn):
                    wait(v, out_ready, i, lo, 1, turn + 1)
                    out = o_ps[1][:, :].rearrange("p (t d) -> p t d", t=TB)
                    v.scalar_tensor_tensor(x_of(i, turn), out, tg[:, 0:1], x_of(i, turn), ALU.mult, ALU.add).then_inc(x_done, 1)

                def rotate(f):
                    half = lambda y, e: y[:, :, :].rearrange("p t (h e d) -> p t h e d", e=2, d=8)[:, :, :, e, :]
                    tab = lambda j, n: cs[:, :, j, :].rearrange("p t (o d) -> p t o d", o=1).broadcast_to([P, TB, n, 8])
                    v.tensor_tensor(r1[:, :, :].rearrange("p t (h d) -> p t h d", d=8), f[:, :, :].rearrange("p t (h d) -> p t h d", d=8), tab(0, 32), ALU.mult)
                    v.tensor_tensor(half(r2, 0), half(f, 1), tab(1, 16), ALU.mult)
                    v.tensor_tensor(half(r2, 1), half(f, 0), tab(2, 16), ALU.mult)
                    v.drain()
                    v.tensor_tensor(f[:, :, :], r1[:, :, :], r2[:, :, :], ALU.add)

                def round_(i, lo, a, pos, kind, part):
                    bank = r_ps[pos % 2]
                    both = bank[:, :].rearrange("p (c s) -> p c s", c=2)
                    if small and kind == "v":
                        wait(v, rd_hi, i, lo, NRD, a + pos + 1)
                        v.tensor_tensor(vf[:, :, :], vf[:, :, :], bc_t(b3[:, 2, :], D), ALU.add)
                        v.drain().then_inc(f_ready, 1)
                        v.drain().then_inc(rd_done, 1)
                        return
                    if small and kind in ("q", "k"):
                        wait(v, rd_ready, i, lo, NRD, a + pos + 1)
                        f = {"q": qf, "k": kf}[kind]
                        j = ("q", "k").index(kind)
                        v.scalar_tensor_tensor(f[:, :, :], both, -scale if kind == "q" else 1.0, bc_t(b3[:, j, :], D), ALU.mult, ALU.add)
                        v.drain()
                        if rotary:
                            rotate(f)
                            v.drain()
                            if kind == "q":
                                b = TB * (i + (a - PRO) // NRD + 1)
                                some = kq[:, b:b + TB] if isinstance(b, int) else kq[:, bass.ds(b, TB)]
                                v.tensor_tensor(f[:, :, :], f[:, :, :], some.rearrange("p (t o) -> p t o", o=1).broadcast_to([P, TB, D]), ALU.mult)
                                v.drain()
                        v.drain().then_inc(f_ready, 1)
                        return
                    wait(v, rd_hi, i, lo, NRD, a + pos + 1)
                    if kind == "nT":
                        if small:
                            v.tensor_tensor(nT[1][:, :, :], both, nT[0][:, :, :].bitcast(F32), ALU.subtract).then_inc(rd_done, 1)
                        else:
                            v.tensor_tensor(nT[1][:, part, :], bank[:, 0:S], nT[0][:, part, :].bitcast(F32), ALU.subtract).then_inc(rd_done, 1)
                    elif small:
                        dst = QT if kind == "qT" else KT
                        v.tensor_copy(dst[:, 2 * part + 1, :], bank[:, S:2 * S]).then_inc(rd_done, 1)
                    elif kind == "qT":
                        for e in range(2):
                            r = slice(64 * e, 64 * e + 64)
                            heads = slice(4 * part + e, 4 * part + 4, 2)
                            ins = v.scalar_tensor_tensor(QT[1][r, heads, :], both[r], -scale, QT[0][r, heads, :].bitcast(F32), ALU.mult, ALU.subtract)
                        ins.then_inc(rd_done, 1)
                    elif kind == "kT":
                        v.tensor_tensor(KT[1][:, 2 * part:2 * part + 2, :], both, KT[0][:, 2 * part:2 * part + 2, :].bitcast(F32), ALU.subtract).then_inc(rd_done, 1)
                    else:
                        half = 512 * (kind == "V1")
                        v.tensor_tensor(V[1][:, part, half:half + 512], bank[:, :], V[0][:, part, half:half + 512].bitcast(F32), ALU.subtract).then_inc(rd_done, 1)

                def laid_lo(i, lo, a, pos, kind):
                    wait(v, rd_hi, i, lo, NRD, a + pos + 1)
                    f, dst = (qf, qs) if kind == "q" else (kf, ks)
                    src4 = f[:, :, :].rearrange("p t (h o d) -> p (t h) o d", o=1, d=dh).broadcast_to([P, TB * H, 2, dh])
                    hi_, lo_ = (dst[:, :, 0:2, :], dst[:, :, 2:4, :]) if kind == "q" else (dst[:, :, 0:3:2, :], dst[:, :, 1:4:2, :])
                    v.tensor_tensor(lo_, src4, hi_.bitcast(F32), ALU.subtract).then_inc(rd_done, 1)

                def v_lo(i, lo, turn, half):
                    wait(v, v_half, i, lo, 2, 2 * turn + half + 1)
                    for kc in range(KC):
                        ins = v.tensor_tensor(v_cols(kc, half, 1), vf_cols(kc, half), v_cols(kc, half, 0).bitcast(F32), ALU.subtract)
                    ins.then_inc(vh_done, 1)

                for pos, (_, kind, part) in enumerate(ROUNDS):
                    round_(0, 0, 0, pos, kind, part)
                    if small and kind in ("q", "k"):
                        laid_lo(0, 0, 0, pos, kind)
                if small:
                    v_lo(0, 0, 0, 0)
                for s in range(LEAD):
                    max_of(0, 0, s)
                for s in range(LEAD - 1):
                    inverse(0, 0, s)

                def body(i, lo, hi):
                    last = hi == B - 1
                    for h in range(H):
                        if not (last and h + LEAD >= H):
                            max_of(i, lo, h + LEAD)
                        p_lo(i, lo, h)
                        if h == 1 and lo > 0:
                            o_lo(i, lo, -1, NGR - 1)
                        if h > 1 and h % GH == 1:
                            o_lo(i, lo, 0, h // GH - 1)
                        if not (last and h + 2 >= H):
                            inverse(i, lo, h + 2)
                        for pos, kind, part in rounds_at(h - 1, last) if small and h else []:
                            if kind in ("q", "k"):
                                laid_lo(i, lo, PRO, pos, kind)
                        for pos, kind, part in rounds_at(h, last):
                            round_(i, lo, PRO, pos, kind, part)
                        if small and h == 2:
                            v_lo(i, lo, 0, 1)
                        if small and h == 10 and not last:
                            v_lo(i, lo, 1, 0)
                        if h == 3 and lo > 0:
                            residual(i, lo, -1)

                run_loop(v, B, CUTS, body)
                o_lo(B - 1, B - 1, 0, NGR - 1)
                residual(B - 1, B - 1, 0)

            @block.gpsimd
            def _(pool):
                def normalize(i, lo, s):
                    wait(pool, r_done, i, lo, H, s + 1)
                    pool.tensor_tensor(p_sb[s % 4][:, :, :], p_sb[s % 4][:, :, :],
                                       ri[:, s % 4, :].rearrange("p (t o) -> p t o", o=1).broadcast_to([P, TB, S]), ALU.mult).then_inc(n_done, 1)

                def per_row(y, q, b):
                    at = TB * b
                    cols = y[q][:, at:at + TB] if isinstance(b, int) else y[q][:, bass.ds(at, TB)]
                    return cols.rearrange("p (t o) -> p t o", o=1).broadcast_to([P, TB, D])

                def norm(i, lo, turn):
                    if not (isinstance(i, int) and i + turn == 0):
                        wait(pool, rd_ready, i, lo, NRD, PRO + (turn - 2) * NRD + done_by("nT", 0 if small else 1))
                    n = n_sb[:, :, :]
                    src = x_of(i, turn)
                    for q in range(len(nmean)):
                        pool.tensor_tensor(n, src, per_row(nmean, q, i + turn), ALU.add)
                        pool.drain()
                        pool.tensor_tensor(n, n, per_row(rstd, q, i + turn), ALU.mult)
                        pool.drain()
                        src = n
                    if inner:
                        pool.tensor_tensor(n, n, bc_t(gb[:, 0, :], D), ALU.mult)
                        pool.drain()
                        pool.tensor_tensor(n, n, bc_t(gb[:, 1, :], D), ALU.add)
                    pool.drain().then_inc(n_ready, 1)

                def add_bias(i, lo, turn):
                    wait(pool, x_done, i, lo, 1, turn + 1)
                    pool.tensor_tensor(x_of(i, turn), x_of(i, turn), bc_t(bo[:, :], D), ALU.add)

                norm(0, 0, 0)
                for s in range(LEAD - 1):
                    normalize(0, 0, s)

                def body(i, lo, hi):
                    for h in range(H):
                        if not (hi == B - 1 and h + 2 >= H):
                            normalize(i, lo, h + 2)
                        if h == 0 and hi < B - 1:
                            norm(i, lo, 1)
                        if h == 5 and lo > 0:
                            add_bias(i, lo, -1)

                run_loop(pool, B, CUTS, body)
                add_bias(B - 1, B - 1, 0)


def attention_layer(nc, G, I, layer):
    if layer == 0:
        single_phase(nc, G, I, "att0", {n: I["L0_xattn_" + n] for n in ("Wq", "Wk", "Wv", "Wcq", "Wck", "Wcv", "W1")},
                     (I["L0_xattn_gamma"], I["L0_xattn_beta"], I["L0_xattn_b1"]))
    if layer == 1:
        heads_phase(nc, G, I, "att1", 1, 16, {"q": I["L1_Wq"], "k": I["L1_Wk"], "v": I["L1_Wv"], "o": I["L1_Wo"], "bo": I["L1_xattn_bo"]},
                    mask=I["mask_BxS2_if1"], rotary=True, biases=(I["L1_bq"], I["L1_bk"], I["L1_bv"]))
    if layer == 2:
        heads_phase(nc, G, I, "att2", 2, 16, {"q": I["L2_xattn_Wq"], "k": I["L2_xattn_Wk"], "v": I["L2_xattn_Wv"], "o": I["L2_Wo"],
                                              "bo": I["L2_xattn_bo"]},
                    mask=I["mask2"], biases=(I["L2_xattn_bq"], I["L2_xattn_bk"], I["L2_xattn_bv"]))
    if layer == 3:
        heads_phase(nc, G, I, "att3", 3, 64, {"q": I["L3_xattn_w_q"], "k": I["L3_w_k"], "v": I["L3_w_v"], "o": I["L3_xattn_w_out"],
                                              "bo": I["L3_xattn_b_out"]},
                    inner=(I["L3_xattn_ln_gamma"], I["L3_xattn_ln_beta"]), gate=I["L3_xattn_gate"])


def single_phase(nc, G, I, name, weights, rows):
    NU, NT = 2, 4
    NI = T // (NU * NT)
    C = NT * P
    scale = -1.0 / 16.0
    W = {"Wq": 0, "Wk": 1, "Wv": 2, "Wcq": 3, "Wck": 4, "Wcv": 5, "W1": 6}
    PRODUCTS = ["nT", "QT", "KT", "V", "S", "cKT", "pT", "A", "cV", "hT", "cQT", "cS", "cpT", "cA", "h2T", "F"]
    NP = len(PRODUCTS)
    at = PRODUCTS.index
    SPLIT = [p for p in PRODUCTS if p not in ("S", "A", "cS", "cA", "F")]
    ROWS = {"nT": 1, "hT": 2, "h2T": 3}

    with ExitStack() as ctx:
        A = Alloc(nc, ctx, name)
        sb, sem = A.sb, A.sem
        hl = lambda n, shape: [sb(f"{n}_{h}", shape, F32R) for h in ("hi", "lo")]
        x, ident, tg = G["x"], G["ident"], G["tanh_g"][:, 0:1]
        w_all = hl("w", [P, len(W), KC, D])
        jobs = []
        for wn, q in W.items():
            for k in range(KC):
                jobs.append((weights[wn][k * P:(k + 1) * P, :], w_all[0][:, q, k, :], w_all[1][:, q, k, :]))
        load_split(nc, name + "w", jobs, D)

        U = range(NU)
        per = lambda n, shape: [sb(f"{n}{u}", shape) for u in U]
        hl_u = lambda n: [hl(f"{n}{u}", [P, 2, 512]) for u in U]
        n_sb, p_sb, a_sb, h_sb, s_m = (per(n, [P, NT, D]) for n in ("n", "p", "a", "h", "s_m"))
        xT, QT, KT, V, pT, cT = (hl_u(n) for n in ("xT", "QT", "KT", "V", "pT", "cT"))
        nm, rs, ri = (per(n, [P, NT]) for n in ("nm", "rs", "ri"))
        st = [{"bn": sb(f"bn{u}", [P, 4, 6]), "mv": sb(f"mv{u}", [P, 4, 2]), "rstd": sb(f"rstd{u}", [P, 4]), "tmp": sb(f"tmp{u}", [P, 4])} for u in U]
        gamma, beta, b1 = (sb(n, [P, D]) for n in ("gamma", "beta", "b1"))
        causal = sb("causal", [P, TB, S])
        met = sb("met", [P, NU])
        ps = [[A.ps(f"ps{u}{q}", [P, 2, 512]) for q in range(2)] for u in U]
        per_sem = lambda n: [sem(f"{n}{u}") for u in U]
        product, hi_done, used, rows_ready, m_ready, e_ready, c_in, gated, unit_free = (
            per_sem(n) for n in ("product", "hi_done", "used", "rows_ready", "m_ready", "e_ready", "c_in", "gated", "unit_free"))
        loaded, zeroed = sem("loaded"), sem("zeroed")
        zeros = sb("zeros", [P, 4, D])

        rows4 = lambda y: y.rearrange("p a (b n) -> p (a b) n", n=D)
        dest = {"nT": xT, "hT": xT, "h2T": xT, "QT": QT, "cQT": QT, "KT": KT, "cKT": KT, "V": V, "cV": V, "pT": pT, "cpT": pT}

        def bank(u, name):
            return ps[u][at(name) % 2]

        def x_of(i, u):
            return x[:, bass.ds(i * (NU * NT) + u * NT, NT), :]

        with nc.Block() as block:
            @block.sync
            def _(sp):
                for dst, src in zip((gamma, beta, b1), rows):
                    sp.dma_start(dst[:, :], src.rearrange("(a d) -> a d", a=1).broadcast_to([P, D])).then_inc(loaded, 16)
                sp.dma_start(causal[:, :, :], I["causal"]).then_inc(loaded, 16)
                sp.wait_ge(loaded, 64)

            @block.gpsimd
            def _(pool):
                pool.memset(zeros[:, :, :], 0.0)
                for u in U:
                    pool.nop().then_inc(unit_free[u], 1)

        with nc.Block() as block:
            @block.sync
            def _(sp):
                with sp.Fori(0, NI) as i:
                    for u in U:
                        srcs = [[G["ctxT"][h][bass.ds(sp.snap(i * (2 * NU) + 2 * u + b), 1)].rearrange("o p k s -> (o p) k s") for b in range(2)]
                                for h in range(2)]
                        sp.wait_ge(unit_free[u], i + 1)
                        for b in range(2):
                            for h in range(2):
                                sp.dma_start(cT[u][h][:, :, b * S:(b + 1) * S].bitcast(F32), srcs[h][b]).then_inc(c_in[u], 16)
                for r in range(0, XROWS, 512):
                    sp.dma_start(G["rows_x"][r:r + 512, :].rearrange("(p t) d -> p t d", p=P), zeros[:, :, :]).then_inc(zeroed, 16)
                sp.wait_ge(zeroed, 16 * len(range(0, XROWS, 512)))

            @block.tensor
            def _(pe):
                def turn_rows(i, u, name, rows):
                    for k in range(2):
                        for t in range(NT):
                            mm = pe.transpose(bank(u, name)[:, k, t * P:(t + 1) * P], rows[u][:, t, k * P:(k + 1) * P], ident[:, :])
                    return mm

                def features(i, u, name, src, w):
                    for c in range(2):
                        for k in range(KC):
                            mm = mm3(pe, bank(u, name)[:, c, :], [y[:, W[w], k, c * P:(c + 1) * P] for y in w_all],
                                     [y[:, k, :] for y in src[u]], k == 0, k == KC - 1)
                    return mm

                def tokens(i, u, name, src, moving):
                    out = rows4(bank(u, name)[:, :, :])
                    for t in range(NT):
                        for k in range(KC):
                            mm = mm3(pe, out[:, t, :], [y[:, k, t * P:(t + 1) * P] for y in src[u]], moving(u, t, k), k == 0, k == KC - 1)
                    return mm

                weight = lambda w: (lambda u, t, k: [y[:, W[w], k, :] for y in w_all])
                keys = lambda u, t, k: [y[:, k, (t // TB) * S:(t // TB + 1) * S] for y in KT[u]]
                vals = lambda u, t, k: [rows4(y[:, :, :])[:, (t // TB) * TB + k, :] for y in V[u]]

                with pe.Fori(0, NI) as i:
                    def before(u, name, operand):
                        need = max(at(operand) + 1 if operand else 0, at(name) - 1)
                        if need > 0:
                            pe.wait_ge(used[u], i * NP + need)

                    for name in PRODUCTS:
                        for u in U:
                            if name == "nT":
                                before(u, name, None)
                                pe.wait_ge(rows_ready[u], i * 3 + 1)
                                mm = turn_rows(i, u, name, n_sb)
                            elif name in ("hT", "h2T"):
                                before(u, name, None)
                                pe.wait_ge(rows_ready[u], i * 3 + ROWS[name])
                                mm = turn_rows(i, u, name, h_sb if name == "hT" else n_sb)
                            elif name in ("pT", "cpT"):
                                before(u, name, None)
                                pe.wait_ge(e_ready[u], i * 2 + (1 if name == "pT" else 2))
                                mm = turn_rows(i, u, name, p_sb)
                            elif name in ("QT", "KT"):
                                before(u, name, "nT")
                                mm = features(i, u, name, xT, {"QT": "Wq", "KT": "Wk"}[name])
                            elif name == "V":
                                before(u, name, "nT")
                                mm = tokens(i, u, name, xT, weight("Wv"))
                            elif name in ("S", "cS"):
                                before(u, name, "KT" if name == "S" else "cQT")
                                mm = tokens(i, u, name, QT, keys)
                            elif name == "cKT":
                                before(u, name, None)
                                pe.wait_ge(c_in[u], i * 64 + 64)
                                mm = features(i, u, name, cT, "Wck")
                            elif name in ("A", "cA"):
                                before(u, name, "pT" if name == "A" else "cpT")
                                mm = tokens(i, u, name, pT, vals)
                            elif name == "cV":
                                before(u, name, None)
                                mm = tokens(i, u, name, cT, weight("Wcv"))
                            elif name == "cQT":
                                before(u, name, "hT")
                                mm = features(i, u, name, xT, "Wcq")
                            else:
                                before(u, name, "h2T")
                                mm = tokens(i, u, name, xT, weight("W1"))
                            mm.then_inc(product[u], 1)

            @block.scalar
            def _(act):
                with act.Fori(0, NI) as i:
                    for name in PRODUCTS:
                        for u in U:
                            if name in SPLIT:
                                act.wait_ge(product[u], i * NP + at(name) + 1)
                                act.activation(dest[name][u][0][:, :, :], bank(u, name)[:, :, :], ACT.Copy,
                                               scale=scale if name in ("QT", "cQT") else 1.0).then_inc(hi_done[u], 1)
                            elif name in ("S", "cS"):
                                act.wait_ge(m_ready[u], i * 2 + (1 if name == "S" else 2))
                                src = s_m[u] if name == "S" else rows4(bank(u, name)[:, :, :])
                                for t in range(NT):
                                    ins = act.activation(p_sb[u][:, t, :], src[:, t, :], ACT.Exp, bias=nm[u][:, t:t + 1], scale=-1.0,
                                                         accum_out=rs[u][:, t:t + 1])
                                ins.then_inc(e_ready[u], 1)

            @block.vector
            def _(v):
                def norm(u, dst, src):
                    s = st[u]
                    for t in range(NT):
                        v.bn_stats(s["bn"][:, t, :], src[:, t, :])
                    v.drain()
                    for t in range(NT):
                        v.bn_aggr(s["mv"][:, t, :], s["bn"][:, t, :])
                    v.drain()
                    rsqrt(v, s["rstd"][:, :], s["mv"][:, :, 1], s["tmp"][:, :], 1e-3)
                    for t in range(NT):
                        v.scalar_tensor_tensor(src[:, t, :], src[:, t, :], s["mv"][:, t, 0:1], gamma[:, :], ALU.subtract, ALU.mult)
                    v.drain()
                    for t in range(NT):
                        ins = v.scalar_tensor_tensor(dst[:, t, :], src[:, t, :], s["rstd"][:, t:t + 1], beta[:, :], ALU.mult, ALU.add)
                    return ins

                with v.Fori(0, NI) as i:
                    split = [p for p in SPLIT]
                    for u in U:
                        v.wait_ge(unit_free[u], i + 1)
                        v.tensor_copy(met[:, u:u + 1], tg)
                        layer_norm(v, n_sb[u][:, :, :], x_of(i, u), st[u], NT, 1e-5)
                        v.drain().then_inc(rows_ready[u], 1)
                    for name in PRODUCTS:
                        for u in U:
                            src = bank(u, name)
                            tiles = rows4(src[:, :, :])
                            if name in SPLIT:
                                v.wait_ge(hi_done[u], i * len(SPLIT) + split.index(name) + 1)
                                hi_, lo_ = (y[:, :, :] for y in dest[name][u])
                                if name in ("QT", "cQT"):
                                    ins = v.scalar_tensor_tensor(lo_, src[:, :, :], scale, hi_.bitcast(F32), ALU.mult, ALU.subtract)
                                else:
                                    ins = v.tensor_tensor(lo_, src[:, :, :], hi_.bitcast(F32), ALU.subtract)
                                ins.then_inc(used[u], 1)
                                continue
                            v.wait_ge(product[u], i * NP + at(name) + 1)
                            if name == "S":
                                v.tensor_copy(met[:, u:u + 1], tg)
                                for t in range(NT):
                                    ins = v.tensor_tensor_reduce(out=s_m[u][:, t, :], in0=tiles[:, t, :], in1=causal[:, t % TB, :], scale=1.0,
                                                                 scalar=BIG, op0=ALU.add, op1=ALU.min, accum_out=nm[u][:, t:t + 1])
                                ins.then_inc(m_ready[u], 1)
                                v.wait_ge(e_ready[u], i * 2 + 1)
                                v.reciprocal(ri[u][:, :], rs[u][:, :]).then_inc(used[u], 1)
                            elif name == "cS":
                                v.tensor_reduce(nm[u][:, :], tiles, AX.X, ALU.min).then_inc(m_ready[u], 1)
                                v.wait_ge(e_ready[u], i * 2 + 2)
                                v.reciprocal(ri[u][:, :], rs[u][:, :]).then_inc(used[u], 1)
                            elif name in ("A", "cA"):
                                base, out = (n_sb, h_sb) if name == "A" else (h_sb, n_sb)
                                for t in range(NT):
                                    ins = v.scalar_tensor_tensor(a_sb[u][:, t, :], tiles[:, t, :], ri[u][:, t:t + 1], base[u][:, t, :], ALU.mult, ALU.add)
                                ins.then_inc(used[u], 1)
                                v.drain()
                                norm(u, out[u], a_sb[u]).then_inc(rows_ready[u], 1)
                            else:
                                v.tensor_tensor(a_sb[u][:, :, :], tiles, b1[:, :].rearrange("p (o d) -> p o d", o=1).broadcast_to([P, NT, D]),
                                                ALU.add).then_inc(used[u], 1)
                                v.drain()
                                v.scalar_tensor_tensor(a_sb[u][:, :, :], a_sb[u][:, :, :], 0.0, n_sb[u][:, :, :], ALU.max, ALU.add)
                                v.drain()
                                norm(u, a_sb[u], a_sb[u])
                                v.drain()
                                v.tensor_scalar(a_sb[u][:, :, :], a_sb[u][:, :, :], 0.0, tg, ALU.max, ALU.mult).then_inc(gated[u], 1)

            @block.gpsimd
            def _(pool):
                with pool.Fori(0, NI) as i:
                    for u in U:
                        pool.wait_ge(gated[u], i + 1)
                        pool.tensor_tensor(x_of(i, u), x_of(i, u), a_sb[u][:, :, :], ALU.add).then_inc(unit_free[u], 1)



def build_program(nc, I, out):
    with ExitStack() as ctx:
        G = globals_of(nc, Alloc(nc, ctx, "g"))
        setup_phase(nc, G, I)
        for layer in range(4):
            attention_layer(nc, G, I, layer)
            moe_layer(nc, G, I, layer)
        final_phase(nc, G, out)


def kernel(**inputs):
    import concourse.bacc as bacc
    from concourse.bass_utils import run_bass_kernel_spmd

    nc = bacc.Bacc("TRN2", target_bir_lowering=False, num_devices=1)
    arrays = {f"in_{name}": np.ascontiguousarray(a) for name, a in lay_out(inputs).items()}
    I = {name[3:]: nc.dram_tensor(name, a.shape, mybir.dt.from_np(a.dtype), kind="ExternalInput").ap()
         for name, a in arrays.items()}
    out = nc.dram_tensor("out", (B, S, D), F32, kind="ExternalOutput").ap()
    build_program(nc, I, out)
    r = run_bass_kernel_spmd(nc, [arrays], core_ids=[0])
    return r.results[0]["out"]
```

```python
from contextlib import ExitStack

import numpy as np

import concourse.bass as bass
from concourse import mybir
from concourse.alu_op_type import AluOpType as ALU

F32 = mybir.dt.float32
F32R = mybir.dt.float32r
BF16 = mybir.dt.bfloat16
I32 = mybir.dt.int32
ACT = mybir.ActivationFunctionType
AX = mybir.AxisListType

P = 128
B = 8
S = 256
D = 256
N = B * S
T = N // P
KC = D // P
TB = S // P
BS = 256
BT = BS // P
XROWS = N + 40 * BS
BIG = 3.0e38


def wait(e, sem, i, lo, a, b):
    if isinstance(i, int):
        if i * a + b > 0:
            e.wait_ge(sem, i * a + b)
    else:
        assert lo * a + b > 0, (lo, a, b)
        e.wait_ge(sem, i * a + b)


def run_loop(e, n, cuts, body, start=0):
    edges = sorted({start, n, *[c for c in cuts if start < c < n]})
    for lo, end in zip(edges, edges[1:]):
        if end - lo == 1:
            body(lo, lo, lo)
        else:
            with e.Fori(lo, end) as i:
                body(i, lo, end - 1)


def rsqrt(v, y, var, tmp, eps):
    v.tensor_scalar(var, var, eps, None, ALU.add)
    v.drain()
    v.tensor_scalar(y.bitcast(I32), var.bitcast(I32), -0.5, float(0x5F3759DF), ALU.mult, ALU.add)
    v.drain()
    for _ in range(3):
        v.scalar_tensor_tensor(tmp, y, -0.5, y, ALU.mult, ALU.mult)
        v.drain()
        v.tensor_tensor(tmp, tmp, var, ALU.mult)
        v.drain()
        v.scalar_tensor_tensor(y, tmp, 1.5, y, ALU.add, ALU.mult)
        v.drain()


def layer_norm(v, dst, src, st, n, eps):
    for t in range(n):
        v.bn_stats(st["bn"][:, t, :], src[:, t, :])
    v.drain()
    for t in range(n):
        v.bn_aggr(st["mv"][:, t, :], st["bn"][:, t, :])
    v.drain()
    rsqrt(v, st["rstd"][:, 0:n], st["mv"][:, 0:n, 1], st["tmp"][:, 0:n], eps)
    for t in range(n):
        v.tensor_scalar(dst[:, t, :], src[:, t, :], st["mv"][:, t, 0:1], st["rstd"][:, t:t + 1],
                        ALU.subtract, ALU.mult)
    v.drain()


def mm3(pe, out, lhs, rhs, first, last, **kw):
    pe.matmul(out, lhs[0], rhs[0], start=first, stop=False, **kw)
    pe.matmul(out, lhs[0], rhs[1], start=False, stop=False, **kw)
    return pe.matmul(out, lhs[1], rhs[0], start=False, stop=last, **kw)


class Alloc:

    def __init__(self, nc, ctx, name):
        self.nc, self.ctx, self.name, self.sems = nc, ctx, name, []
        ctx.callback(self.close)

    def close(self):
        if self.sems:
            self.nc.clear_and_free_semaphores(self.sems)
            self.nc.all_engine_barrier()

    def sb(self, name, shape, dt=F32):
        return self.ctx.enter_context(self.nc.sbuf_tensor(f"{self.name}_{name}", shape, dt))

    def ps(self, name, shape, dt=F32):
        return self.ctx.enter_context(self.nc.psum_tensor(f"{self.name}_{name}", shape, dt))

    def sem(self, name):
        self.sems.append(self.nc.alloc_semaphore(f"{self.name}_{name}"))
        return self.sems[-1]



def moe_phase(nc, G, name, layer, E, K, FC, glu, func, shared, w_dram, rw_dram, rb_dram=None,
              biases=False, renorm=False, eps_sum=0.0, cap=None, clip=None, inner_norm=None, add_input=False,
              jobs=()):
    NB = (N * K + E * (BS - 1)) // BS
    SJ = N // BS if shared else 0
    JT = 4 if FC == 2 else 2
    NJ = SJ + NB
    NR = NB
    NI = -(-NJ // JT)
    JL = NJ - 1 - JT * (NI - 1)
    BASE = N if shared else 0
    ROWS = BASE + NR * BS
    W1 = (2 if glu else 1) * P
    WW = KC * W1 + D
    CW = WW + (1 + P if biases else 0)
    CI = JT * FC
    NS = max(FC, 8) if JT == 4 else FC
    LG = 1 if glu and FC > 6 else 2
    LA = LG + 2
    RG = 2 * LG
    TX = 2 if FC <= LG else 1
    per_slot = CI // NS
    assert CI % NS == 0 and ROWS <= XROWS
    rows_x, rows_y = G["rows_x"], G["rows_y"]
    x, ident = G["x"], G["ident"]
    tg = G["tanh_g"][:, 4 + layer:5 + layer]

    with ExitStack() as ctx:
        A = Alloc(nc, ctx, name)
        sb, ps, sem = A.sb, A.ps, A.sem
        n_all = sb("n_all", [P, T, D])
        p_k = [sb(f"p_{k}", [P, T]) for k in range(K)]
        slot_w = sb("slot_w", [P, T, K], I32)
        slot_r = sb("slot_r", [P, T, K], I32)
        blk = sb("blk", [P, NR], I32)

        with ExitStack() as c2:
            R = Alloc(nc, c2, name + "r")
            nT = R.sb("nT", [P, 2, KC, 512])
            bn, mv = R.sb("bn", [P, T, 6]), R.sb("mv", [P, T, 2])
            rstd, nb, tmp = (R.sb(n, [P, T]) for n in ("rstd", "nb", "tmp"))
            rw = R.sb("rw", [P, KC, E])
            lgT = R.sb("lgT", [P, 2, 512])
            lg, ex = R.sb("lg", [P, T, E]), R.sb("ex", [P, T, E])
            t1, t2 = R.sb("t1", [P, T, E]), R.sb("t2", [P, T, E])
            oh = [R.sb(f"oh{k}", [P, T, E]) for k in range(K)]
            m, r = R.sb("m", [P, T]), R.sb("r", [P, T])
            Mb = R.sb("Mb", [P, T, E], BF16)
            cnt, cnti = R.sb("cnt", [P, E]), R.sb("cnti", [P, E], I32)
            offs, ends = R.sb("offs", [P, E]), R.sb("ends", [P, E])
            tE = R.sb("tE", [P, E, E])
            tB, nblk = R.sb("tB", [P, NR, E]), R.sb("nblk", [P, NR])
            keep = R.sb("keep", [P, T])
            gb = None
            if inner_norm:
                gb = R.sb("gb", [P, 2, D])
            rb = R.sb("rb", [P, E]) if rb_dram is not None else None
            trp = [[R.ps(f"trp{q}{k}", [P, 512]) for k in range(KC)] for q in range(2)]
            lgp = [R.ps(f"lgp{q}", [P, 512]) for q in range(2)]
            small = R.ps("small", [P, 512])
            ltp, rank = (small[:, a:a + T * E].rearrange("p (t e) -> p t e", e=E) for a in (0, T * E))
            cntp = small[:, 2 * T * E:2 * T * E + E]
            loaded, stats, stats2, normed, scaled, n_ready, tr_ready, nT_ready = (R.sem(s) for s in (
                "loaded", "stats", "stats2", "normed", "scaled", "n_ready", "tr_ready", "nT_ready"))
            lg_ready, lgT_ready, lt_ready = (R.sem(s) for s in ("lg_ready", "lgT_ready", "lt_ready"))
            shifted, exped, mask_ready, rank_ready, rows_out = (R.sem(s) for s in ("shifted", "exped", "mask_ready", "rank_ready", "rows_out"))
            n_loads = 1 + 2 * bool(inner_norm) + (rb is not None)
            QT = T // 4

            with nc.Block() as block:
                @block.sync
                def _(sp):
                    sp.dma_start(rw[:, :, :], rw_dram).then_inc(loaded, 16)
                    if inner_norm:
                        for q in range(2):
                            sp.dma_start(gb[:, q, :], inner_norm[q].rearrange("(a d) -> a d", a=1).broadcast_to([P, D])).then_inc(loaded, 16)
                    if rb is not None:
                        sp.dma_start(rb[:, :], rb_dram.rearrange("(a d) -> a d", a=1).broadcast_to([P, E])).then_inc(loaded, 16)
                    for q in range(QT if shared else 0):
                        sp.wait_ge(n_ready, q + 1)
                        sp.dma_start(rows_x[512 * q:512 * (q + 1), :].rearrange("(t p) d -> p t d", p=P),
                                     n_all[:, 4 * q:4 * q + 4, :]).then_inc(rows_out, 16)
                    if shared:
                        sp.wait_ge(rows_out, 16 * QT)

                @block.scalar
                def _(act):
                    def apply(g, src, sem, done):
                        act.wait_ge(sem, g + 1)
                        for t in range(8 * g, 8 * g + 8):
                            ins = act.activation(n_all[:, t, :], src[:, t, :], ACT.Identity, scale=rstd[:, t:t + 1], bias=nb[:, t:t + 1])
                            if t % 4 == 3:
                                ins.then_inc(done, 1)

                    for g in range(2):
                        if inner_norm:
                            if g == 0:
                                apply(0, x, stats, normed)
                                apply(1, x, stats, normed)
                            apply(g, n_all, stats2, normed)
                        else:
                            apply(g, x, stats, n_ready)
                        for q in (2 * g, 2 * g + 1):
                            act.wait_ge(tr_ready, q + 1)
                            if q >= 2:
                                act.wait_ge(lg_ready, q - 1)
                            for k in range(KC):
                                ins = act.activation(nT[:, q % 2, k, :], trp[q % 2][k][:, :], ACT.Copy)
                            ins.then_inc(nT_ready, 1)
                        for q in (2 * g, 2 * g + 1):
                            act.wait_ge(lg_ready, q + 1)
                            if q >= 2:
                                act.wait_ge(lt_ready, q - 1)
                            act.activation(lgT[0:E, q % 2, :], lgp[q % 2][0:E, :], ACT.Copy).then_inc(lgT_ready, 1)
                    act.wait_ge(shifted, 1)
                    act.activation(ex[:, :, :], t1[:, :, :], ACT.Exp).then_inc(exped, 1)

                if inner_norm:
                    @block.gpsimd
                    def _(pool):
                        pool.wait_ge(loaded, 16 * n_loads)
                        for q in range(QT):
                            pool.wait_ge(scaled, q + 1)
                            blk4 = n_all[:, 4 * q:4 * q + 4, :]
                            pool.tensor_tensor(blk4, blk4, gb[:, 1, :].rearrange("p (o d) -> p o d", o=1).broadcast_to([P, 4, D]),
                                               ALU.add).then_inc(n_ready, 1)

                @block.tensor
                def _(pe):
                    def turn_rows(q):
                        pe.wait_ge(n_ready, q + 1)
                        if q >= 2:
                            pe.wait_ge(nT_ready, q - 1)
                        for k in range(KC):
                            for t in range(4):
                                mm = pe.transpose(trp[q % 2][k][:, t * P:(t + 1) * P],
                                                  n_all[:, 4 * q + t, k * P:(k + 1) * P], ident[:, :])
                        mm.then_inc(tr_ready, 1)

                    def logits(q):
                        if q == 0:
                            pe.wait_ge(loaded, 16 * n_loads)
                        if q >= 2:
                            pe.wait_ge(lgT_ready, q - 1)
                        pe.wait_ge(nT_ready, q + 1)
                        for k in range(KC):
                            mm = pe.matmul(lgp[q % 2][0:E, :], rw[:, k, :], nT[:, q % 2, k, :], start=(k == 0), stop=(k == KC - 1))
                        mm.then_inc(lg_ready, 1)

                    def turn_logits(q):
                        pe.wait_ge(lgT_ready, q + 1)
                        for t in range(4):
                            mm = pe.transpose(ltp[:, 4 * q + t, :], lgT[0:E, q % 2, t * P:(t + 1) * P], ident[0:E, 0:E])
                        mm.then_inc(lt_ready, 1)

                    for g in range(2):
                        turn_rows(2 * g)
                        turn_rows(2 * g + 1)
                        logits(2 * g)
                        logits(2 * g + 1)
                        turn_logits(2 * g)
                        turn_logits(2 * g + 1)
                    pe.wait_ge(mask_ready, 1)
                    for s in range(T - 1, 0, -1):
                        pe.matmul(rank[:, s:T, :], G["ones_bf"][:, :], Mb[:, 0:T - s, :], start=(s == T - 1), stop=False,
                                  skip_group_check=True)
                    pe.matmul(rank[:, :, :], G["before_bf"][:, :], Mb[:, :, :], start=False, stop=True, skip_group_check=True)
                    for t in range(T):
                        mm = pe.matmul(cntp, G["ones_bf"][:, :], Mb[:, t, :], start=(t == 0), stop=(t == T - 1), skip_group_check=True)
                    mm.then_inc(rank_ready, 1)

                @block.vector
                def _(v):
                    def bc_e(a):
                        return a[:, :].rearrange("p (t o) -> p t o", o=1).broadcast_to([P, T, E])

                    def stats_of(g, src, done):
                        r8 = slice(8 * g, 8 * g + 8)
                        for t in range(8 * g, 8 * g + 8):
                            v.bn_stats(bn[:, t, :], src[:, t, :])
                        v.drain()
                        for t in range(8 * g, 8 * g + 8):
                            v.bn_aggr(mv[:, t, :], bn[:, t, :])
                        v.drain()
                        rsqrt(v, rstd[:, r8], mv[:, r8, 1], tmp[:, r8], 1e-5)
                        v.scalar_tensor_tensor(nb[:, r8], mv[:, r8, 0], -1.0, rstd[:, r8], ALU.mult, ALU.mult).then_inc(done, 1)

                    stats_of(0, x, stats)
                    stats_of(1, x, stats)
                    if inner_norm:
                        v.wait_ge(loaded, 16 * n_loads)
                        for g in range(2):
                            v.wait_ge(normed, 2 * g + 2)
                            stats_of(g, n_all, stats2)
                        for q in range(QT):
                            v.wait_ge(normed, 4 + q + 1)
                            blk4 = n_all[:, 4 * q:4 * q + 4, :]
                            v.tensor_tensor(blk4, blk4, gb[:, 0, :].rearrange("p (o d) -> p o d", o=1).broadcast_to([P, 4, D]),
                                            ALU.mult).then_inc(scaled, 1)
                    v.wait_ge(loaded, 16 * n_loads)
                    v.wait_ge(lt_ready, QT)
                    if rb is not None:
                        v.tensor_tensor(lg[:, :, :], ltp[:, :, :], rb[:, :].rearrange("p (o e) -> p o e", o=1).broadcast_to([P, T, E]), ALU.add)
                    elif clip:
                        v.tensor_scalar(lg[:, :, :], ltp[:, :, :], clip, -clip, ALU.min, ALU.max)
                    else:
                        v.tensor_copy(lg[:, :, :], ltp[:, :, :])
                    v.drain()
                    v.tensor_reduce(m[:, :], lg[:, :, :], AX.X, ALU.max)
                    v.drain()
                    v.tensor_tensor(t1[:, :, :], lg[:, :, :], bc_e(m), ALU.subtract).then_inc(shifted, 1)
                    v.wait_ge(exped, 1)
                    v.tensor_reduce(r[:, :], ex[:, :, :], AX.X, ALU.add)
                    v.drain()
                    if eps_sum and not renorm:
                        v.tensor_scalar(r[:, :], r[:, :], eps_sum, None, ALU.add)
                        v.drain()
                    v.reciprocal(r[:, :], r[:, :])
                    v.drain()
                    v.tensor_tensor(ex[:, :, :], ex[:, :, :], bc_e(r), ALU.mult)
                    v.drain()
                    iota = G["iota_e"][:, 0:E].rearrange("p (o e) -> p o e", o=1).broadcast_to([P, T, E])
                    for k in range(K):
                        v.tensor_reduce(p_k[k][:, :], ex[:, :, :], AX.X, ALU.max)
                        v.drain()
                        v.tensor_tensor(t1[:, :, :], ex[:, :, :], bc_e(p_k[k]), ALU.is_lt)
                        v.drain()
                        v.scalar_tensor_tensor(t1[:, :, :], t1[:, :, :], 64.0, iota, ALU.mult, ALU.add)
                        v.drain()
                        v.tensor_reduce(m[:, :], t1[:, :, :], AX.X, ALU.min)
                        v.drain()
                        v.tensor_tensor(oh[k][:, :, :], iota, bc_e(m), ALU.is_equal)
                        v.drain()
                        v.scalar_tensor_tensor(ex[:, :, :], oh[k][:, :, :], -4.0, ex[:, :, :], ALU.mult, ALU.add)
                        v.drain()
                    if renorm:
                        v.tensor_tensor(m[:, :], p_k[0][:, :], p_k[1][:, :], ALU.add)
                        v.drain()
                        v.tensor_scalar(m[:, :], m[:, :], eps_sum, None, ALU.add)
                        v.drain()
                        v.reciprocal(m[:, :], m[:, :])
                        v.drain()
                        for k in range(K):
                            v.tensor_tensor(p_k[k][:, :], p_k[k][:, :], m[:, :], ALU.mult)
                        v.drain()
                    v.tensor_tensor(t1[:, :, :], oh[0][:, :, :], oh[1][:, :, :], ALU.add)
                    v.drain()
                    for k in range(2, K):
                        v.tensor_tensor(t1[:, :, :], t1[:, :, :], oh[k][:, :, :], ALU.add)
                        v.drain()
                    v.tensor_copy(Mb[:, :, :], t1[:, :, :]).then_inc(mask_ready, 1)
                    v.wait_ge(rank_ready, 1)
                    if cap:
                        v.tensor_scalar(cnti[:, :], cntp, float(cap), float(BS - 1), ALU.min, ALU.add)
                    else:
                        v.tensor_scalar(cnti[:, :], cntp, float(BS - 1), None, ALU.add)
                    v.drain()
                    sh = BS.bit_length() - 1
                    v.tensor_scalar(cnti[:, :], cnti[:, :], sh, sh, ALU.logical_shift_right, ALU.logical_shift_left)
                    v.drain()
                    v.tensor_copy(cnt[:, :], cnti[:, :])
                    v.drain()
                    v.tensor_tensor(tE[:, :, :], cnt[:, :].rearrange("p (o e) -> p o e", o=1).broadcast_to([P, E, E]),
                                    G["below_e"][:, 0:E, 0:E], ALU.mult)
                    v.drain()
                    v.tensor_reduce(offs[:, :], tE[:, :, :], AX.X, ALU.add)
                    v.drain()
                    v.tensor_tensor(ends[:, :], offs[:, :], cnt[:, :], ALU.add)
                    v.drain()
                    v.tensor_tensor(tB[:, :, :], ends[:, :].rearrange("p (o e) -> p o e", o=1).broadcast_to([P, NR, E]),
                                    G["iota_b"][:, 0:NR].rearrange("p (b o) -> p b o", o=1).broadcast_to([P, NR, E]), ALU.is_le)
                    v.drain()
                    v.tensor_reduce(nblk[:, :], tB[:, :, :], AX.X, ALU.add)
                    v.drain()
                    v.tensor_scalar(blk[:, :], nblk[:, :], float(E - 1), float(shared), ALU.min, ALU.add)
                    if cap:
                        v.tensor_scalar(t2[:, :, :], rank[:, :, :], float(cap), None, ALU.is_lt)
                    v.tensor_tensor(lg[:, :, :], rank[:, :, :], offs[:, :].rearrange("p (o e) -> p o e", o=1).broadcast_to([P, T, E]), ALU.add)
                    v.drain()
                    for k in range(K):
                        v.tensor_tensor(t1[:, :, :], lg[:, :, :], oh[k][:, :, :], ALU.mult)
                        v.drain()
                        v.tensor_reduce(m[:, :], t1[:, :, :], AX.X, ALU.add)
                        v.drain()
                        if cap:
                            v.tensor_tensor(t1[:, :, :], t2[:, :, :], oh[k][:, :, :], ALU.mult)
                            v.drain()
                            v.tensor_reduce(keep[:, :], t1[:, :, :], AX.X, ALU.add)
                            v.drain()
                            v.tensor_tensor(p_k[k][:, :], p_k[k][:, :], keep[:, :], ALU.mult)
                            v.tensor_scalar(r[:, :], keep[:, :], -1.0e6, 1.0e6 + BASE, ALU.mult, ALU.add)
                            v.drain()
                            v.tensor_tensor(m[:, :], m[:, :], r[:, :], ALU.add)
                            v.drain()
                            v.tensor_copy(slot_w[:, :, k], m[:, :])
                            v.tensor_scalar(slot_r[:, :, k], m[:, :], float(ROWS - 1), None, ALU.min)
                        else:
                            v.tensor_scalar(slot_w[:, :, k], m[:, :], float(BASE), None, ALU.add)
                            v.tensor_scalar(slot_r[:, :, k], m[:, :], float(BASE), None, ALU.add)
                        v.tensor_scalar(p_k[k][:, :], p_k[k][:, :], tg, None, ALU.mult)
                        v.drain()

        with ExitStack() as c2:
            M = Alloc(nc, c2, name + "m")
            raw = [M.sb(f"raw{s}", [P, CW]) for s in range(NS)]
            whi = [M.sb(f"whi{s}", [P, WW], F32R) for s in range(NS)]
            wlo = [M.sb(f"wlo{s}", [P, WW], F32R) for s in range(NS)]
            b12 = [M.sb(f"b12_{s}", [P, 1 + P]) for s in range(NS)] if biases else None
            xr = [M.sb(f"xr{q}", [P, BT, D]) for q in range(2)]
            xT = [[M.sb(f"xT{h}{q}", [P, KC, BS], F32R) for q in range(2)] for h in ("hi", "lo")]
            act_sb = [M.sb(f"act{q}", [P, BS]) for q in range(RG)]
            h_f = [M.sb(f"h_f{q}", [P, BS]) for q in range(RG)] if glu else act_sb
            hh = [[M.sb(f"h{h}{q}", [P, BS], F32R) for q in range(RG)] for h in ("hi", "lo")]
            y_sb = [M.sb(f"y{q}", [P, BT, D]) for q in range(2)]
            NG = 4
            gath = [M.sb(f"gath{q}", [P, K + 1, D]) for q in range(NG)]
            gu = [M.ps(f"gu{q}", [P, 512]) for q in range(RG)]
            yp = [M.ps(f"yp{q}", [P, 512]) for q in range(2)]
            xtp = [M.ps(f"xtp{q}", [P, 512]) for q in range(2)]
            w_in = [M.sem(f"w_in{s}") for s in range(NS)]
            x_in = [M.sem(f"x_in{q}") for q in range(2)]
            y_out = [M.sem(f"y_out{q}") for q in range(2)]
            w_hi, w_lo_v, w_lo_p, b_ok, scattered, xt_ready, xT_hi, xT_lo, gu_ready, act_done, h_ready, h_used, y_copied = (
                M.sem(s) for s in ("w_hi", "w_lo_v", "w_lo_p", "b_ok", "scattered", "xt_ready", "xT_hi", "xT_lo", "gu_ready",
                                   "act_done", "h_ready", "h_used", "y_copied"))
            all_out = M.sem("all_out")
            g_in = [M.sem(f"g_in{q}") for q in range(NG)]
            s_in = [M.sem(f"s_in{q}") for q in range(NG)]
            g_used = M.sem("g_used")
            NP4 = 4
            pre_in = [M.sem(f"pre_in{q}") for q in range(NP4)]
            pre_hi, pre_lo = M.sem("pre_hi"), M.sem("pre_lo")
            per_tile = -(-len(jobs) // T)

            def jobs_of(t):
                return list(enumerate(jobs))[t * per_tile:(t + 1) * per_tile]
            SI = SJ // JT
            XA = TX + 1
            CUTS = [1, 2, *([SI - 2, SI - 1, SI, SI + 1] if shared else []), NI - 2, NI - 1]

            def is_job(lo, hi, job):
                a, b = JT * lo + job < NJ, JT * hi + job < NJ
                assert a == b
                return a


            def w_views(s):
                hi, lo = whi[s], wlo[s]
                first = [[(hi[:, k * W1 + g * P:k * W1 + (g + 1) * P], lo[:, k * W1 + g * P:k * W1 + (g + 1) * P])
                          for g in range(W1 // P)] for k in range(KC)]
                return first, (hi[:, KC * W1:WW], lo[:, KC * W1:WW])

            def in_shared(i, lo, hi, job):
                a, b = JT * lo + job < SJ, JT * hi + job < SJ
                assert a == b
                return a

            def of_lo(i, lo, hi, c):
                return (w_lo_v, CI, c + 1) if in_shared(i, lo, hi, c // FC) else (w_lo_p, CI, c + 1 - SJ * FC)

            def split_lo(e, i, lo, hi, c):
                s = c % NS
                wait(e, b_ok if biases else w_hi, i, lo, CI, c + 1)
                wait(e, h_used, i, lo, CI, c - NS + 1)
                e.tensor_tensor(wlo[s][:, :], raw[s][:, 0:WW], whi[s][:, :].bitcast(F32), ALU.subtract).then_inc(
                    w_lo_v if in_shared(i, lo, hi, c // FC) else w_lo_p, 1)

            with nc.Block() as block:
                @block.sync
                def _(sp):
                    def load_w(i, lo, hi, c, expert):
                        s = c % NS
                        src = w_dram[expert, c % FC] if isinstance(expert, int) else \
                            w_dram[bass.ds(expert, 1), c % FC].rearrange("o p w -> (o p) w")
                        sem, a, b = of_lo(i, lo, hi, c - NS)
                        wait(sp, sem, i, lo, a, b)
                        sp.dma_start(raw[s][:, :], src).then_inc(w_in[s], 16)

                    def load_x(i, lo, hi, job):
                        q, rows = job % 2, rows_of(rows_x, i, job)
                        wait(sp, xt_ready, i, lo, JT, job - 1)
                        sp.dma_start(xr[q][:, :, :], rows).then_inc(x_in[q], 16)

                    def rows_of(dram, i, job):
                        a = (JT * i + job) * BS
                        if isinstance(i, int):
                            return dram[a:a + BS, :].rearrange("(t p) d -> p t d", p=P)
                        return dram[bass.ds(sp.snap(a), BS), :].rearrange("(t p) d -> p t d", p=P)

                    def expert_of(i, lo, hi, job):
                        if in_shared(i, lo, hi, job):
                            return 0
                        at = JT * i + (job - SJ)
                        ap = blk[0:1, at:at + 1] if isinstance(i, int) else blk[0:1, bass.ds(at, 1)]
                        return sp.value_load(ap, min_val=0, max_val=E - 1 + shared)

                    first = [expert_of(0, 0, 0, j) for j in range((NS - 1) // FC + 1)]
                    for c in range(NS):
                        load_w(0, 0, 0, c, first[c // FC])
                        if shared and c == 0:
                            for job in range(XA):
                                load_x(0, 0, 0, job)
                    if not shared:
                        sp.wait_ge(scattered, 16 * T * K)
                        for job in range(XA):
                            load_x(0, 0, 0, job)

                    def body(i, lo, hi):
                        known = {}
                        for c in range(CI):
                            j, cj = divmod(c, FC)
                            if not is_job(lo, hi, j):
                                continue
                            if cj == 0:
                                if is_job(lo, hi, j + XA):
                                    if shared and JT * lo + j + XA == SJ:
                                        sp.wait_ge(scattered, 16 * T * K)
                                    load_x(i, lo, hi, j + XA)
                            if is_job(lo, hi, (c + NS) // FC):
                                tj = (c + NS) // FC
                                if tj not in known:
                                    known[tj] = expert_of(i, lo, hi, tj)
                                load_w(i, lo, hi, c + NS, known[tj])
                            if cj == min(1, FC - 1):
                                if not (lo == 0 and j == 0):
                                    store_y(i, lo, hi, j - 1)

                    def store_y(i, lo, hi, job):
                        q, rows = job % 2, rows_of(rows_y, i, job)
                        wait(sp, y_copied, i, lo, JT, job + 1)
                        sp.dma_start(rows, y_sb[q][:, :, :]).then_inc(y_out[q], 16)

                    run_loop(sp, NI, CUTS, body)
                    store_y(NI - 1, NI - 1, NI - 1, JL)
                    for q in range(2):
                        sp.wait_ge(y_out[q], 16 * ((NJ + 1 - q) // 2))
                    sp.nop().then_inc(all_out, 1)
                    for t in range(T):
                        if shared:
                            if t >= NG:
                                sp.wait_ge(g_used, t - NG + 1)
                            sp.dma_start(gath[t % NG][:, K, :], rows_y[t * P:(t + 1) * P, :]).then_inc(s_in[t % NG], 16)
                        for n, (src, hi_, lo_) in jobs_of(t):
                            if n >= NP4:
                                sp.wait_ge(pre_lo, n - NP4 + 1)
                            sp.dma_start(raw[n % NP4][:, 0:src.shape[1]], src).then_inc(pre_in[n % NP4], 16)

                @block.gpsimd
                def _(pool):
                    def scatter(t, k):
                        pool.indirect_dma_start(out=rows_x[0:ROWS, :],
                                                out_offset=bass.IndirectOffsetOnAxis(ap=slot_w[:, t, k:k + 1], axis=0),
                                                in_=n_all[:, t, :], in_offset=None,
                                                bounds_check=ROWS - 1, oob_is_err=False).then_inc(scattered, 16)

                    for t in range(T):
                        for k in range(K):
                            scatter(t, k)

                    if not shared:
                        for c in range(LA):
                            split_lo(pool, 0, 0, 0, c)

                    def body(i, lo, hi):
                        for c in range(LA, CI + LA):
                            if not is_job(lo, hi, c // FC):
                                continue
                            if not in_shared(i, lo, hi, c // FC):
                                split_lo(pool, i, lo, hi, c)

                    run_loop(pool, NI, CUTS, body, start=max(SI - 1, 0))
                    pool.wait_ge(all_out, 1)
                    for t in range(T):
                        if t >= NG:
                            pool.wait_ge(g_used, t - NG + 1)
                        for k in range(K):
                            pool.indirect_dma_start(out=gath[t % NG][:, k, :], out_offset=None, in_=rows_y[0:ROWS, :],
                                                    in_offset=bass.IndirectOffsetOnAxis(ap=slot_r[:, t, k:k + 1], axis=0)
                                                    ).then_inc(g_in[t % NG], 16)

                @block.scalar
                def _(act):
                    def split_hi(i, lo, hi, c):
                        s = c % NS
                        wait(act, w_in[s], i, lo, 16 * per_slot, 16 * (c // NS + 1))
                        wait(act, h_used, i, lo, CI, c - NS + 1)
                        act.activation(whi[s][:, :], raw[s][:, 0:WW], ACT.Copy).then_inc(w_hi, 1)

                    def x_hi(i, lo, hi, job):
                        wait(act, xt_ready, i, lo, JT, job + 1)
                        wait(act, gu_ready, i, lo, CI, FC * (job - 1))
                        act.activation(xT[0][job % 2][:, :, :], xtp[job % 2][:, :].rearrange("p (k n) -> p k n", k=KC), ACT.Copy).then_inc(xT_hi, 1)

                    def copy_y(i, lo, hi, job):
                        q = job % 2
                        wait(act, h_used, i, lo, CI, FC * (job + 1))
                        wait(act, y_out[q], i, lo, 16 * JT // 2, 16 * ((job - 2 - q) // 2 + 1))
                        act.activation(y_sb[q][:, :, :], yp[q][:, :].rearrange("p (t n) -> p t n", t=BT), ACT.Copy).then_inc(y_copied, 1)

                    split_hi(0, 0, 0, 0)
                    for job in range(TX):
                        x_hi(0, 0, 0, job)
                    for c in range(1, LA):
                        split_hi(0, 0, 0, c)

                    def body(i, lo, hi):
                        for c in range(CI):
                            j, cj = divmod(c, FC)
                            if not is_job(lo, hi, j):
                                continue
                            wait(act, gu_ready, i, lo, CI, c + 1)
                            if glu:
                                wait(act, h_ready, i, lo, CI, c - RG + 1)
                                act.activation(act_sb[c % RG][:, :], gu[c % RG][:, 0:BS], func).then_inc(act_done, 1)
                            else:
                                wait(act, h_ready, i, lo, CI, c - RG + 1)
                                if biases:
                                    wait(act, b_ok, i, lo, CI, c + 1)
                                    act.activation(h_f[c % RG][:, :], gu[c % RG][:, 0:BS], func, bias=b12[c % NS][:, 0:1]).then_inc(act_done, 1)
                                else:
                                    act.activation(h_f[c % RG][:, :], gu[c % RG][:, 0:BS], func).then_inc(act_done, 1)
                            if is_job(lo, hi, (c + LA) // FC):
                                split_hi(i, lo, hi, c + LA)
                            if cj == LG - 1 and is_job(lo, hi, j + TX):
                                x_hi(i, lo, hi, j + TX)
                            if not biases and cj == 0 and not (lo == 0 and j == 0):
                                copy_y(i, lo, hi, j - 1)

                    run_loop(act, NI, CUTS, body)
                    if not biases:
                        copy_y(NI - 1, NI - 1, NI - 1, JL)
                    for n, (src, hi_, lo_) in enumerate(jobs):
                        act.wait_ge(pre_in[n % NP4], 16 * (n // NP4 + 1))
                        act.activation(hi_, raw[n % NP4][:, 0:src.shape[1]], ACT.Copy).then_inc(pre_hi, 1)

                @block.vector
                def _(v):
                    def x_lo(i, lo, hi, job):
                        wait(v, xT_hi, i, lo, JT, job + 1)
                        v.tensor_tensor(xT[1][job % 2][:, :, :], xtp[job % 2][:, :].rearrange("p (k n) -> p k n", k=KC),
                                        xT[0][job % 2][:, :, :].bitcast(F32), ALU.subtract).then_inc(xT_lo, 1)

                    def take_b(i, lo, hi, c):
                        s = c % NS
                        wait(v, w_hi, i, lo, CI, c + 1)
                        wait(v, h_used, i, lo, CI, c - NS + 1)
                        v.tensor_copy(b12[s][:, :], raw[s][:, WW:CW]).then_inc(b_ok, 1)

                    def y_bias(i, lo, hi, job):
                        q = job % 2
                        wait(v, h_used, i, lo, CI, FC * (job + 1))
                        wait(v, y_out[q], i, lo, 16 * JT // 2, 16 * ((job - 2 - q) // 2 + 1))
                        for cj in range(FC):
                            s = (job * FC + cj) % NS
                            b2 = b12[s][:, 1:1 + P].rearrange("p (o n) -> p o n", o=1).broadcast_to([P, BT, P])
                            ins = v.tensor_tensor(y_sb[q][:, :, cj * P:(cj + 1) * P],
                                                  yp[q][:, :].rearrange("p (t n) -> p t n", t=BT)[:, :, cj * P:(cj + 1) * P], b2, ALU.add)
                        ins.then_inc(y_copied, 1)

                    for c in range(LA if biases else 0):
                        take_b(0, 0, 0, c)
                    for c in range(LA if shared else 0):
                        split_lo(v, 0, 0, 0, c)
                    for job in range(TX):
                        x_lo(0, 0, 0, job)

                    def body(i, lo, hi):
                        for c in range(CI):
                            j, cj = divmod(c, FC)
                            if not is_job(lo, hi, j):
                                continue
                            wait(v, act_done, i, lo, CI, c + 1)
                            q = c % RG
                            if glu:
                                v.tensor_tensor(h_f[q][:, :], act_sb[q][:, :], gu[q][:, BS:2 * BS], ALU.mult)
                                v.drain()
                            wait(v, h_used, i, lo, CI, c - RG + 1)
                            v.tensor_copy(hh[0][q][:, :], h_f[q][:, :])
                            v.drain()
                            v.tensor_tensor(hh[1][q][:, :], h_f[q][:, :], hh[0][q][:, :].bitcast(F32), ALU.subtract).then_inc(h_ready, 1)
                            if biases and cj == 0 and not (lo == 0 and j == 0):
                                y_bias(i, lo, hi, j - 1)
                            if is_job(lo, hi, (c + LA) // FC):
                                if biases:
                                    take_b(i, lo, hi, c + LA)
                                if in_shared(i, lo, hi, (c + LA) // FC):
                                    split_lo(v, i, lo, hi, c + LA)
                            if cj == LG - 1 and is_job(lo, hi, j + TX):
                                x_lo(i, lo, hi, j + TX)

                    run_loop(v, NI, CUTS, body)
                    if biases:
                        y_bias(NI - 1, NI - 1, NI - 1, JL)
                    for t in range(T):
                        q = t % NG
                        if shared:
                            v.wait_ge(s_in[q], 16 * (t // NG + 1))
                            v.scalar_tensor_tensor(x[:, t, :], gath[q][:, K, :], tg, x[:, t, :], ALU.mult, ALU.add)
                            v.drain()
                        v.wait_ge(g_in[q], 16 * K * (t // NG + 1))
                        for k in range(K):
                            ins = v.scalar_tensor_tensor(x[:, t, :], gath[q][:, k, :], p_k[k][:, t:t + 1], x[:, t, :], ALU.mult, ALU.add)
                            v.drain()
                        if add_input:
                            v.scalar_tensor_tensor(x[:, t, :], n_all[:, t, :], tg, x[:, t, :], ALU.mult, ALU.add)
                        v.drain().then_inc(g_used, 1)
                        if jobs:
                            v.bn_stats(G["bn"][:, t, :], x[:, t, :])
                        for n, (src, hi_, lo_) in jobs_of(t):
                            v.wait_ge(pre_hi, n + 1)
                            v.tensor_tensor(lo_, raw[n % NP4][:, 0:src.shape[1]], hi_.bitcast(F32), ALU.subtract).then_inc(pre_lo, 1)

                @block.tensor
                def _(pe):
                    def x_turn(i, lo, hi, job):
                        q = job % 2
                        wait(pe, x_in[q], i, lo, 16 * JT // 2, 16 * (job // 2 + 1))
                        wait(pe, xT_lo, i, lo, JT, job - 1)
                        for k in range(KC):
                            for t in range(BT):
                                mm = pe.transpose(xtp[q][:, k * BS + t * P:k * BS + (t + 1) * P], xr[q][:, t, k * P:(k + 1) * P], ident[:, :])
                        mm.then_inc(xt_ready, 1)

                    def first_product(i, lo, hi, c):
                        j, cj = divmod(c, FC)
                        q, s = j % 2, c % NS
                        if cj == 0:
                            wait(pe, xT_lo, i, lo, JT, j + 1)
                        wait(pe, w_hi, i, lo, CI, c + 1)
                        sem, a, b = of_lo(i, lo, hi, c)
                        wait(pe, sem, i, lo, a, b)
                        wait(pe, h_ready, i, lo, CI, c - RG + 1)
                        w, _ = w_views(s)
                        for g in range(W1 // P):
                            for k in range(KC):
                                mm = mm3(pe, gu[c % RG][:, g * BS:(g + 1) * BS], w[k][g],
                                         (xT[0][q][:, k, :], xT[1][q][:, k, :]), k == 0, k == KC - 1)
                        mm.then_inc(gu_ready, 1)

                    def second_product(i, lo, hi, c):
                        j, cj = divmod(c, FC)
                        q, s = j % 2, c % NS
                        wait(pe, h_ready, i, lo, CI, c + 1)
                        if cj == 0:
                            wait(pe, y_copied, i, lo, JT, j - 1)
                        _, w = w_views(s)
                        for t in range(BT):
                            h = (hh[0][c % RG][:, t * P:(t + 1) * P], hh[1][c % RG][:, t * P:(t + 1) * P])
                            mm = mm3(pe, yp[q][:, t * D:(t + 1) * D], h, w, cj == 0 and t == 0, cj == FC - 1 and t == BT - 1,
                                     skip_group_check=True)
                        mm.then_inc(h_used, 1)

                    for job in range(TX):
                        x_turn(0, 0, 0, job)
                    for c in range(LG):
                        first_product(0, 0, 0, c)

                    def body(i, lo, hi):
                        for c in range(CI):
                            j, cj = divmod(c, FC)
                            if not is_job(lo, hi, j):
                                continue
                            if cj == 0 and TX == 1 and is_job(lo, hi, j + TX):
                                x_turn(i, lo, hi, j + TX)
                            if is_job(lo, hi, (c + LG) // FC):
                                first_product(i, lo, hi, c + LG)
                            if cj == 0 and TX > 1 and is_job(lo, hi, j + TX):
                                x_turn(i, lo, hi, j + TX)
                            second_product(i, lo, hi, c)

                    run_loop(pe, NI, CUTS, body)



def constants():
    i = np.arange(P)
    e = np.arange(16)
    f = np.arange(S, dtype=np.float32)[:, None] * (1.0 / 10000.0 ** (np.arange(0, 16, 2, dtype=np.float32) / 16)).astype(np.float32)[None]
    cs = np.stack([np.cos(f), -np.sin(f), np.sin(f)], 1).astype(np.float32).reshape(TB, P, 3, 8).transpose(1, 0, 2, 3)
    later = np.where(np.arange(S)[None, :] > np.arange(S)[:, None], 1e9, 0.0).astype(np.float32).reshape(TB, P, S).transpose(1, 0, 2)
    return {
        "rotary": np.ascontiguousarray(cs),
        "causal": np.ascontiguousarray(later),
        "ident": np.eye(P, dtype=np.float32),
        "before": (i[:, None] < i[None, :]).astype(np.float32),
        "below_e": np.broadcast_to((e[None, :] < e[:, None]).astype(np.float32), (P, 16, 16)).copy(),
        "iota_e": np.broadcast_to(e.astype(np.float32), (P, 16)).copy(),
        "iota_b": np.broadcast_to((BS * np.arange(40)).astype(np.float32), (P, 40)).copy(),
    }


def setup_phase(nc, G, I):
    with ExitStack() as ctx:
        A = Alloc(nc, ctx, "set")
        loaded = A.sem("loaded")
        before = A.sb("before", [P, P])
        g8 = A.sb("g8", [P, 8])
        with nc.Block() as block:
            @block.sync
            def _(sp):
                sp.dma_start(G["x"][:, :, :], I["x"].rearrange("b (t p) d -> p (b t) d", p=P)).then_inc(loaded, 16)
                for q, name in enumerate(("g_xattn", "g_ffn")):
                    sp.dma_start(g8[:, 4 * q:4 * q + 4], I[name].rearrange("(a n) -> a n", a=1).broadcast_to([P, 4])).then_inc(loaded, 16)
                for name in ("ident", "below_e", "iota_e", "iota_b"):
                    sp.dma_start(G[name].ap(), I[name]).then_inc(loaded, 16)
                sp.dma_start(before[:, :], I["before"]).then_inc(loaded, 16)
                sp.wait_ge(loaded, 16 * 8)

            @block.vector
            def _(v):
                v.memset(G["ones_bf"][:, :], 1.0)
                v.wait_ge(loaded, 16 * 8)
                v.tensor_copy(G["before_bf"][:, :], before[:, :])

            @block.scalar
            def _(act):
                act.wait_ge(loaded, 16 * 8)
                act.activation(G["tanh_g"][:, :], g8[:, :], ACT.Tanh)
                act.activation(G["identr"][:, :], G["ident"][:, :], ACT.Copy)


def globals_of(nc, A):
    G = {
        "x": A.sb("x", [P, T, D]),
        "ident": A.sb("ident", [P, P]),
        "identr": A.sb("identr", [P, P], F32R),
        "before_bf": A.sb("before_bf", [P, P], BF16),
        "ones_bf": A.sb("ones_bf", [P, P], BF16),
        "below_e": A.sb("below_e", [P, 16, 16]),
        "iota_e": A.sb("iota_e", [P, 16]),
        "iota_b": A.sb("iota_b", [P, 40]),
        "bn": A.sb("bn", [P, T, 6]),
        "tanh_g": A.sb("tanh_g", [P, 8]),
        "rows_x": nc.dram_tensor("rows_x", [XROWS, D], F32).ap(),
        "ctxT": [nc.dram_tensor(f"ctxT_{h}", [B, P, KC, S], F32).ap() for h in ("hi", "lo")],
        "rows_y": nc.dram_tensor("rows_y", [XROWS, D], F32).ap(),
    }
    return G


def final_phase(nc, G, out):
    with ExitStack() as ctx:
        A = Alloc(nc, ctx, "fin")
        stored = A.sem("stored")
        with nc.Block() as block:
            @block.sync
            def _(sp):
                sp.dma_start(out.rearrange("b (t p) d -> p (b t) d", p=P), G["x"][:, :, :]).then_inc(stored, 16)
                sp.wait_ge(stored, 16)


def moe_layer(nc, G, I, layer, jobs=()):
    if layer == 0:
        moe_phase(nc, G, "moe0", 0, E=15, K=3, FC=2, glu=False, func=ACT.Relu, shared=True, w_dram=I["moe_w0"],
                  rw_dram=I["L0_ffn_router_W"].rearrange("(k p) e -> p k e", p=P), rb_dram=I["L0_ffn_router_b"], biases=True, jobs=jobs)
    if layer == 1:
        moe_phase(nc, G, "moe1", 1, E=8, K=2, FC=6, glu=True, func=ACT.Silu, shared=True, w_dram=I["moe_w1"],
                  rw_dram=I["rw1"].rearrange("(k p) e -> p k e", p=P), renorm=True, eps_sum=1e-20, jobs=jobs)
    if layer == 2:
        moe_phase(nc, G, "moe2", 2, E=8, K=2, FC=8, glu=True, func=ACT.Silu, shared=False, w_dram=I["moe_w2"],
                  rw_dram=I["rw2"].rearrange("(k p) e -> p k e", p=P), eps_sum=1e-12, cap=640, clip=10000.0,
                  inner_norm=(I["L2_ffn_ln_gamma"], I["L2_ffn_ln_beta"]), jobs=jobs)
    if layer == 3:
        moe_phase(nc, G, "moe3", 3, E=8, K=2, FC=8, glu=False, func=ACT.Gelu, shared=True, w_dram=I["moe_w3"],
                  rw_dram=I["L3_ffn_router_w"].rearrange("(k p) e -> p k e", p=P), add_input=True)


def pack_chunks(ups, down, b1=None, b2=None):
    e, _, f = ups[0].shape
    fc = -(-f // P)
    up = np.stack(ups, 2)
    up = np.pad(up, ((0, 0), (0, 0), (0, 0), (0, fc * P - f)))
    up = up.reshape(e, KC, P, len(ups), fc, P).transpose(0, 4, 2, 1, 3, 5)
    dn = np.pad(down, ((0, 0), (0, fc * P - f), (0, 0))).reshape(e, fc, P, D)
    parts = [up.reshape(e, fc, P, -1), dn]
    if b1 is not None:
        parts.append(b1.reshape(e, fc, P, 1))
        parts.append(np.broadcast_to(b2.reshape(e, fc, 1, P), (e, fc, P, P)))
    return np.ascontiguousarray(np.concatenate(parts, 3))


def lay_out(inp):
    a = {k: np.asarray(v) for k, v in inp.items()}
    tr = lambda w: np.swapaxes(w, -1, -2)
    cat = lambda s, e: np.concatenate([s[None], e], 0)
    out = dict(constants())
    for k in ("ctx_1024", "mask_BxS2_if1", "L1_xattn_bo", "L2_xattn_bq", "L2_xattn_bk", "L2_xattn_bv", "L2_xattn_bo", "L2_xattn_Wq",
              "L2_xattn_Wk", "L2_xattn_Wv", "L3_xattn_ln_gamma", "L3_xattn_ln_beta", "L3_xattn_w_q", "L3_xattn_w_out", "L3_xattn_b_out",
              "L3_xattn_gate", "L0_xattn_Wq", "L0_xattn_Wk", "L0_xattn_Wv", "L0_xattn_Wcq", "L0_xattn_Wck", "L0_xattn_Wcv",
              "L0_xattn_gamma", "L0_xattn_beta", "L0_xattn_W1", "L0_xattn_b1"):
        out[k] = a[k]
    turn = lambda w: np.ascontiguousarray(w.reshape(*w.shape[:-1], 16, 8, 2).swapaxes(-1, -2).reshape(w.shape))
    twice = lambda w: np.ascontiguousarray(np.broadcast_to(w.reshape(16, 1, 16, D), (16, 2, 16, D)).reshape(512, D))
    for n in ("q", "k"):
        out[f"L1_W{n}"] = turn(np.ascontiguousarray(tr(a[f"L1_xattn_W{n}"])))
        out[f"L1_b{n}"] = turn(a[f"L1_xattn_b{n}"])
    out["L1_Wv"], out["L1_bv"] = np.ascontiguousarray(tr(a["L1_xattn_Wv"])), a["L1_xattn_bv"]
    out["L1_Wo"], out["L2_Wo"] = twice(tr(a["L1_xattn_Wo"])), twice(a["L2_xattn_Wo"])
    out["mask2"] = a["mask_Bx1xS2_ik0"].reshape(B, S)
    out["L3_w_k"], out["L3_w_v"] = (np.ascontiguousarray(a["L3_xattn_w_kv"][:, 1024 * q:1024 * (q + 1)]) for q in range(2))
    for k in ("x", "g_xattn", "g_ffn", "L0_ffn_router_W", "L0_ffn_router_b", "L2_ffn_ln_gamma", "L2_ffn_ln_beta", "L3_ffn_router_w"):
        out[k] = a[k]
    out["moe_w0"] = pack_chunks([cat(a["L0_ffn_sW1"], a["L0_ffn_eW1"])], cat(a["L0_ffn_sW2"], a["L0_ffn_eW2"]),
                                cat(a["L0_ffn_sb1"], a["L0_ffn_eb1"]), cat(a["L0_ffn_sb2"], a["L0_ffn_eb2"]))
    out["moe_w1"] = pack_chunks([tr(cat(a["L1_ffn_shared_gate"], a["L1_ffn_expert_gate"])), tr(cat(a["L1_ffn_shared_up"], a["L1_ffn_expert_up"]))],
                                tr(cat(a["L1_ffn_shared_down"], a["L1_ffn_expert_down"])))
    out["rw1"] = np.ascontiguousarray(tr(a["L1_ffn_gate_w"]))
    w12 = tr(a["L2_ffn_W12"])
    out["moe_w2"] = pack_chunks([w12[:, :, :1024], w12[:, :, 1024:]], tr(a["L2_ffn_W3"]))
    out["rw2"] = np.ascontiguousarray(tr(a["L2_ffn_Wr"]))
    out["moe_w3"] = pack_chunks([np.concatenate([a["L3_ffn_shared_up"], a["L3_ffn_routed_up"]])], np.concatenate([a["L3_ffn_shared_down"], a["L3_ffn_routed_down"]]))
    return out



def stats_all(v, src, bn, st, nmean, rstd):
    if src is not None:
        for t in range(T):
            v.bn_stats(bn[:, t, :], src[:, t, :])
        v.drain()
    for t in range(T):
        v.bn_aggr(st["mv"][:, t, :], bn[:, t, :])
    v.drain()
    v.tensor_scalar(nmean, st["mv"][:, :, 0], -1.0, None, ALU.mult)
    rsqrt(v, rstd, st["mv"][:, :, 1], st["tmp"][:, :], 1e-5)


def load_split(nc, name, jobs, st_cols, loads=None, vector_first=None, scalar_first=None, pool_work=None):
    with ExitStack() as ctx:
        A = Alloc(nc, ctx, name)
        NR = 4
        raw = [A.sb(f"raw{q}", [P, st_cols]) for q in range(NR)]
        came = [A.sem(f"came{q}") for q in range(NR)]
        hi_done, lo_done = A.sem("hi_done"), A.sem("lo_done")
        with nc.Block() as block:
            @block.sync
            def _(sp):
                if loads:
                    loads(sp)
                for n, (src, hi, lo) in enumerate(jobs):
                    if n >= NR:
                        sp.wait_ge(lo_done, n - NR + 1)
                    sp.dma_start(raw[n % NR][:, 0:src.shape[1]], src).then_inc(came[n % NR], 16)

            @block.scalar
            def _(act):
                if scalar_first:
                    scalar_first(act)
                for n, (src, hi, lo) in enumerate(jobs):
                    act.wait_ge(came[n % NR], 16 * (n // NR + 1))
                    act.activation(hi, raw[n % NR][:, 0:src.shape[1]], ACT.Copy).then_inc(hi_done, 1)

            @block.vector
            def _(v):
                if vector_first:
                    vector_first(v)
                for n, (src, hi, lo) in enumerate(jobs):
                    v.wait_ge(hi_done, n + 1)
                    v.tensor_tensor(lo, raw[n % NR][:, 0:src.shape[1]], hi.bitcast(F32), ALU.subtract).then_inc(lo_done, 1)

            if pool_work:
                @block.gpsimd
                def _(pool):
                    pool_work(pool)


def head_weights(A, dh, weights):
    HD, OC = 16 * dh, 4 if dh == 16 else 8
    w = {n: [A.sb(f"w{n}_{h}", [P, KC, HD], F32R) for h in ("hi", "lo")] for n in ("q", "k", "v")}
    w["o"] = [A.sb(f"wo_{h}", [P, OC, D], F32R) for h in ("hi", "lo")]
    jobs = []
    for n in ("q", "k", "v"):
        for k in range(KC):
            for c in range(0, HD, 512):
                e = min(c + 512, HD)
                jobs.append((weights[n][k * P:(k + 1) * P, c:e], w[n][0][:, k, c:e], w[n][1][:, k, c:e]))
    for c in range(OC):
        jobs.append((weights["o"][c * P:(c + 1) * P, :], w["o"][0][:, c, :], w["o"][1][:, c, :]))
    return w, jobs


def heads_phase(nc, G, I, name, layer, dh, weights, w, mask=None, rotary=False, inner=None, biases=None, gate=None):
    H = 16
    small = dh == 16
    GH = 4 if small else 2
    NGR = H // GH
    OC = NGR
    LEAD = 3
    scale = 1.0 / float(np.sqrt(dh))
    HD = H * dh
    if small:
        ROUNDS = [(3, "nT", 0), (4, "q", 0), (5, "k", 0), (8, "v", 0), (9, "qT", 0), (10, "kT", 0), (11, "qT", 1), (12, "kT", 1),
                  (13, "qT", 2), (14, "kT", 2), (15, "qT", 3), (15, "kT", 3)]
        OWN = []
    else:
        ROUNDS = [(4, "nT", 0), (5, "nT", 1), (6, "qT", 0), (7, "kT", 0), (8, "qT", 1), (9, "kT", 1), (10, "V0", 0), (10, "qT", 2),
                  (11, "kT", 2), (12, "V0", 1), (13, "qT", 3), (14, "kT", 3)]
        OWN = [(2, "V1", 0), (3, "V1", 1)]
    PRO = len(ROUNDS)
    BODY = sorted(OWN + ROUNDS, key=lambda r: r[0])
    NRD = len(BODY)
    assert PRO % 2 == 0 and NRD % 2 == 0

    with ExitStack() as ctx:
        A = Alloc(nc, ctx, name)
        sb, ps, sem = A.sb, A.ps, A.sem
        hl = lambda n, shape: [sb(f"{n}_{h}", shape, F32R) for h in ("hi", "lo")]
        x, ident, identr = G["x"], G["ident"], G["identr"]
        wq, wk, wv, wo = (w[n] for n in ("q", "k", "v", "o"))
        nmean, rstd = ([sb(f"{n}{q}", [P, T]) for q in range(2 if inner else 1)] for n in ("nmean", "rstd"))
        tg = sb("tg", [P, 1])
        bo = sb("bo", [P, D])
        gb = sb("gb", [P, 2, D]) if inner else None
        gate_sb = sb("gate", [P, 1]) if gate is not None else None
        if small:
            b3 = sb("b3", [P, 3, D])
            MT = TB if rotary else 1
            mask16 = sb("mask16", [P, B, MT, S], BF16)
            ident16 = sb("ident16", [P, P], BF16)
            kq = sb("kq", [P, B * TB])
            cs = sb("cs", [P, TB, 3, 8]) if rotary else None

            vp = sb("vp", [P, TB, 4, 640], F32R)
        else:
            QT = hl("QT", [P, H, S])

        with ExitStack() as c2:
            R = Alloc(nc, c2, name + "p")
            st = {"mv": R.sb("mv", [P, T, 2]), "tmp": R.sb("tmp", [P, T])}
            loaded, tg_ready, once, normed = (R.sem(n) for n in ("loaded", "tg_ready", "once", "normed"))
            n1 = R.sb("n1", [P, T, D]) if inner else None
            nb = R.sb("nb", [P, T]) if inner else None
            if small:
                mi = R.sb("mi", [P, B, S], I32)
                row0 = R.sb("row0", [P, B, S], BF16)
                causal, causal16 = (R.sb("causal", [P, TB, S]), R.sb("causal16", [P, TB, S], BF16)) if rotary else (None, None)
            n_loads = 1 + (2 if inner else 0) + (gate is not None) + ((4 + 2 * rotary) if small else 0)

            def loads(sp):
                def row(dst, src, n):
                    sp.dma_start(dst, src.rearrange("(a d) -> a d", a=1).broadcast_to([P, n])).then_inc(loaded, 16)
                if small:
                    sp.dma_start(mi[:, :, :], mask.rearrange("b s -> (b s)").rearrange("(o n) -> o n", o=1).broadcast_to([P, B * S])
                                 .rearrange("p (b s) -> p b s", s=S)).then_inc(loaded, 16)
                    if rotary:
                        sp.dma_start(cs[:, :, :, :], I["rotary"]).then_inc(loaded, 16)
                        sp.dma_start(causal[:, :, :], I["causal"]).then_inc(loaded, 16)
                    for q in range(3):
                        row(b3[:, q, :], biases[q], D)
                row(bo[:, :], weights["bo"], D)
                if inner:
                    for q in range(2):
                        row(gb[:, q, :], inner[q], D)
                if gate is not None:
                    row(gate_sb[:, :], gate, 1)

            def vector_first(v):
                stats_all(v, None, G["bn"], st, nmean[0][:, :], rstd[0][:, :])
                if inner:
                    v.tensor_tensor(nb[:, :], nmean[0][:, :], rstd[0][:, :], ALU.mult).then_inc(once, 1)
                    v.wait_ge(normed, 1)
                    stats_all(v, n1, G["bn"], st, nmean[1][:, :], rstd[1][:, :])
                v.wait_ge(loaded, 16 * n_loads)
                if gate is not None:
                    v.wait_ge(tg_ready, 1)
                    v.tensor_tensor(tg[:, :], gate_sb[:, :], G["tanh_g"][:, layer:layer + 1], ALU.mult)
                else:
                    v.tensor_copy(tg[:, :], G["tanh_g"][:, layer:layer + 1])
                v.drain()
                v.tensor_scalar(bo[:, :], bo[:, :], tg[:, :], None, ALU.mult)
                if small:
                    v.tensor_scalar(b3[:, 0, :], b3[:, 0, :], -scale, None, ALU.mult)
                    v.tensor_copy(ident16[:, :], ident[:, :])
                    v.tensor_scalar(row0[:, :, :] if rotary else mask16[:, :, 0, :], mi[:, :, :], 0.0, 1.0e9 if rotary else BIG,
                                    ALU.is_equal, ALU.mult)
                if rotary:
                    v.tensor_copy(causal16[:, :, :], causal[:, :, :])
                    v.drain()
                    for b in range(B):
                        v.tensor_tensor(mask16[:, b, :, :], causal16[:, :, :],
                                        row0[:, b, :].rearrange("p (o s) -> p o s", o=1).broadcast_to([P, TB, S]), ALU.max)
                    v.drain()
                    v.tensor_reduce(kq[:, :], mask16[:, :, :, :].rearrange("p b t s -> p (b t) s"), AX.X, ALU.min)
                    v.drain()
                    v.tensor_scalar(kq[:, :], kq[:, :], 0.0, None, ALU.is_equal)

            def scalar_first(act):
                if inner:
                    act.wait_ge(once, 1)
                    for t in range(T):
                        ins = act.activation(n1[:, t, :], x[:, t, :], ACT.Identity, scale=rstd[0][:, t:t + 1], bias=nb[:, t:t + 1])
                    ins.then_inc(normed, 1)
                if gate is not None:
                    act.wait_ge(loaded, 16 * n_loads)
                    act.activation(gate_sb[:, :], gate_sb[:, :], ACT.Tanh).then_inc(tg_ready, 1)

            def pool_work(pool):
                if small:
                    pool.memset(vp[:, :, :, :].bitcast(F32), 0.0)
                else:
                    for y in QT:
                        pool.memset(y[:, :, :].bitcast(F32), 0.0)

            load_split(nc, name + "w", (), 1, loads, vector_first, scalar_first, pool_work)

        n_sb = sb("n", [P, TB, D])
        nT = hl("nT", [P, KC, S])
        cT = hl("cT", [P, KC, S])
        if small:
            QT, KT = sb("QT", [P, 8, S], F32R), sb("KT", [P, 8, S], F32R)
            qf, kf, vf = sb("qf", [P, TB, D]), sb("kf", [P, TB, D]), sb("vf", [P, TB, D])
            qs, ks = (sb(n, [P, TB * H, 4, dh], F32R) for n in ("qs", "ks"))
            if rotary:
                r1, r2 = sb("turn1", [P, TB, D]), sb("turn2", [P, TB, D])
        else:
            KT = hl("KT", [P, 8, S])
            V = hl("V", [P, TB, HD])
        p_sb = [sb(f"p{q}", [P, TB, S]) for q in range(4)]
        nm, rs, ri = (sb(n, [P, 4, TB]) for n in ("nm", "rs", "ri"))
        pT = [[sb(f"pT{h}{q}", [P, KC, S], F32R) for q in range(4)] for h in ("hi", "lo")]
        OT = hl("OT", [P, OC, S])
        s_ps = [ps(f"s{q}", [P, TB, S]) for q in range(2)]
        t_ps = [ps(f"t{q}", [P, KC, S]) for q in range(2)]
        o_ps = [ps(f"o{q}", [P, 512]) for q in range(2)]
        r_ps = [ps(f"r{q}", [P, 512]) for q in range(2)]
        c_in, normed = sem("c_in"), sem("normed")
        s_ready, m_ready, e_done, r_done, n_done, t_ready, ph_done, pl_done, pv_done, oh_done, ol_done, out_ready, x_done = (
            sem(n) for n in ("s_ready", "m_ready", "e_done", "r_done", "n_done", "t_ready", "ph_done", "pl_done", "pv_done",
                             "oh_done", "ol_done", "out_ready", "x_done"))
        n_ready, rd_ready, rd_hi, rd_done, f_raw, f_ready, v_ready, v_half = (
            sem(n) for n in ("n_ready", "rd_ready", "rd_hi", "rd_done", "f_raw", "f_ready", "v_ready", "v_half"))
        vh_done = sem("vh_done")
        CUTS = [1, B - 1]

        def body_rounds(last):
            return [r for r in BODY if not last or r in OWN]

        def rounds_at(h, last):
            return [(pos, kind, part) for pos, (slot, kind, part) in enumerate(body_rounds(last)) if slot == h]

        def laid_at(h, h_q, h_k, last):
            kind = {h_q: "q", h_k: "k"}.get(h) if small and not last else None
            return [(pos, k, part) for pos, (_, k, part) in enumerate(BODY) if k == kind]

        def done_by(kind, part=0):
            return [(r[1], r[2]) for r in BODY].index((kind, part)) + 1

        def _(v):
                if small:
                    v.memset(vp[:, :, :, :].bitcast(F32), 0.0)
                else:
                    v.memset(QT[0][:, :, :].bitcast(F32), 0.0)
                    v.memset(QT[1][:, :, :].bitcast(F32), 0.0)

        def x_of(i, b):
            at = TB * (i + b)
            return x[:, at:at + TB, :] if isinstance(i, int) else x[:, bass.ds(at, TB), :]

        def v_cols(kc, half, e):
            cols = vp[:, kc, 2 * half:2 * half + 2, :].rearrange("p g (j c) -> p g j c", c=P + 32)
            return cols[:, :, :, dh * e:dh * e + dh]

        def vf_cols(kc, half):
            return vf[:, kc, 128 * half:128 * half + 128].rearrange("p (g j d) -> p g j d", g=2, j=4)

        def bc_t(a, n):
            return a.rearrange("p (o n) -> p o n", o=1).broadcast_to([P, TB, n])

        with nc.Block() as block:
            @block.sync
            def _(sp):
                def load_c(i, lo, hi, nxt):
                    b = i + nxt
                    srcs = [G["ctxT"][h][b] if isinstance(b, int) else
                            G["ctxT"][h][bass.ds(sp.snap(b), 1)].rearrange("o p k s -> (o p) k s") for h in range(2)]
                    if small:
                        if not (isinstance(i, int) and i + nxt == 0):
                            wait(sp, rd_ready, i, lo, NRD, PRO + NRD * (nxt - 2) + done_by("v"))
                    elif not (isinstance(i, int) and i + nxt == 0):
                        wait(sp, rd_ready, i, lo, NRD, PRO + NRD * (nxt - 1) + done_by("V1", 1))
                    for h in range(2):
                        sp.dma_start(cT[h][:, :, :].bitcast(F32), srcs[h]).then_inc(c_in, 16)

                load_c(0, 0, 0, 0)

                def body(i, lo, hi):
                    if hi < B - 1:
                        load_c(i, lo, hi, 1)

                run_loop(sp, B, CUTS, body)

            @block.tensor
            def _(pe):
                def scores(i, lo, s):
                    h = s % H
                    q = s % 2
                    part = h // 4
                    if h % 4 == 0:
                        turn = s // H - 1
                        wait(pe, rd_done, i, lo, NRD, PRO + turn * NRD + done_by("kT", part))
                    wait(pe, e_done, i, lo, H, s - 1)
                    if small:
                        b = i + s // H
                        row = mask16[:, b, :, :] if isinstance(b, int) else mask16[:, bass.ds(b, 1), :, :].rearrange("p o t s -> p (o t) s")
                        pe.matmul(s_ps[q][:, :, :], ident16[:, :], row if rotary else row.broadcast_to([P, TB, S]), start=True, stop=False,
                                  skip_group_check=True)
                    for t in range(TB):
                        if small:
                            r = 64 * (h % 2)
                            mm = pe.matmul(s_ps[q][:, t, :], QT[r:r + 64, h // 2, t * P:(t + 1) * P], KT[r:r + 64, h // 2, :], start=False, stop=True,
                                           skip_group_check=True)
                        else:
                            mm = mm3(pe, s_ps[q][:, t, :], [a[:, h, t * P:(t + 1) * P] for a in QT], [a[:, h // 2, :] for a in KT], True, True)
                    mm.then_inc(s_ready, 1)

                def turn_p(i, lo, s):
                    wait(pe, n_done, i, lo, H, s + 1)
                    wait(pe, pl_done, i, lo, H, s - 1)
                    for kc in range(KC):
                        for t in range(TB):
                            mm = pe.transpose(t_ps[s % 2][:, kc, t * P:(t + 1) * P], p_sb[s % 4][:, t, kc * P:(kc + 1) * P], ident[:, :])
                    mm.then_inc(t_ready, 1)

                def values(i, lo, s, last=False):
                    h = s % H
                    g = h // GH
                    if h % GH == 0:
                        wait(pe, ol_done, i, lo, NGR, (s // H) * NGR + g - 1)
                        if g == 1:
                            wait(pe, x_done, i, lo, 1, s // H)
                    wait(pe, pl_done, i, lo, H, s + 1)
                    if small:
                        if h == 0 or h == 8:
                            wait(pe, vh_done, i, lo, 2, 2 * (s // H) + 1 + h // 8)
                        out = o_ps[g % 2][:, 0:S]
                        for kc in range(KC):
                            for e in range(2):
                                mm = pe.matmul(out, vp[:, kc, h // 4, P * (h % 4):P * (h % 4) + P], pT[e][s % 4][:, kc, :], start=(h % GH == 0 and kc == 0 and e == 0),
                                               stop=(h % GH == GH - 1 and kc == KC - 1 and e == 1))
                    else:
                        if h == 0:
                            wait(pe, rd_done, i, lo, NRD, PRO + (s // H - 1) * NRD + done_by("V0", 1))
                        if h == 8:
                            wait(pe, rd_done, i, lo, NRD, PRO + (s // H) * NRD + 1 + [r[1:] for r in body_rounds(last)].index(("V1", 1)))
                        out = o_ps[g % 2][:, (h % 2) * S:(h % 2 + 1) * S]
                        for kc in range(KC):
                            mm = mm3(pe, out, [a[:, kc, (h // 2) * P:(h // 2 + 1) * P] for a in V], [a[s % 4][:, kc, :] for a in pT],
                                     kc == 0, kc == KC - 1)
                    mm.then_inc(pv_done, 1)

                def project(i, lo, nxt):
                    wait(pe, ol_done, i, lo, NGR, (nxt + 1) * NGR)
                    out = o_ps[1][:, :].rearrange("p (t d) -> p t d", t=TB)
                    for t in range(TB):
                        for c in range(OC):
                            mm = mm3(pe, out[:, t, :], [a[:, c, t * P:(t + 1) * P] for a in OT], [a[:, c, :] for a in wo], c == 0, c == OC - 1)
                    mm.then_inc(out_ready, 1)

                def round_(i, lo, a, pos, kind, part):
                    bank = r_ps[pos % 2]
                    wait(pe, rd_done, i, lo, NRD, a + pos - 1)
                    own = kind == "V1"
                    batch = (a - PRO) // NRD + (0 if own else 1)
                    if kind == "nT":
                        wait(pe, n_ready, i, lo, 1, batch + 1)
                        if small:
                            for k in range(KC):
                                for t in range(TB):
                                    mm = pe.transpose(bank[:, k * S + t * P:k * S + (t + 1) * P], n_sb[:, t, k * P:(k + 1) * P], ident[:, :])
                        else:
                            for t in range(TB):
                                mm = pe.transpose(bank[:, t * P:(t + 1) * P], n_sb[:, t, part * P:(part + 1) * P], ident[:, :])
                    elif small and kind in ("q", "k", "v"):
                        src, w = (nT, wq) if kind == "q" else (cT, wk if kind == "k" else wv)
                        if kind == "q":
                            wait(pe, rd_done, i, lo, NRD, a + pos - (done_by("q") - done_by("nT")) + 1)
                        if kind == "k":
                            wait(pe, c_in, i, lo, 32, 32 * (batch + 1))
                        for t in range(TB):
                            for k in range(KC):
                                mm = mm3(pe, bank[:, t * D:(t + 1) * D], [y[:, k, t * P:(t + 1) * P] for y in src], [y[:, k, :] for y in w],
                                         k == 0, k == KC - 1)
                    elif small:
                        src = qs if kind == "qT" else ks
                        if part == 0:
                            back = done_by(kind, 0) - done_by("q" if kind == "qT" else "k")
                            wait(pe, rd_done, i, lo, NRD, a + pos - back + 1)
                        flat = src[:, :, :, :].rearrange("p (t h) g d -> p t (h g d)", t=TB)
                        for c in range(2):
                            for t in range(TB):
                                mm = pe.transpose(bank[:, c * S + t * P:c * S + (t + 1) * P].bitcast(F32R),
                                                  flat[:, t, (2 * part + c) * P:(2 * part + c + 1) * P], identr[:, :])
                    elif kind in ("qT", "kT"):
                        src, w = (nT, wq) if kind == "qT" else (cT, wk)
                        if kind == "qT" and part == 0:
                            wait(pe, rd_done, i, lo, NRD, a + pos - (done_by("qT") - done_by("nT", 1)) + 1)
                        if kind == "kT" and part == 0:
                            wait(pe, c_in, i, lo, 32, 32 * (batch + 1))
                        for c in range(2):
                            for k in range(KC):
                                col = (2 * part + c) * P
                                mm = mm3(pe, bank[:, c * S:(c + 1) * S], [y[:, k, col:col + P] for y in w], [y[:, k, :] for y in src],
                                         k == 0, k == KC - 1)
                    else:
                        half = 512 * (kind == "V1")
                        for k in range(KC):
                            mm = mm3(pe, bank[:, :], [y[:, k, part * P:(part + 1) * P] for y in cT], [y[:, k, half:half + 512] for y in wv],
                                     k == 0, k == KC - 1)
                    mm.then_inc(rd_ready, 1)

                for pos, (_, kind, part) in enumerate(ROUNDS):
                    round_(0, 0, 0, pos, kind, part)
                for s in range(LEAD):
                    scores(0, 0, s)

                def body(i, lo, hi):
                    last = hi == B - 1
                    for h in range(H):
                        if not (last and h + LEAD >= H):
                            scores(i, lo, h + LEAD)
                        turn_p(i, lo, h)
                        for pos, kind, part in rounds_at(h, last):
                            round_(i, lo, PRO, pos, kind, part)
                        if not (lo == 0 and h < 2):
                            values(i, lo, h - 2, last)
                        if h == 2 and lo > 0:
                            project(i, lo, -1)

                run_loop(pe, B, CUTS, body)
                values(B - 1, B - 1, H - 2, True)
                values(B - 1, B - 1, H - 1, True)
                project(B - 1, B - 1, 0)

            @block.scalar
            def _(act):
                def weights_of(i, lo, s):
                    wait(act, m_ready, i, lo, H, s + 1)
                    wait(act, t_ready, i, lo, H, s - 3)
                    src = s_ps[s % 2]
                    for t in range(TB):
                        ins = act.activation(p_sb[s % 4][:, t, :], src[:, t, :], ACT.Exp, bias=nm[:, s % 4, t:t + 1], scale=-1.0,
                                             accum_out=rs[:, s % 4, t:t + 1])
                    ins.then_inc(e_done, 1)

                def p_hi(i, lo, s):
                    wait(act, t_ready, i, lo, H, s + 1)
                    wait(act, pv_done, i, lo, H, s - 3)
                    act.activation(pT[0][s % 4][:, :, :], t_ps[s % 2][:, :, :], ACT.Copy).then_inc(ph_done, 1)

                def o_hi(i, lo, turn, g):
                    wait(act, pv_done, i, lo, H, turn * H + (g + 1) * GH)
                    if g == 0:
                        wait(act, out_ready, i, lo, 1, turn)
                    if small:
                        ins = act.activation(OT[0][:, g, :], o_ps[g % 2][:, 0:S], ACT.Copy)
                    else:
                        for e in range(2):
                            ins = act.activation(OT[0][64 * e:64 * e + 64, g, :], o_ps[g % 2][64 * e:64 * e + 64, e * S:(e + 1) * S], ACT.Copy)
                    ins.then_inc(oh_done, 1)

                def round_(i, lo, a, pos, kind, part):
                    bank = r_ps[pos % 2]
                    both = lambda y: y[:, :].rearrange("p (c s) -> p c s", c=2)
                    batch = (a - PRO) // NRD + (0 if kind == "V1" else 1)
                    if small and kind in ("q", "k"):
                        wait(act, f_ready, i, lo, 2, 2 * batch + 1 + ("q", "k").index(kind))
                        src, dst = (qf, qs) if kind == "q" else (kf, ks)
                        wait(act, rd_ready, i, lo, NRD, a + pos + 1)
                        src4 = src[:, :, :].rearrange("p t (h o d) -> p (t h) o d", o=1, d=dh).broadcast_to([P, TB * H, 2, dh])
                        out = dst[:, :, 0:2, :] if kind == "q" else dst[:, :, 0:3:2, :]
                        act.activation(out, src4, ACT.Copy).then_inc(rd_hi, 1)
                        return
                    wait(act, rd_ready, i, lo, NRD, a + pos + 1)
                    if small and kind == "v":
                        wait(act, vh_done, i, lo, 2, 2 * batch)
                        act.activation(vf[:, :, :], both(bank), ACT.Copy).then_inc(rd_hi, 1)
                    elif kind == "nT":
                        if small:
                            act.activation(nT[0][:, :, :], both(bank), ACT.Copy).then_inc(rd_hi, 1)
                        else:
                            act.activation(nT[0][:, part, :], bank[:, 0:S], ACT.Copy).then_inc(rd_hi, 1)
                    elif small:
                        wait(act, s_ready, i, lo, H, H * batch - H + 4 * part + 4)
                        dst = QT if kind == "qT" else KT
                        act.activation(dst[:, 2 * part, :], bank[:, 0:S], ACT.Copy).then_inc(rd_hi, 1)
                    elif kind == "qT":
                        wait(act, s_ready, i, lo, H, H * batch - H + 4 * part + 4)
                        for e in range(2):
                            ins = act.activation(QT[0][64 * e:64 * e + 64, 4 * part + e:4 * part + 4:2, :], both(bank)[64 * e:64 * e + 64], ACT.Copy,
                                                 scale=-scale)
                        ins.then_inc(rd_hi, 1)
                    elif kind == "kT":
                        wait(act, s_ready, i, lo, H, H * batch - H + 4 * part + 4)
                        act.activation(KT[0][:, 2 * part:2 * part + 2, :], both(bank), ACT.Copy).then_inc(rd_hi, 1)
                    else:
                        half = 512 * (kind == "V1")
                        wait(act, pv_done, i, lo, H, H * batch - H + (16 if half else 8))
                        act.activation(V[0][:, part, half:half + 512], bank[:, :], ACT.Copy).then_inc(rd_hi, 1)

                def v_hi(i, lo, turn, half):
                    wait(act, v_ready, i, lo, 1, turn + 1)
                    wait(act, pv_done, i, lo, H, H * turn - H + 8 * half + 8)
                    for kc in range(KC):
                        ins = act.activation(v_cols(kc, half, 0), vf_cols(kc, half), ACT.Copy)
                    ins.then_inc(v_half, 1)

                for pos, (_, kind, part) in enumerate(ROUNDS):
                    round_(0, 0, 0, pos, kind, part)
                if small:
                    v_hi(0, 0, 0, 0)
                for s in range(LEAD - 1):
                    weights_of(0, 0, s)

                def body(i, lo, hi):
                    last = hi == B - 1
                    for h in range(H):
                        if not (last and h + 2 >= H):
                            weights_of(i, lo, h + 2)
                        p_hi(i, lo, h)
                        if h == 1 and lo > 0:
                            o_hi(i, lo, -1, NGR - 1)
                        if h > 1 and h % GH == 1:
                            o_hi(i, lo, 0, h // GH - 1)
                        for pos, kind, part in laid_at(h, 6, 8, last) + rounds_at(h, last):
                            if not small or kind not in ("q", "k") or h in (6, 8):
                                round_(i, lo, PRO, pos, kind, part)
                        if small and h == 2:
                            v_hi(i, lo, 0, 1)
                        if small and h == 10 and not last:
                            v_hi(i, lo, 1, 0)

                run_loop(act, B, CUTS, body)
                o_hi(B - 1, B - 1, 0, NGR - 1)

            @block.vector
            def _(v):
                def max_of(i, lo, s):
                    wait(v, e_done, i, lo, H, s - 1)
                    wait(v, s_ready, i, lo, H, s + 1)
                    v.tensor_reduce(nm[:, s % 4, :], s_ps[s % 2][:, :, :], AX.X, ALU.min).then_inc(m_ready, 1)

                def inverse(i, lo, s):
                    wait(v, e_done, i, lo, H, s + 1)
                    v.reciprocal(ri[:, s % 4, :], rs[:, s % 4, :]).then_inc(r_done, 1)

                def p_lo(i, lo, s):
                    wait(v, ph_done, i, lo, H, s + 1)
                    v.tensor_tensor(pT[1][s % 4][:, :, :], t_ps[s % 2][:, :, :], pT[0][s % 4][:, :, :].bitcast(F32), ALU.subtract).then_inc(pl_done, 1)

                def o_lo(i, lo, turn, g):
                    wait(v, oh_done, i, lo, NGR, turn * NGR + g + 1)
                    if small:
                        ins = v.tensor_tensor(OT[1][:, g, :], o_ps[g % 2][:, 0:S], OT[0][:, g, :].bitcast(F32), ALU.subtract)
                    else:
                        for e in range(2):
                            r = slice(64 * e, 64 * e + 64)
                            ins = v.tensor_tensor(OT[1][r, g, :], o_ps[g % 2][r, e * S:(e + 1) * S], OT[0][r, g, :].bitcast(F32), ALU.subtract)
                    ins.then_inc(ol_done, 1)

                def residual(i, lo, turn):
                    wait(v, out_ready, i, lo, 1, turn + 1)
                    out = o_ps[1][:, :].rearrange("p (t d) -> p t d", t=TB)
                    v.scalar_tensor_tensor(x_of(i, turn), out, tg[:, 0:1], x_of(i, turn), ALU.mult, ALU.add).then_inc(x_done, 1)

                def round_(i, lo, a, pos, kind, part):
                    bank = r_ps[pos % 2]
                    both = bank[:, :].rearrange("p (c s) -> p c s", c=2)
                    if small and kind == "v":
                        wait(v, rd_hi, i, lo, NRD, a + pos + 1)
                        v.tensor_tensor(vf[:, :, :], vf[:, :, :], bc_t(b3[:, 2, :], D), ALU.add)
                        v.drain().then_inc(v_ready, 1)
                        v.drain().then_inc(rd_done, 1)
                        return
                    if small and kind in ("q", "k"):
                        wait(v, rd_ready, i, lo, NRD, a + pos + 1)
                        f = {"q": qf, "k": kf}[kind]
                        j = ("q", "k").index(kind)
                        v.scalar_tensor_tensor(f[:, :, :], both, -scale if kind == "q" else 1.0, bc_t(b3[:, j, :], D), ALU.mult, ALU.add)
                        v.drain().then_inc(f_raw if rotary else f_ready, 1)
                        return
                    wait(v, rd_hi, i, lo, NRD, a + pos + 1)
                    if kind == "nT":
                        if small:
                            v.tensor_tensor(nT[1][:, :, :], both, nT[0][:, :, :].bitcast(F32), ALU.subtract).then_inc(rd_done, 1)
                        else:
                            v.tensor_tensor(nT[1][:, part, :], bank[:, 0:S], nT[0][:, part, :].bitcast(F32), ALU.subtract).then_inc(rd_done, 1)
                    elif small:
                        dst = QT if kind == "qT" else KT
                        v.tensor_copy(dst[:, 2 * part + 1, :], bank[:, S:2 * S]).then_inc(rd_done, 1)
                    elif kind == "qT":
                        for e in range(2):
                            r = slice(64 * e, 64 * e + 64)
                            heads = slice(4 * part + e, 4 * part + 4, 2)
                            ins = v.scalar_tensor_tensor(QT[1][r, heads, :], both[r], -scale, QT[0][r, heads, :].bitcast(F32), ALU.mult, ALU.subtract)
                        ins.then_inc(rd_done, 1)
                    elif kind == "kT":
                        v.tensor_tensor(KT[1][:, 2 * part:2 * part + 2, :], both, KT[0][:, 2 * part:2 * part + 2, :].bitcast(F32), ALU.subtract).then_inc(rd_done, 1)
                    else:
                        half = 512 * (kind == "V1")
                        v.tensor_tensor(V[1][:, part, half:half + 512], bank[:, :], V[0][:, part, half:half + 512].bitcast(F32), ALU.subtract).then_inc(rd_done, 1)

                def laid_lo(i, lo, a, pos, kind):
                    wait(v, rd_hi, i, lo, NRD, a + pos + 1)
                    f, dst = (qf, qs) if kind == "q" else (kf, ks)
                    src4 = f[:, :, :].rearrange("p t (h o d) -> p (t h) o d", o=1, d=dh).broadcast_to([P, TB * H, 2, dh])
                    hi_, lo_ = (dst[:, :, 0:2, :], dst[:, :, 2:4, :]) if kind == "q" else (dst[:, :, 0:3:2, :], dst[:, :, 1:4:2, :])
                    v.tensor_tensor(lo_, src4, hi_.bitcast(F32), ALU.subtract).then_inc(rd_done, 1)

                def v_lo(i, lo, turn, half):
                    wait(v, v_half, i, lo, 2, 2 * turn + half + 1)
                    for kc in range(KC):
                        ins = v.tensor_tensor(v_cols(kc, half, 1), vf_cols(kc, half), v_cols(kc, half, 0).bitcast(F32), ALU.subtract)
                    ins.then_inc(vh_done, 1)

                for pos, (_, kind, part) in enumerate(ROUNDS):
                    round_(0, 0, 0, pos, kind, part)
                    if small and kind in ("q", "k"):
                        laid_lo(0, 0, 0, pos, kind)
                if small:
                    v_lo(0, 0, 0, 0)
                for s in range(LEAD):
                    max_of(0, 0, s)
                for s in range(LEAD - 1):
                    inverse(0, 0, s)

                def body(i, lo, hi):
                    last = hi == B - 1
                    for h in range(H):
                        if not (last and h + LEAD >= H):
                            max_of(i, lo, h + LEAD)
                        p_lo(i, lo, h)
                        if h == 1 and lo > 0:
                            o_lo(i, lo, -1, NGR - 1)
                        if h > 1 and h % GH == 1:
                            o_lo(i, lo, 0, h // GH - 1)
                        if not (last and h + 2 >= H):
                            inverse(i, lo, h + 2)
                        for pos, kind, part in laid_at(h, 7, 8, last):
                            laid_lo(i, lo, PRO, pos, kind)
                        for pos, kind, part in rounds_at(h, last):
                            round_(i, lo, PRO, pos, kind, part)
                        if small and h == 2:
                            v_lo(i, lo, 0, 1)
                        if small and h == 10 and not last:
                            v_lo(i, lo, 1, 0)
                        if h == 3 and lo > 0:
                            residual(i, lo, -1)

                run_loop(v, B, CUTS, body)
                o_lo(B - 1, B - 1, 0, NGR - 1)
                residual(B - 1, B - 1, 0)

            @block.gpsimd
            def _(pool):
                def normalize(i, lo, s):
                    wait(pool, r_done, i, lo, H, s + 1)
                    pool.tensor_tensor(p_sb[s % 4][:, :, :], p_sb[s % 4][:, :, :],
                                       ri[:, s % 4, :].rearrange("p (t o) -> p t o", o=1).broadcast_to([P, TB, S]), ALU.mult).then_inc(n_done, 1)

                def per_row(y, q, b):
                    at = TB * b
                    cols = y[q][:, at:at + TB] if isinstance(b, int) else y[q][:, bass.ds(at, TB)]
                    return cols.rearrange("p (t o) -> p t o", o=1).broadcast_to([P, TB, D])

                def norm(i, lo, turn):
                    if not (isinstance(i, int) and i + turn == 0):
                        wait(pool, rd_ready, i, lo, NRD, PRO + (turn - 2) * NRD + done_by("nT", 0 if small else 1))
                    n = n_sb[:, :, :]
                    src = x_of(i, turn)
                    for q in range(len(nmean)):
                        pool.tensor_tensor(n, src, per_row(nmean, q, i + turn), ALU.add)
                        pool.drain()
                        pool.tensor_tensor(n, n, per_row(rstd, q, i + turn), ALU.mult)
                        pool.drain()
                        src = n
                    if inner:
                        pool.tensor_tensor(n, n, bc_t(gb[:, 0, :], D), ALU.mult)
                        pool.drain()
                        pool.tensor_tensor(n, n, bc_t(gb[:, 1, :], D), ALU.add)
                    pool.drain().then_inc(n_ready, 1)

                def rotate_products(i, lo, turn, kind):
                    j = ("q", "k").index(kind)
                    f = (qf, kf)[j]
                    wait(pool, f_raw, i, lo, 2, 2 * turn + j + 1)
                    half = lambda y, e: y[:, :, :].rearrange("p t (h e d) -> p t h e d", e=2, d=8)[:, :, :, e, :]
                    tab = lambda q, n: cs[:, :, q, :].rearrange("p t (o d) -> p t o d", o=1).broadcast_to([P, TB, n, 8])
                    pool.tensor_tensor(r1[:, :, :].rearrange("p t (h d) -> p t h d", d=8), f[:, :, :].rearrange("p t (h d) -> p t h d", d=8),
                                       tab(0, 32), ALU.mult)
                    pool.tensor_tensor(half(r2, 0), half(f, 1), tab(1, 16), ALU.mult)
                    pool.tensor_tensor(half(r2, 1), half(f, 0), tab(2, 16), ALU.mult)
                    pool.drain()

                def rotate_sum(i, lo, turn, kind):
                    f = qf if kind == "q" else kf
                    ins = pool.tensor_tensor(f[:, :, :], r1[:, :, :], r2[:, :, :], ALU.add)
                    if kind == "q":
                        pool.drain()
                        ins = pool.tensor_tensor(f[:, :, :], f[:, :, :], per_row([kq], 0, i + turn), ALU.mult)
                    ins.then_inc(f_ready, 1)

                def add_bias(i, lo, turn):
                    wait(pool, x_done, i, lo, 1, turn + 1)
                    pool.tensor_tensor(x_of(i, turn), x_of(i, turn), bc_t(bo[:, :], D), ALU.add)

                norm(0, 0, 0)
                for kind in ("q", "k") if rotary else ():
                    rotate_products(0, 0, 0, kind)
                    rotate_sum(0, 0, 0, kind)
                for s in range(LEAD - 1):
                    normalize(0, 0, s)

                def body(i, lo, hi):
                    for h in range(H):
                        if not (hi == B - 1 and h + 2 >= H):
                            normalize(i, lo, h + 2)
                        if h == 0 and hi < B - 1:
                            norm(i, lo, 1)
                        if rotary and h in (4, 6) and hi < B - 1:
                            rotate_products(i, lo, 1, "q" if h == 4 else "k")
                        if rotary and h in (5, 7) and hi < B - 1:
                            rotate_sum(i, lo, 1, "q" if h == 5 else "k")
                        if h == 9 and lo > 0:
                            add_bias(i, lo, -1)

                run_loop(pool, B, CUTS, body)
                add_bias(B - 1, B - 1, 0)


def head_sources(I, layer):
    if layer == 1:
        return {"q": I["L1_Wq"], "k": I["L1_Wk"], "v": I["L1_Wv"], "o": I["L1_Wo"], "bo": I["L1_xattn_bo"]}
    if layer == 2:
        return {"q": I["L2_xattn_Wq"], "k": I["L2_xattn_Wk"], "v": I["L2_xattn_Wv"], "o": I["L2_Wo"], "bo": I["L2_xattn_bo"]}
    return {"q": I["L3_xattn_w_q"], "k": I["L3_w_k"], "v": I["L3_w_v"], "o": I["L3_xattn_w_out"], "bo": I["L3_xattn_b_out"]}


def attention_layer(nc, G, I, layer, w=None):
    if layer == 0:
        single_phase(nc, G, I, "att0", {n: I["L0_xattn_" + n] for n in ("Wq", "Wk", "Wv", "Wcq", "Wck", "Wcv", "W1")},
                     (I["L0_xattn_gamma"], I["L0_xattn_beta"], I["L0_xattn_b1"]))
    if layer == 1:
        heads_phase(nc, G, I, "att1", 1, 16, head_sources(I, 1), w, mask=I["mask_BxS2_if1"], rotary=True,
                    biases=(I["L1_bq"], I["L1_bk"], I["L1_bv"]))
    if layer == 2:
        heads_phase(nc, G, I, "att2", 2, 16, head_sources(I, 2), w, mask=I["mask2"],
                    biases=(I["L2_xattn_bq"], I["L2_xattn_bk"], I["L2_xattn_bv"]))
    if layer == 3:
        heads_phase(nc, G, I, "att3", 3, 64, head_sources(I, 3), w,
                    inner=(I["L3_xattn_ln_gamma"], I["L3_xattn_ln_beta"]), gate=I["L3_xattn_gate"])


def single_phase(nc, G, I, name, weights, rows):
    NU, NT = 2, 4
    C = NT * P
    scale = -1.0 / 16.0
    W = {"Wq": 0, "Wk": 1, "Wv": 2, "Wcq": 3, "Wck": 4, "Wcv": 5, "W1": 6}
    PRODUCTS = ["nT", "QT", "KT", "cT", "V", "S", "cKT", "pT", "A", "cV", "hT", "cQT", "cS", "cpT", "cA", "h2T", "F"]
    NP = len(PRODUCTS)
    at = PRODUCTS.index
    SPLIT = [p for p in PRODUCTS if p not in ("S", "A", "cS", "cA", "F")]
    NK = T // NT
    when = lambda k, name: k // 2 * NP + {"n": at("cA") + 0.5 - NP, "tail": NP + at("QT") + 0.5}.get(name, at(name) if name in PRODUCTS else 0)
    ORDER = sorted(((when(k, name), k, name) for k in range(NK) for name in ["n", "tail", *PRODUCTS]), key=lambda s: s[:2])
    ROWS = {"hT": 1, "h2T": 2}

    with ExitStack() as ctx:
        A = Alloc(nc, ctx, name)
        sb, sem = A.sb, A.sem
        hl = lambda n, shape: [sb(f"{n}_{h}", shape, F32R) for h in ("hi", "lo")]
        x, ident, tg = G["x"], G["ident"], G["tanh_g"][:, 0:1]
        w_all = hl("w", [P, len(W), KC, D])
        jobs = []
        for wn, q in W.items():
            for k in range(KC):
                jobs.append((weights[wn][k * P:(k + 1) * P, :], w_all[0][:, q, k, :], w_all[1][:, q, k, :]))
        load_split(nc, name + "w", jobs, D)

        U = range(NU)
        per = lambda n, shape: [sb(f"{n}{u}", shape) for u in U]
        hl_u = lambda n: [hl(f"{n}{u}", [P, 2, 512]) for u in U]
        n_sb, p_sb, a_sb, h_sb, s_m = (per(n, [P, NT, D]) for n in ("n", "p", "a", "h", "s_m"))
        xT, QT, KT, V, pT, cT = (hl_u(n) for n in ("xT", "QT", "KT", "V", "pT", "cT"))
        c_raw, h2_sb = per("c_raw", [P, NT, D]), per("h2", [P, NT, D])
        st_n = [{n: sb(f"n_{n}{u}", shape) for n, shape in (("bn", [P, 4, 6]), ("mv", [P, 4, 2]), ("rstd", [P, 4]), ("tmp", [P, 4]), ("nb", [P, 4]))} for u in U]
        nm, rs, ri = (per(n, [P, NT]) for n in ("nm", "rs", "ri"))
        st = [{"bn": sb(f"bn{u}", [P, 4, 6]), "mv": sb(f"mv{u}", [P, 4, 2]), "rstd": sb(f"rstd{u}", [P, 4]), "tmp": sb(f"tmp{u}", [P, 4])} for u in U]
        gamma, beta, b1 = (sb(n, [P, D]) for n in ("gamma", "beta", "b1"))
        causal = sb("causal", [P, TB, S])
        ps = [[A.ps(f"ps{u}{q}", [P, 2, 512]) for q in range(2)] for u in U]
        per_sem = lambda n: [sem(f"{n}{u}") for u in U]
        var_ready, rstd_ready, product, hi_done, used, n_stats, n_ready, rows_ready, m_ready, e_ready, c_in, c_out, gated, unit_done = (
            per_sem(n) for n in ("var_ready", "rstd_ready", "product", "hi_done", "used", "n_stats", "n_ready", "rows_ready", "m_ready", "e_ready", "c_in", "c_out", "gated", "unit_done"))
        loaded, zeroed = sem("loaded"), sem("zeroed")
        minus_half = sb("minus_half", [P, NT])
        zeros = sb("zeros", [P, 1, D])

        rows4 = lambda y: y.rearrange("p a (b n) -> p (a b) n", n=D)
        dest = {"cT": cT, "nT": xT, "hT": xT, "h2T": xT, "QT": QT, "cQT": QT, "KT": KT, "cKT": KT, "V": V, "cV": V, "pT": pT, "cpT": pT}

        def bank(u, i, name):
            return ps[u][(i * NP + at(name)) % 2]

        def x_of(k):
            return x[:, k * NT:(k + 1) * NT, :]

        with nc.Block() as block:
            @block.sync
            def _(sp):
                for dst, src in zip((gamma, beta, b1), rows):
                    sp.dma_start(dst[:, :], src.rearrange("(a d) -> a d", a=1).broadcast_to([P, D])).then_inc(loaded, 16)
                sp.dma_start(causal[:, :, :], I["causal"]).then_inc(loaded, 16)
                sp.wait_ge(loaded, 64)

            @block.gpsimd
            def _(pool):
                pool.memset(zeros[:, :, :], 0.0)
                pool.memset(minus_half[:, :], -0.5)

        def store_c(sp, k):
            sp.wait_ge(used[k % 2], k // 2 * NP + at("cT") + 1)
            for b in range(2):
                for h in range(2):
                    sp.dma_start(G["ctxT"][h][2 * k + b], cT[k % 2][h][:, :, b * S:(b + 1) * S].bitcast(F32)).then_inc(c_out[k % 2], 16)

        with nc.Block() as block:
            @block.sync
            def _(sp):
                for k in range(T // NT):
                    u = k % 2
                    if k >= 2:
                        sp.wait_ge(product[u], (k // 2 - 1) * NP + at("cT") + 1)
                    sp.dma_start(c_raw[u][:, :, :], I["ctx_1024"][2 * k:2 * k + 2].rearrange("b (t p) d -> p (b t) d", p=P)).then_inc(c_in[u], 16)
                    if k >= 1:
                        store_c(sp, k - 1)
                store_c(sp, T // NT - 1)
                for u in U:
                    sp.wait_ge(c_out[u], 64 * (T // NT // 2))
                for r in range(0, XROWS, 512):
                    sp.dma_start(G["rows_x"][r:r + 512, :].rearrange("(p t) d -> p t d", p=P), zeros[:, :, :].broadcast_to([P, 4, D])).then_inc(zeroed, 16)
                sp.wait_ge(zeroed, 16 * len(range(0, XROWS, 512)))

            @block.tensor
            def _(pe):
                def turn_rows(i, u, name, rows):
                    for k in range(2):
                        for t in range(NT):
                            mm = pe.transpose(bank(u, i, name)[:, k, t * P:(t + 1) * P], rows[u][:, t, k * P:(k + 1) * P], ident[:, :])
                    return mm

                def features(i, u, name, src, w):
                    for c in range(2):
                        for k in range(KC):
                            mm = mm3(pe, bank(u, i, name)[:, c, :], [y[:, W[w], k, c * P:(c + 1) * P] for y in w_all],
                                     [y[:, k, :] for y in src[u]], k == 0, k == KC - 1)
                    return mm

                def tokens(i, u, name, src, moving):
                    out = rows4(bank(u, i, name)[:, :, :])
                    for t in range(NT):
                        for k in range(KC):
                            mm = mm3(pe, out[:, t, :], [y[:, k, t * P:(t + 1) * P] for y in src[u]], moving(u, t, k), k == 0, k == KC - 1)
                    return mm

                weight = lambda w: (lambda u, t, k: [y[:, W[w], k, :] for y in w_all])
                keys = lambda u, t, k: [y[:, k, (t // TB) * S:(t // TB + 1) * S] for y in KT[u]]
                vals = lambda u, t, k: [rows4(y[:, :, :])[:, (t // TB) * TB + k, :] for y in V[u]]

                def before(u, i, name, operand):
                    need = i * NP + max(at(operand) + 1 if operand else 0, at(name) - 1)
                    if need > 0:
                        pe.wait_ge(used[u], need)

                for _, k, name in ORDER:
                    u, i = k % 2, k // 2
                    if name in PRODUCTS:
                        if name == "nT":
                            before(u, i, name, None)
                            pe.wait_ge(n_ready[u], i + 1)
                            mm = turn_rows(i, u, name, n_sb)
                        elif name == "cT":
                            before(u, i, name, None)
                            pe.wait_ge(c_in[u], i * 16 + 16)
                            mm = turn_rows(i, u, name, c_raw)
                        elif name in ("hT", "h2T"):
                            before(u, i, name, None)
                            pe.wait_ge(rows_ready[u], i * 2 + ROWS[name])
                            mm = turn_rows(i, u, name, h_sb if name == "hT" else h2_sb)
                        elif name in ("pT", "cpT"):
                            before(u, i, name, None)
                            pe.wait_ge(e_ready[u], i * 2 + (1 if name == "pT" else 2))
                            mm = turn_rows(i, u, name, p_sb)
                        elif name in ("QT", "KT"):
                            before(u, i, name, "nT")
                            mm = features(i, u, name, xT, {"QT": "Wq", "KT": "Wk"}[name])
                        elif name == "V":
                            before(u, i, name, "nT")
                            mm = tokens(i, u, name, xT, weight("Wv"))
                        elif name in ("S", "cS"):
                            before(u, i, name, "KT" if name == "S" else "cQT")
                            mm = tokens(i, u, name, QT, keys)
                        elif name == "cKT":
                            before(u, i, name, "cT")
                            mm = features(i, u, name, cT, "Wck")
                        elif name in ("A", "cA"):
                            before(u, i, name, "pT" if name == "A" else "cpT")
                            mm = tokens(i, u, name, pT, vals)
                        elif name == "cV":
                            before(u, i, name, None)
                            mm = tokens(i, u, name, cT, weight("Wcv"))
                        elif name == "cQT":
                            before(u, i, name, "hT")
                            mm = features(i, u, name, xT, "Wcq")
                        else:
                            before(u, i, name, "h2T")
                            mm = tokens(i, u, name, xT, weight("W1"))
                        mm.then_inc(product[u], 1)

            @block.scalar
            def _(act):
                for _, k, name in ORDER:
                    u, i = k % 2, k // 2
                    if name == "n":
                        act.wait_ge(n_stats[u], i + 1)
                        for t in range(NT):
                            ins = act.activation(n_sb[u][:, t, :], x_of(k)[:, t, :], ACT.Identity, scale=st_n[u]["rstd"][:, t:t + 1],
                                                 bias=st_n[u]["nb"][:, t:t + 1])
                        ins.then_inc(n_ready[u], 1)
                    if name in PRODUCTS:
                        if name in SPLIT:
                            if name == "cT" and k >= 2:
                                act.wait_ge(c_out[u], i * 64)
                            act.wait_ge(product[u], i * NP + at(name) + 1)
                            act.activation(dest[name][u][0][:, :, :], bank(u, i, name)[:, :, :], ACT.Copy,
                                           scale=scale if name in ("QT", "cQT") else 1.0).then_inc(hi_done[u], 1)
                        elif name in ("S", "cS"):
                            act.wait_ge(m_ready[u], i * 2 + (1 if name == "S" else 2))
                            src = s_m[u] if name == "S" else rows4(bank(u, i, name)[:, :, :])
                            for t in range(NT):
                                ins = act.activation(p_sb[u][:, t, :], src[:, t, :], ACT.Exp, bias=nm[u][:, t:t + 1], scale=-1.0,
                                                     accum_out=rs[u][:, t:t + 1])
                            ins.then_inc(e_ready[u], 1)

            @block.vector
            def _(v):
                roots = [0, 0]

                def statistics(u, s, src, eps):
                    for t in range(NT):
                        v.bn_stats(s["bn"][:, t, :], src[:, t, :])
                    v.drain()
                    for t in range(NT):
                        v.bn_aggr(s["mv"][:, t, :], s["bn"][:, t, :])
                    v.drain()
                    v.tensor_scalar(s["tmp"][:, :], s["mv"][:, :, 1], eps, None, ALU.add).then_inc(var_ready[u], 1)
                    roots[u] += 1

                def norm(u, dst, src):
                    s = st[u]
                    statistics(u, s, src, 1e-3)
                    for t in range(NT):
                        v.scalar_tensor_tensor(src[:, t, :], src[:, t, :], s["mv"][:, t, 0:1], gamma[:, :], ALU.subtract, ALU.mult)
                    v.drain()
                    v.wait_ge(rstd_ready[u], roots[u])
                    for t in range(NT):
                        ins = v.scalar_tensor_tensor(dst[:, t, :], src[:, t, :], s["rstd"][:, t:t + 1], beta[:, :], ALU.mult, ALU.add)
                    return ins

                for _, k, name in ORDER:
                    u, i = k % 2, k // 2
                    if name == "n":
                        s = st_n[u]
                        statistics(u, s, x_of(k), 1e-5)
                        v.wait_ge(rstd_ready[u], roots[u])
                        v.scalar_tensor_tensor(s["nb"][:, :], s["mv"][:, :, 0], -1.0, s["rstd"][:, :], ALU.mult, ALU.mult).then_inc(n_stats[u], 1)
                    elif name == "tail":
                        norm(u, a_sb[u], a_sb[u])
                        v.drain()
                        v.tensor_scalar(a_sb[u][:, :, :], a_sb[u][:, :, :], 0.0, tg, ALU.max, ALU.mult).then_inc(gated[u], 1)
                    else:
                        src = bank(u, i, name)
                        tiles = rows4(src[:, :, :])
                        if name == "pT":
                            v.wait_ge(e_ready[u], i * 2 + 1)
                            v.reciprocal(ri[u][:, :], rs[u][:, :])
                        if name == "cpT":
                            v.wait_ge(e_ready[u], i * 2 + 2)
                            v.reciprocal(ri[u][:, :], rs[u][:, :]).then_inc(used[u], 1)
                        if name in SPLIT:
                            v.wait_ge(hi_done[u], i * len(SPLIT) + SPLIT.index(name) + 1)
                            hi_, lo_ = (y[:, :, :] for y in dest[name][u])
                            if name in ("QT", "cQT"):
                                ins = v.scalar_tensor_tensor(lo_, src[:, :, :], scale, hi_.bitcast(F32), ALU.mult, ALU.subtract)
                            else:
                                ins = v.tensor_tensor(lo_, src[:, :, :], hi_.bitcast(F32), ALU.subtract)
                            ins.then_inc(used[u], 1)
                            continue
                        v.wait_ge(product[u], i * NP + at(name) + 1)
                        if name == "S":
                            for t in range(NT):
                                ins = v.tensor_tensor_reduce(out=s_m[u][:, t, :], in0=tiles[:, t, :], in1=causal[:, t % TB, :], scale=1.0,
                                                             scalar=BIG, op0=ALU.add, op1=ALU.min, accum_out=nm[u][:, t:t + 1])
                            ins.then_inc(m_ready[u], 1)
                            v.drain().then_inc(used[u], 1)
                        elif name == "cS":
                            v.tensor_reduce(nm[u][:, :], tiles, AX.X, ALU.min).then_inc(m_ready[u], 1)
                        elif name in ("A", "cA"):
                            base, out = (n_sb, h_sb) if name == "A" else (h_sb, h2_sb)
                            if name == "A":
                                if i:
                                    v.wait_ge(unit_done[u], i)
                                v.wait_ge(n_ready[u], i + 1)
                            for t in range(NT):
                                ins = v.scalar_tensor_tensor(a_sb[u][:, t, :], tiles[:, t, :], ri[u][:, t:t + 1], base[u][:, t, :], ALU.mult, ALU.add)
                            ins.then_inc(used[u], 1)
                            v.drain()
                            norm(u, out[u], a_sb[u]).then_inc(rows_ready[u], 1)
                        else:
                            v.tensor_tensor(a_sb[u][:, :, :], tiles, b1[:, :].rearrange("p (o d) -> p o d", o=1).broadcast_to([P, NT, D]),
                                            ALU.add).then_inc(used[u], 1)
                            v.drain()
                            v.scalar_tensor_tensor(a_sb[u][:, :, :], a_sb[u][:, :, :], 0.0, h2_sb[u][:, :, :], ALU.max, ALU.add)
                            v.drain()

            @block.gpsimd
            def _(pool):
                roots = [0, 0]
                for _, k, name in ORDER:
                    u, i = k % 2, k // 2
                    if name in ("n", "A", "cA", "tail"):
                        s = st_n[u] if name == "n" else st[u]
                        roots[u] += 1
                        pool.wait_ge(var_ready[u], roots[u])
                        pool.tensor_tensor(s["rstd"][:, :], s["tmp"][:, :], minus_half[:, :], ALU.pow).then_inc(rstd_ready[u], 1)
                    if name == "tail":
                        pool.wait_ge(gated[u], i + 1)
                        pool.tensor_tensor(x_of(k), x_of(k), a_sb[u][:, :, :], ALU.add).then_inc(unit_done[u], 1)



def build_program(nc, I, out):
    with ExitStack() as ctx:
        G = globals_of(nc, Alloc(nc, ctx, "g"))
        setup_phase(nc, G, I)
        attention_layer(nc, G, I, 0)
        for layer in range(3):
            with ExitStack() as c2:
                w, jobs = head_weights(Alloc(nc, c2, f"w{layer + 1}"), 64 if layer == 2 else 16, head_sources(I, layer + 1))
                moe_layer(nc, G, I, layer, jobs)
                attention_layer(nc, G, I, layer + 1, w)
        moe_layer(nc, G, I, 3)
        final_phase(nc, G, out)


def kernel(**inputs):
    import concourse.bacc as bacc
    from concourse.bass_utils import run_bass_kernel_spmd

    nc = bacc.Bacc("TRN2", target_bir_lowering=False, num_devices=1)
    arrays = {f"in_{name}": np.ascontiguousarray(a) for name, a in lay_out(inputs).items()}
    I = {name[3:]: nc.dram_tensor(name, a.shape, mybir.dt.from_np(a.dtype), kind="ExternalInput").ap()
         for name, a in arrays.items()}
    out = nc.dram_tensor("out", (B, S, D), F32, kind="ExternalOutput").ap()
    build_program(nc, I, out)
    r = run_bass_kernel_spmd(nc, [arrays], core_ids=[0])
    return r.results[0]["out"]
```
